# Optimizing a Trainium2 kernel written in Bass

```python
import numpy as np
import jax
import jax.numpy as jnp

def _softmax(x, axis=-1):
    return jax.nn.softmax(x, axis=axis)

def _gelu(x):
    return jax.nn.gelu(x, approximate=True)

def _silu(x):
    return jax.nn.silu(x)

def _sigmoid(x):
    return jax.nn.sigmoid(x)

def _layernorm(x, axis=-1, eps=1e-05):
    m = jnp.mean(x, axis=axis, keepdims=True)
    v = jnp.var(x, axis=axis, keepdims=True)
    return (x - m) / jnp.sqrt(v + eps)

def _scatter_add(tgt, idx, src, axis=0):
    return tgt.at[idx].add(src)

def _segment_sum(src, seg, n):
    return jax.ops.segment_sum(src, seg, n)
kernel_name = 'mk_gnn_resnorm_d4_gnn_r16_00aae8'

def setup_inputs(seed: int=0):
    np.random.seed(seed)
    _w = jnp.asarray

    def _rec_inputs():
        import jax
        import jax.numpy as jnp
        _gk = jax.random.key(seed)
        x = -0.000202 + 1 * jax.random.normal(jax.random.fold_in(_gk, 1), (6250, 64), jnp.float32)
        src = jax.random.randint(jax.random.fold_in(_gk, 2), (200000,), 0, 6250, jnp.int32)
        dst = jnp.minimum((6250 * jax.random.uniform(jax.random.fold_in(_gk, 3), (200000,)) ** 2.0).astype(jnp.int32), 99999)
        _o = jnp.argsort(dst, stable=True)
        src = src[_o]
        dst = dst[_o]
        edge_attr_32 = -8.62073e-06 + 0.999901 * jax.random.normal(jax.random.fold_in(_gk, 12), (200000, 32), jnp.float32)
        return (x, src, dst, edge_attr_32)
    x, src, dst, edge_attr_32 = _rec_inputs()

    def _L0_gnn_setup():
        import jax, jax.numpy as jnp
        import numpy as np
        IN_DIM, E_DIM, OUT_DIM = (64, 32, 64)
        N_NODES, N_EDGES = (6250, 62500)
        NEG_SLOPE = 0.2
        key = jax.random.key(seed)
        ks = jax.random.split(key, 9)
        gain = float(np.sqrt(2.0))

        def xavier(k, shape):
            fan_out, fan_in = shape
            std = gain * np.sqrt(2.0 / (fan_in + fan_out))
            return jax.random.normal(k, shape, dtype=jnp.float32) * std
        nfeats = jax.random.normal(ks[0], (N_NODES, IN_DIM), dtype=jnp.float32)
        efeats = jax.random.normal(ks[1], (N_EDGES, E_DIM), dtype=jnp.float32)
        src = jax.random.randint(ks[2], (N_EDGES,), 0, N_NODES, dtype=jnp.int32)
        dst = jax.random.randint(ks[3], (N_EDGES,), 0, N_NODES, dtype=jnp.int32)
        proj_w = xavier(ks[4], (OUT_DIM, IN_DIM + E_DIM))
        attn_w = xavier(ks[5], (1, 2 * IN_DIM))
        attn_b = jnp.zeros((1,), dtype=jnp.float32)
        apply_w = xavier(ks[6], (OUT_DIM, IN_DIM + OUT_DIM))
        apply_b = jnp.zeros((OUT_DIM,), dtype=jnp.float32)
        return {'nfeats': nfeats, 'efeats': efeats, 'src': src, 'dst': dst, 'proj_w': proj_w, 'attn_w': attn_w, 'attn_b': attn_b, 'apply_w': apply_w, 'apply_b': apply_b}
    _L0_gnn_all = _L0_gnn_setup()
    _L0_gnn_in = {k: v for k, v in _L0_gnn_all.items() if k in ('proj_w', 'attn_w', 'attn_b', 'apply_w', 'apply_b')}
    del _L0_gnn_all

    def _L1_gnn_setup():
        import jax, jax.numpy as jnp
        import numpy as np
        NEG_SLOPE = 0.2

        def _gat_forward(atom_features, edges, W, a, merge_kernel):
            N = atom_features.shape[0]
            U = W.shape[-1]
            src, dst = (edges[:, 0], edges[:, 1])
            h = jnp.einsum('nf,hfu->nhu', atom_features, W)
            a_src = a[:, :U, 0]
            a_dst = a[:, U:, 0]
            alpha_src = jnp.einsum('nhu,hu->nh', h, a_src)
            alpha_dst = jnp.einsum('nhu,hu->nh', h, a_dst)
            scores = jax.nn.leaky_relu(alpha_src[src] + alpha_dst[dst], NEG_SLOPE)
            att = jnp.exp(jnp.clip(scores, -2.0, 2.0))
            att_sum = jax.ops.segment_sum(att, src, num_segments=N)
            att_norm = att / att_sum[src]
            msgs = h[dst] * att_norm[:, :, None]
            out = jax.ops.segment_sum(msgs, src, num_segments=N)
            merged = out.reshape(N, -1)
            return jax.nn.leaky_relu(merged @ merge_kernel, NEG_SLOPE)
        key = jax.random.key(seed)
        ks = jax.random.split(key, 6)
        N, E, F, U, H = (3125, 50000, 64, 64, 8)
        atom_features = jax.random.normal(ks[0], (N, F), dtype=jnp.float32)
        src = jnp.sort(jax.random.randint(ks[1], (E,), 0, N, dtype=jnp.int32))
        dst = jax.random.randint(ks[2], (E,), 0, N, dtype=jnp.int32)
        edges = jnp.stack([src, dst], axis=1)
        W = jax.random.normal(ks[3], (H, F, U), dtype=jnp.float32) * 0.1
        a = jax.random.normal(ks[4], (H, 2 * U, 1), dtype=jnp.float32) * 0.1
        merge_kernel = jax.random.normal(ks[5], (H * U, U), dtype=jnp.float32) * 0.05
        return {'atom_features': atom_features, 'edges': edges, 'W': W, 'a': a, 'merge_kernel': merge_kernel}
    _L1_gnn_all = _L1_gnn_setup()
    _L1_gnn_in = {k: v for k, v in _L1_gnn_all.items() if k in ('W', 'a', 'merge_kernel')}
    del _L1_gnn_all

    def _L2_gnn_setup():
        import jax, jax.numpy as jnp
        import numpy as np
        N, E = (3125, 78125)
        IN_DIM, OUT_DIM, HEADS = (64, 64, 4)
        NEG_SLOPE = 0.2
        LN_EPS = 1e-05
        SM_EPS = 1e-16

        def _gat_conv(x, src, dst, W, a_src, a_dst, b, heads, out_c, concat):
            n = x.shape[0]
            xw = (x @ W).reshape(n, heads, out_c)
            asrc = jnp.einsum('nhc,hc->nh', xw, a_src)
            adst = jnp.einsum('nhc,hc->nh', xw, a_dst)
            loop = jnp.arange(n, dtype=src.dtype)
            s = jnp.concatenate([src, loop])
            d = jnp.concatenate([dst, loop])
            e = jax.nn.leaky_relu(asrc[s] + adst[d], NEG_SLOPE)
            m = jax.ops.segment_max(e, d, num_segments=n)
            ex = jnp.exp(e - m[d])
            denom = jax.ops.segment_sum(ex, d, num_segments=n)
            att = ex / (denom[d] + SM_EPS)
            msg = xw[s] * att[:, :, None]
            out = jax.ops.segment_sum(msg, d, num_segments=n)
            out = out.reshape(n, heads * out_c) if concat else out.mean(axis=1)
            return out + b

        def _layer_norm(x, g, b):
            mu = x.mean(-1, keepdims=True)
            var = ((x - mu) ** 2).mean(-1, keepdims=True)
            return (x - mu) * jax.lax.rsqrt(var + LN_EPS) * g + b
        key = jax.random.key(seed)
        ks = jax.random.split(key, 12)
        s = 0.1
        return {'h': jax.random.normal(ks[0], (N, IN_DIM), jnp.float32), 'edge_index': jax.random.randint(ks[1], (2, E), 0, N, jnp.int32), 'W1': jax.random.normal(ks[2], (IN_DIM, HEADS * 16), jnp.float32) * s, 'a1_src': jax.random.normal(ks[3], (HEADS, 16), jnp.float32) * s, 'a1_dst': jax.random.normal(ks[4], (HEADS, 16), jnp.float32) * s, 'b1': jnp.zeros((HEADS * 16,), jnp.float32), 'W2': jax.random.normal(ks[5], (OUT_DIM, OUT_DIM), jnp.float32) * s, 'a2_src': jax.random.normal(ks[6], (1, OUT_DIM), jnp.float32) * s, 'a2_dst': jax.random.normal(ks[7], (1, OUT_DIM), jnp.float32) * s, 'b2': jnp.zeros((OUT_DIM,), jnp.float32), 'ln1_g': jnp.ones((OUT_DIM,), jnp.float32), 'ln1_b': jnp.zeros((OUT_DIM,), jnp.float32), 'ln2_g': jnp.ones((OUT_DIM,), jnp.float32), 'ln2_b': jnp.zeros((OUT_DIM,), jnp.float32)}
    _L2_gnn_all = _L2_gnn_setup()
    _L2_gnn_in = {k: v for k, v in _L2_gnn_all.items() if k in ('W1', 'a1_src', 'a1_dst', 'b1', 'W2', 'a2_src', 'a2_dst', 'b2', 'ln1_g', 'ln1_b', 'ln2_g', 'ln2_b')}
    del _L2_gnn_all

    def _L3_gnn_setup():
        import jax, jax.numpy as jnp
        import numpy as np
        N_NODES = 6250
        N_EDGES = 100000
        IN_DIM = 64
        HID = 64
        EPS = 1e-12

        def _sage_layer(x, src, dst, deg_inv, Wl, bl, Wr):
            n = x.shape[0]
            agg = jax.ops.segment_sum(x[src], dst, num_segments=n) * deg_inv
            h = agg @ Wl.T + bl + x @ Wr.T
            norm = jnp.maximum(jnp.linalg.norm(h, axis=-1, keepdims=True), EPS)
            return jax.nn.relu(h / norm)
        key = jax.random.key(seed)
        ks = jax.random.split(key, 8)
        x = jax.random.normal(ks[0], (N_NODES, IN_DIM), dtype=jnp.float32)
        edge_index = jax.random.randint(ks[1], (2, N_EDGES), 0, N_NODES, dtype=jnp.int64)
        s = 1.0 / np.sqrt(IN_DIM)
        Wl0 = jax.random.uniform(ks[2], (HID, IN_DIM), jnp.float32, -s, s)
        bl0 = jnp.zeros((HID,), jnp.float32)
        Wr0 = jax.random.uniform(ks[3], (HID, IN_DIM), jnp.float32, -s, s)
        sh = 1.0 / np.sqrt(HID)
        Wl1 = jax.random.uniform(ks[4], (HID, HID), jnp.float32, -sh, sh)
        bl1 = jnp.zeros((HID,), jnp.float32)
        Wr1 = jax.random.uniform(ks[5], (HID, HID), jnp.float32, -sh, sh)
        return {'x': x, 'edge_index': edge_index, 'Wl0': Wl0, 'bl0': bl0, 'Wr0': Wr0, 'Wl1': Wl1, 'bl1': bl1, 'Wr1': Wr1}
    _L3_gnn_all = _L3_gnn_setup()
    _L3_gnn_in = {k: v for k, v in _L3_gnn_all.items() if k in ('Wl0', 'bl0', 'Wr0', 'Wl1', 'bl1', 'Wr1')}
    del _L3_gnn_all
    return {'x': x, 'src': src, 'dst': dst, 'edge_attr_32': edge_attr_32, 'L0_gnn_proj_w': _L0_gnn_in['proj_w'], 'L0_gnn_attn_w': _L0_gnn_in['attn_w'], 'L0_gnn_attn_b': _L0_gnn_in['attn_b'], 'L0_gnn_apply_w': _L0_gnn_in['apply_w'], 'L0_gnn_apply_b': _L0_gnn_in['apply_b'], 'L1_gnn_W': _L1_gnn_in['W'], 'L1_gnn_a': _L1_gnn_in['a'], 'L1_gnn_merge_kernel': _L1_gnn_in['merge_kernel'], 'L2_gnn_W1': _L2_gnn_in['W1'], 'L2_gnn_a1_src': _L2_gnn_in['a1_src'], 'L2_gnn_a1_dst': _L2_gnn_in['a1_dst'], 'L2_gnn_b1': _L2_gnn_in['b1'], 'L2_gnn_W2': _L2_gnn_in['W2'], 'L2_gnn_a2_src': _L2_gnn_in['a2_src'], 'L2_gnn_a2_dst': _L2_gnn_in['a2_dst'], 'L2_gnn_b2': _L2_gnn_in['b2'], 'L2_gnn_ln1_g': _L2_gnn_in['ln1_g'], 'L2_gnn_ln1_b': _L2_gnn_in['ln1_b'], 'L2_gnn_ln2_g': _L2_gnn_in['ln2_g'], 'L2_gnn_ln2_b': _L2_gnn_in['ln2_b'], 'L3_gnn_Wl0': _L3_gnn_in['Wl0'], 'L3_gnn_bl0': _L3_gnn_in['bl0'], 'L3_gnn_Wr0': _L3_gnn_in['Wr0'], 'L3_gnn_Wl1': _L3_gnn_in['Wl1'], 'L3_gnn_bl1': _L3_gnn_in['bl1'], 'L3_gnn_Wr1': _L3_gnn_in['Wr1']}

def reference(x, src, dst, edge_attr_32, L0_gnn_proj_w, L0_gnn_attn_w, L0_gnn_attn_b, L0_gnn_apply_w, L0_gnn_apply_b, L1_gnn_W, L1_gnn_a, L1_gnn_merge_kernel, L2_gnn_W1, L2_gnn_a1_src, L2_gnn_a1_dst, L2_gnn_b1, L2_gnn_W2, L2_gnn_a2_src, L2_gnn_a2_dst, L2_gnn_b2, L2_gnn_ln1_g, L2_gnn_ln1_b, L2_gnn_ln2_g, L2_gnn_ln2_b, L3_gnn_Wl0, L3_gnn_bl0, L3_gnn_Wr0, L3_gnn_Wl1, L3_gnn_bl1, L3_gnn_Wr1):
    import jax
    import jax.numpy as jnp

    def _L0_gnn_ref(nfeats, efeats, src, dst, proj_w, attn_w, attn_b, apply_w, apply_b):
        import jax, jax.numpy as jnp
        import numpy as np
        IN_DIM, E_DIM, OUT_DIM = (64, 32, 64)
        N_NODES, N_EDGES = (6250, 62500)
        NEG_SLOPE = 0.2
        n_nodes = nfeats.shape[0]
        h_src = nfeats[src]
        h_dst = nfeats[dst]
        e = h_src @ attn_w[0, :IN_DIM] + h_dst @ attn_w[0, IN_DIM:] + attn_b[0]
        e = jnp.where(e >= 0, e, NEG_SLOPE * e)
        m = h_src @ proj_w[:, :IN_DIM].T + efeats @ proj_w[:, IN_DIM:].T
        e_max = jax.ops.segment_max(e, dst, num_segments=n_nodes)
        e_exp = jnp.exp(e - e_max[dst])
        denom = jax.ops.segment_sum(e_exp, dst, num_segments=n_nodes)
        alpha = e_exp / denom[dst]
        z = jax.ops.segment_sum(alpha[:, None] * m, dst, num_segments=n_nodes)
        out = jnp.concatenate([nfeats, z], axis=1) @ apply_w.T + apply_b
        return jax.nn.relu(out)

    def _L1_gnn_ref(atom_features, edges, W, a, merge_kernel):
        import jax, jax.numpy as jnp
        import numpy as np
        NEG_SLOPE = 0.2

        def _gat_forward(atom_features, edges, W, a, merge_kernel):
            N = atom_features.shape[0]
            U = W.shape[-1]
            src, dst = (edges[:, 0], edges[:, 1])
            h = jnp.einsum('nf,hfu->nhu', atom_features, W)
            a_src = a[:, :U, 0]
            a_dst = a[:, U:, 0]
            alpha_src = jnp.einsum('nhu,hu->nh', h, a_src)
            alpha_dst = jnp.einsum('nhu,hu->nh', h, a_dst)
            scores = jax.nn.leaky_relu(alpha_src[src] + alpha_dst[dst], NEG_SLOPE)
            att = jnp.exp(jnp.clip(scores, -2.0, 2.0))
            att_sum = jax.ops.segment_sum(att, src, num_segments=N)
            att_norm = att / att_sum[src]
            msgs = h[dst] * att_norm[:, :, None]
            out = jax.ops.segment_sum(msgs, src, num_segments=N)
            merged = out.reshape(N, -1)
            return jax.nn.leaky_relu(merged @ merge_kernel, NEG_SLOPE)
        return _gat_forward(atom_features, edges, W, a, merge_kernel)

    def _L2_gnn_ref(h, edge_index, W1, a1_src, a1_dst, b1, W2, a2_src, a2_dst, b2, ln1_g, ln1_b, ln2_g, ln2_b):
        import jax, jax.numpy as jnp
        import numpy as np
        N, E = (3125, 78125)
        IN_DIM, OUT_DIM, HEADS = (64, 64, 4)
        NEG_SLOPE = 0.2
        LN_EPS = 1e-05
        SM_EPS = 1e-16

        def _gat_conv(x, src, dst, W, a_src, a_dst, b, heads, out_c, concat):
            n = x.shape[0]
            xw = (x @ W).reshape(n, heads, out_c)
            asrc = jnp.einsum('nhc,hc->nh', xw, a_src)
            adst = jnp.einsum('nhc,hc->nh', xw, a_dst)
            loop = jnp.arange(n, dtype=src.dtype)
            s = jnp.concatenate([src, loop])
            d = jnp.concatenate([dst, loop])
            e = jax.nn.leaky_relu(asrc[s] + adst[d], NEG_SLOPE)
            m = jax.ops.segment_max(e, d, num_segments=n)
            ex = jnp.exp(e - m[d])
            denom = jax.ops.segment_sum(ex, d, num_segments=n)
            att = ex / (denom[d] + SM_EPS)
            msg = xw[s] * att[:, :, None]
            out = jax.ops.segment_sum(msg, d, num_segments=n)
            out = out.reshape(n, heads * out_c) if concat else out.mean(axis=1)
            return out + b

        def _layer_norm(x, g, b):
            mu = x.mean(-1, keepdims=True)
            var = ((x - mu) ** 2).mean(-1, keepdims=True)
            return (x - mu) * jax.lax.rsqrt(var + LN_EPS) * g + b
        src, dst = (edge_index[0], edge_index[1])
        x = _gat_conv(h, src, dst, W1, a1_src, a1_dst, b1, HEADS, 16, True)
        x = jax.nn.elu(_layer_norm(x, ln1_g, ln1_b))
        z = _gat_conv(x, src, dst, W2, a2_src, a2_dst, b2, 1, OUT_DIM, False)
        z = jax.nn.elu(_layer_norm(z, ln2_g, ln2_b))
        return z

    def _L3_gnn_ref(x, edge_index, Wl0, bl0, Wr0, Wl1, bl1, Wr1):
        import jax, jax.numpy as jnp
        import numpy as np
        N_NODES = 6250
        N_EDGES = 100000
        IN_DIM = 64
        HID = 64
        EPS = 1e-12

        def _sage_layer(x, src, dst, deg_inv, Wl, bl, Wr):
            n = x.shape[0]
            agg = jax.ops.segment_sum(x[src], dst, num_segments=n) * deg_inv
            h = agg @ Wl.T + bl + x @ Wr.T
            norm = jnp.maximum(jnp.linalg.norm(h, axis=-1, keepdims=True), EPS)
            return jax.nn.relu(h / norm)
        src, dst = (edge_index[0], edge_index[1])
        deg = jax.ops.segment_sum(jnp.ones((src.shape[0],), x.dtype), dst, num_segments=x.shape[0])
        deg_inv = (1.0 / jnp.maximum(deg, 1.0))[:, None]
        h = _sage_layer(x, src, dst, deg_inv, Wl0, bl0, Wr0)
        h = _sage_layer(h, src, dst, deg_inv, Wl1, bl1, Wr1)
        return h
    edge_index = jnp.stack([src, dst])
    edge_index_t = jnp.stack([src, dst], axis=1)
    x = _layernorm(x + _L0_gnn_ref(x, edge_attr_32, src, dst, L0_gnn_proj_w, L0_gnn_attn_w, L0_gnn_attn_b, L0_gnn_apply_w, L0_gnn_apply_b), axis=-1)
    x = _layernorm(x + _L1_gnn_ref(x, edge_index_t, L1_gnn_W, L1_gnn_a, L1_gnn_merge_kernel), axis=-1)
    x = _layernorm(x + _L2_gnn_ref(x, edge_index, L2_gnn_W1, L2_gnn_a1_src, L2_gnn_a1_dst, L2_gnn_b1, L2_gnn_W2, L2_gnn_a2_src, L2_gnn_a2_dst, L2_gnn_b2, L2_gnn_ln1_g, L2_gnn_ln1_b, L2_gnn_ln2_g, L2_gnn_ln2_b), axis=-1)
    x = _layernorm(x + _L3_gnn_ref(x, edge_index, L3_gnn_Wl0, L3_gnn_bl0, L3_gnn_Wr0, L3_gnn_Wl1, L3_gnn_bl1, L3_gnn_Wr1), axis=-1)
    return x

_drawn_inputs = setup_inputs


def setup_inputs(seed=0):
    import zlib

    import numpy as np

    out = dict(_drawn_inputs(seed))
    spreads = {'L0_gnn_apply_b': (0.0, 0.1),
     'L2_gnn_b1': (0.0, 0.1),
     'L2_gnn_b2': (0.0, 0.1),
     'L2_gnn_ln1_g': (1.0, 0.2),
     'L2_gnn_ln1_b': (0.0, 0.1),
     'L2_gnn_ln2_g': (1.0, 0.2),
     'L2_gnn_ln2_b': (0.0, 0.1),
     'L3_gnn_bl0': (0.0, 0.1),
     'L3_gnn_bl1': (0.0, 0.1)}
    factors = {}
    for name, (base, spread) in spreads.items():
        noise = np.random.default_rng([zlib.crc32(name.encode()), seed]).standard_normal(out[name].shape)
        drawn = base * np.exp(spread * noise) if base else spread * noise
        out[name] = jnp.asarray(drawn.astype(out[name].dtype))
    for name, factor in factors.items():
        out[name] = (out[name] * factor).astype(out[name].dtype)
    return out
```

```python
from contextlib import ExitStack

import concourse.bass as bass
from concourse import mybir

fp32 = mybir.dt.float32
i32 = mybir.dt.int32
bf16 = mybir.dt.bfloat16
ALU = mybir.AluOpType
ACT = mybir.ActivationFunctionType
AX = mybir.AxisListType.X
RMAX = bass.bass_isa.ReduceOp.max

P = 128
N, E, D, DE = 6250, 200000, 64, 32
G = 4
GE = G * P
U = 4
NW = -(-N // P)
NB = NW + 1
WB = 2
NP = 52
FULL, TAIL = N // P, N % P
NG = -(-((E + NW * (GE - 1)) // GE) // U) * U
GP = max(p for p in range(1, P + 1) if NG % p == 0)
GC = NG // GP
SP_, SC = 125, E // 125
SU = 16
H1, H2 = 8, 4
SLOPE = 0.2
SPAN = 16.0
BIG_NODE = 1 << 20


class Chain:

    def __init__(self, eng, sem):
        self.eng, self.sem, self.n = eng, sem, 0

    def __call__(self, ins):
        self.n += 1
        ins.then_inc(self.sem, 1)
        self.eng.wait_ge(self.sem, self.n)


def since(eng, sem, value, before=0):
    if isinstance(value, int) and value <= 0:
        return
    eng.wait_ge(sem, value + before)


def pipelined(eng, count, unroll, stages, body_start=None):
    def step(i, s):
        for lag, stage in stages:
            k = i * unroll + s + lag
            if not isinstance(i, int) or 0 <= k < count:
                stage(k, (s + lag) % unroll, i + (s + lag) // unroll)

    ahead = max(lag for lag, _ in stages)
    behind = -min(lag for lag, _ in stages)
    assert ahead < unroll + 1 and behind <= unroll
    if body_start:
        body_start(0)
    for k in range(-ahead, unroll):
        step(k // unroll, k % unroll)
    with eng.Fori(1, count // unroll - 1) as i:
        if body_start:
            body_start(i)
        for s in range(unroll):
            step(i, s)
    if body_start:
        body_start(count // unroll - 1)
    for k in range(count - unroll, count + behind):
        step(k // unroll, k % unroll)


def build(nc, a, out):
    ctx = ExitStack()
    with ctx:
        def sb(name, shape, dt=fp32):
            return ctx.enter_context(nc.sbuf_tensor(name, shape, dt))

        def ps(name, shape):
            return ctx.enter_context(nc.psum_tensor(name, shape, fp32))

        def sem(name):
            return ctx.enter_context(nc.semaphore(name))

        def dram(name, shape, dt=fp32):
            return nc.dram_tensor(name, shape, dt, kind="Internal").ap()

        records = {s: dram(f"records_{s}", [NG * GE, 2], i32) for s in ("dst", "src")}
        group_window = {s: dram(f"group_window_{s}", [NG], i32) for s in ("dst", "src")}
        group_start = dram("group_start", [NG], i32)
        ROW = [65, 72, 68, 65, 65, 65]
        tables = [dram(f"table{p}", [NP * P, ROW[p]]) for p in range(6)]

        HEADS = [1, H1, H2, 1, 0, 0]
        OUTW = [D + DE + 1, H1 * D + H1, D + H2, D + 1, D + 1, D + 1]
        SIDE = ["dst", "src", "dst", "dst", "dst", "dst"]

        ACCF = NP * OUTW[1]
        acc_all = sb("acc_all", [P, ACCF])
        xcur = sb("xcur", [P, NP, D])
        pre = sb("pre", [P, NP, D])
        tab = sb("tab", [P, NP, 80])
        ntab = sb("ntab", [P, NP, 2 * H1])
        ntab3 = sb("ntab3", [P, 3, NP, 2 * H1], bf16)
        rden = sb("rden", [P, NP, H1])
        mtmp = acc_all[:, 19400:19400 + NP * H1].rearrange("p (w h) -> p w h", w=NP)
        deginv = sb("deginv", [P, NP])
        stat = sb("stat", [P, NP])
        idx = sb("idx", [P, NG * G], i32)
        local = sb("local", [P, NG * G])
        wrow = sb("wrow", [1, NG], i32)
        srow = sb("srow", [1, NG], i32)
        idx_slot = sb("idx_slot", [P, U, G], i32)
        rows = sb("rows", [P, U, G * 72])
        attrs = sb("attrs", [P, U, G, DE])
        flat_pre = pre[:, :, :].rearrange("p w f -> p (w f)")
        onehot = flat_pre[:, 0:U * GE].rearrange("p (s g n) -> p s g n", s=U, g=G)
        onehot_t = flat_pre[:, U * GE:(U + 1) * GE].bitcast(bf16).rearrange("p (s g n) -> p s g n", s=2, g=G)
        t12 = sb("t12", [P, 2, G, 2 * H1])
        zmax = sb("zmax", [P, 2, G * H1])
        rhs = sb("rhs", [P, 2, G * OUTW[1]])
        flat_rhs = rhs[:, :, :].rearrange("p a b -> p (a b)")
        staged = flat_rhs[:, 0:2048].rearrange("p (a b) -> p a b", a=2)
        node_t = flat_rhs[:, 2048:4096].rearrange("p (a b) -> p a b", a=2)

        def region(at, shape, dt=fp32):
            n = 1
            for d in shape[1:]:
                n *= d
            v = acc_all[0:shape[0], at:at + n]
            if dt is not fp32:
                v = v.bitcast(dt)
            if len(shape) == 2:
                return v
            names = "abc"[:len(shape) - 1]
            return v.rearrange(f"p ({' '.join(names)}) -> p {' '.join(names)}",
                               **{c: d for c, d in zip(names, shape[1:])})

        flat_rec = region(0, [SP_, SC, 2], i32)
        keyw = region(2 * SC, [SP_, SC])
        keyi = region(3 * SC, [SP_, SC], i32)
        ind = region(4 * SC, [SP_, SC])
        cum = region(5 * SC, [SP_, SC])
        pos = region(6 * SC, [SP_, SC])
        posi = region(7 * SC, [SP_, SC], i32)
        grec = region(20000, [P, NG * G, 2], i32)
        wb = region(26300, [P, NG])
        wbi = region(23520, [P, NG], i32)
        pad = region(24000, [P, 1024, 2], i32)
        tmp = region(16000, [P, NP, D])
        assert 20000 + 2 * NG * G <= 24000

        ident = sb("ident", [P, P])
        ones = sb("ones", [P, P])
        below = sb("below", [P, P])
        iota_n = sb("iota_n", [P, P])
        iota_ni = sb("iota_ni", [P, P], i32)
        iota_g = sb("iota_g", [P, GC])
        iota_gi = sb("iota_gi", [P, GC], i32)
        gsm = region(12800, [P, 8, NB])
        gsi = region(13200, [P, 2, NB], i32)
        cnt = region(13300, [P, 2, NB])
        base = region(13400, [P, NB])
        gcmp = region(26100, [GP, GC, NW])
        gw = region(13450, [P, 2, GC])
        gwi = region(13470, [P, 2, GC], i32)
        pos_slot = region(13500, [SP_, 2, SU], i32)
        rec_slot = region(13550, [SP_, 2, SU, 2], i32)
        gm = sb("gm", [P, 2, 2 * H2]); flag = sb("flag", [P, 2]); flagi = sb("flagi", [P, 1], i32)

        w_attn = sb("w_attn", [D, 2]); b_attn = sb("b_attn", [P, 1])
        w_proj = region(13800, [D, D + DE]); w_a1 = sb("w_a1", [D, D]); w_a2 = region(13900, [D, D])
        b_apply = sb("b_apply", [P, D]); w_pa = sb("w_pa", [D + DE, D])
        w1t = region(14000, [D, H1, D]); a1v = region(14520, [D, H1, 2]); mk = region(14600, [D, H1, D])
        w_s1 = sb("w_s1", [D, 2 * H1]); w_m1 = sb("w_m1", [P, H1 // 2, D])
        w_2 = sb("w_2", [D, D + 2 * H2]); a2b = region(15120, [D, 2, D]); w_3 = sb("w_3", [D, D + 2])
        a3b = region(15260, [D, 2, D]); wtmp = region(15400, [D, 2, D])
        vec = sb("vec", [P, 8, D])
        w_sage = sb("w_sage", [P, 2, D])

        ps_t = ps("ps_t", [P, 2, 512])
        ps_x = ps("ps_x", [P, 2, 512])
        ps_a = ps("ps_a", [P, 2, 1024])

        loaded_w = sem("loaded_w"); loaded_x = sem("loaded_x"); loaded_rec = sem("loaded_rec")
        pool_consts = sem("pool_consts"); rec_half = sem("rec_half"); half_staged = sem("half_staged")
        consts_ready = sem("consts_ready")
        dve_chain = sem("dve_chain")
        loop_count = sem("loop_count"); loop_ind = sem("loop_ind"); loop_cum = sem("loop_cum")
        loop_pos = sem("loop_pos")
        counted = sem("counted"); totals = sem("totals"); sorted_ = sem("sorted")
        groups_ready = sem("groups_ready"); groups_stored = sem("groups_stored")
        starts_loaded = sem("starts_loaded"); dst_runs = sem("dst_runs")
        records_stored = sem("records_stored"); pad_ready = sem("pad_ready")
        pad_stored = sem("pad_stored")
        pos_staged = sem("pos_staged"); rec_staged = sem("rec_staged")
        scattered = [sem(f"scattered{i}") for i in range(2)]
        scatter_done = sem("scatter_done")
        weights_made = sem("weights_made"); weights_mm = sem("weights_mm")
        pool_steps = sem("pool_steps"); pe_steps = sem("pe_steps")
        score_max = sem("score_max"); score_all = sem("score_all")
        flag_ready = sem("flag_ready"); side_free = sem("side_free"); side_loaded = sem("side_loaded"); side_ready = sem("side_ready")
        table_made = sem("table_made"); table_written = sem("table_written")
        act_ask = sem("act_ask"); act_done = sem("act_done")
        final_made = sem("final_made"); out_written = sem("out_written")

        class Pass:
            pass

        passes = []
        for p in range(6):
            q = Pass()
            q.n, q.H, q.F, q.W, q.side = p, HEADS[p], ROW[p], OUTW[p], SIDE[p]
            q.banks = -(-q.W // 512)
            q.idx_staged = sem(f"p{p}_idx_staged")
            q.begun = sem(f"p{p}_begun")
            q.landed = [sem(f"p{p}_landed{s}") for s in range(U)]
            q.attr_landed = [sem(f"p{p}_attr{s}") for s in range(U)] if p == 0 else None
            q.onehot_made = sem(f"p{p}_onehot_made")
            q.summed = sem(f"p{p}_summed")
            q.added = sem(f"p{p}_added")
            if q.H:
                q.transposed = sem(f"p{p}_transposed")
                q.copied = sem(f"p{p}_copied")
                q.expanded = sem(f"p{p}_expanded")
                q.scored = sem(f"p{p}_scored")
                q.maxed = sem(f"p{p}_maxed")
                q.clipped = sem(f"p{p}_clipped")
                q.weighed = sem(f"p{p}_weighed")
                q.rhs_made = sem(f"p{p}_rhs_made")
            if p in (0, 2, 3):
                q.m_idx = sem(f"p{p}_m_idx"); q.m_landed = sem(f"p{p}_m_landed")
                q.m_masked = sem(f"p{p}_m_masked"); q.m_transposed = sem(f"p{p}_m_transposed")
                q.m_chain = sem(f"p{p}_m_chain")
            if p == 0:
                q.rhs_half = sem(f"p{p}_rhs_half")
            passes.append(q)

        class Projection:
            pass

        def projection(chunks, dst, at, width):
            j = Projection()
            j.chunks, j.dst, j.at, j.N = chunks, dst, at, width
            j.before = numbered[0] * (NP // WB)
            numbered[0] += 1
            j.number = numbered[0]
            j.ready, j.staged, j.transposed, j.copied, j.multiplied, j.stored = proj_sems
            return j

        numbered = [0]
        proj_sems = [sem(f"proj_{n}") for n in ("ready", "staged", "transposed", "copied", "multiplied", "stored")]

        J = {
            "s0": projection([(D, w_attn[:, :])], tab, D, 2),
            "o0": projection([(D + DE, w_pa[:, :]), (D, w_a1[:, :])], pre, 0, D),
            "s1": projection([(D, w_s1[:, :])], tab, D, 2 * H1),
            "o1": projection([(P, w_m1[:, c, :]) for c in range(H1 // 2)], pre, 0, D),
            "s2": projection([(D, w_2[:, :])], tab, 0, D + 2 * H2),
            "s3": projection([(D, w_3[:, :])], tab, 0, D + 2),
            "o4": projection([(P, w_sage[:, 0, :])], pre, 0, D),
            "o5": projection([(P, w_sage[:, 1, :])], pre, 0, D),
        }
        ORDER = [("s0", 0, "o0"), ("s1", 1, "o1"), ("s2", 2, None), ("s3", 3, None),
                 (None, 4, "o4"), (None, 5, "o5")]

        block = ctx.enter_context(nc.Block())

        @block.sync
        def _(sp):
            sp.dma_start(flat_rec, a["rec"][0:E, :].rearrange("(p c) t -> p c t", p=SP_))\
              .then_inc(loaded_rec, 16)
            sp.wait_ge(consts_ready, 1)
            sp.dma_start(xcur[:, 0:FULL, :], a["x"][0:FULL * P, :].rearrange("(w p) f -> p w f", p=P))\
              .then_inc(loaded_x, 16)
            sp.dma_start(xcur[0:TAIL, FULL, :], a["x"][FULL * P:N, :]).then_inc(loaded_x, 16)
            loads = [
                (w_attn[:, :], a["attn_wT"]), (b_attn[:, :], a["attn_b"].partition_broadcast(P)),
                (w_proj[:, :], a["proj_w"]), (w_a1[:, :], a["apply_wT"][0:D, :]),
                (w_a2[:, :], a["apply_wT"][D:2 * D, :]), (b_apply[:, :], a["apply_b"].partition_broadcast(P)),
                (w1t[:, :, :], a["W_t"]), (a1v[:, :, :], a["a_t"]), (mk[:, :, :], a["merge_t"]),
                (w_2[:, 0:D], a["W1"]), (w_3[:, 0:D], a["W2"]),
                (a2b[:, 0, :], a["a1_src"].partition_broadcast(D)),
                (a2b[:, 1, :], a["a1_dst"].partition_broadcast(D)),
                (a3b[:, 0, :], a["a2_src"].partition_broadcast(D)),
                (a3b[:, 1, :], a["a2_dst"].partition_broadcast(D)),
                (w_sage[0:D, 0, :], a["Wl0T"]), (w_sage[D:P, 0, :], a["Wr0T"]),
                (w_sage[0:D, 1, :], a["Wl1T"]), (w_sage[D:P, 1, :], a["Wr1T"]),
            ] + [(vec[:, i, :], a[n].partition_broadcast(P)) for i, n in
                 enumerate(("b1", "ln1_g", "ln1_b", "b2", "ln2_g", "ln2_b", "bl0", "bl1"))]
            for dst, src in loads:
                sp.dma_start(dst, src).then_inc(loaded_w, 16)
            sp.wait_ge(pad_ready, 2)
            rec_flat = records["src"].rearrange("(p c) t -> p c t", p=P)
            per = NG * G
            for c in range(0, per, 1024):
                n = min(1024, per - c)
                sp.dma_start(rec_flat[:, c:c + n, :], pad[:, 0:n, :]).then_inc(pad_stored, 16)
            sp.wait_ge(groups_ready, 1)
            sp.dma_start(group_window["dst"].rearrange("(p c) -> p c", p=GP), gwi[0:GP, 0, :]).then_inc(groups_stored, 16)
            sp.dma_start(group_start.rearrange("(p c) -> p c", p=GP), gwi[0:GP, 1, :]).then_inc(groups_stored, 16)
            sp.wait_ge(groups_stored, 32)
            sp.dma_start(srow[:, :], group_start.rearrange("(a n) -> a n", a=1)).then_inc(starts_loaded, 16)
            sp.wait_ge(groups_ready, 2)
            sp.dma_start(group_window["src"].rearrange("(p c) -> p c", p=GP), gwi[0:GP, 0, :]).then_inc(groups_stored, 16)
            sp.wait_ge(starts_loaded, 16)
            with sp.Fori(0, NG) as k:
                start = sp.value_load(srow[0:1, bass.ds(k, 1)], min_val=0, max_val=E)
                sp.dma_start(grec[:, bass.ds(k * G, G), :],
                             a["rec"][bass.ds(start, GE), :].rearrange("(p g) t -> p g t", p=P))\
                  .then_inc(dst_runs, 16)
            sp.wait_ge(dst_runs, 16 * NG)
            sp.dma_start(records["dst"].rearrange("(k p g) t -> p k g t", p=P, g=G),
                         grec.rearrange("p (k g) t -> p k g t", g=G)).then_inc(records_stored, 16)

            def side(q, n):
                sp.wait_ge(side_free, n + 1)
                if q.side == "src":
                    sp.wait_ge(scatter_done, 1)
                sp.wait_ge(records_stored, 16)
                sp.wait_ge(groups_stored, 48)
                sp.dma_start(grec.rearrange("p (k g) t -> p k g t", g=G),
                             records[q.side].rearrange("(k p g) t -> p k g t", p=P, g=G)).then_inc(side_loaded, 16)
                sp.dma_start(wrow[:, :], group_window[q.side].rearrange("(a n) -> a n", a=1)).then_inc(side_loaded, 16)
                sp.dma_start(wbi[:, :], group_window[q.side].partition_broadcast(P)).then_inc(side_loaded, 16)

            for q in passes:
                sp.wait_ge(table_made, q.n + 1)
                sp.dma_start(tables[q.n].rearrange("(w p) f -> p w f", p=P), tab[:, :, 0:q.F])\
                  .then_inc(table_written, 16)
                if q.n in (0, 1, 2):
                    side(q, q.n)
                if q.n == 0:
                    def attr_load(k, s, turn):
                        start = sp.value_load(srow[0:1, bass.ds(k, 1)], min_val=0, max_val=E)
                        since(sp, q.rhs_made, k - U + 1)
                        sp.dma_start(attrs[:, s, :, :],
                                     a["attr"][bass.ds(start, GE), :].rearrange("(p g) f -> p g f", p=P))\
                          .then_inc(q.attr_landed[s], 16)
                    pipelined(sp, NG, U, [(0, attr_load)])
            sp.wait_ge(final_made, 1)
            sp.dma_start(out[0:FULL * P, :].rearrange("(w p) f -> p w f", p=P), xcur[:, 0:FULL, :]).then_inc(out_written, 16)
            sp.dma_start(out[FULL * P:N, :], xcur[0:TAIL, FULL, :]).then_inc(out_written, 16)
            sp.wait_ge(out_written, 32)

        @block.gpsimd
        def _(pool):
            nc.gpsimd.memset(xcur[:, :, :], 0.0).then_inc(consts_ready, 1)
            nc.gpsimd.iota(pad[:, :, 0:1], pattern=[[0, 1024]], base=BIG_NODE, channel_multiplier=0).then_inc(pad_ready, 1)
            nc.gpsimd.iota(pad[:, :, 1:2], pattern=[[0, 1024]], base=0, channel_multiplier=0).then_inc(pad_ready, 1)
            nc.gpsimd.memset(ones[:, :], 1.0).then_inc(pool_consts, 1)
            nc.gpsimd.iota(iota_ni[:, :], pattern=[[1, P]], base=0, channel_multiplier=0).then_inc(pool_consts, 1)
            nc.gpsimd.iota(iota_gi[:, :], pattern=[[1, GC]], base=0, channel_multiplier=GC).then_inc(pool_consts, 1)
            pool.wait_ge(pool_consts, 3)
            nc.gpsimd.affine_select(out=ident[:, :], in_=ones[:, :], pattern=[[-1, P]], compare_op=ALU.is_equal,
                                    fill=0.0, base=0, channel_multiplier=1).then_inc(pool_consts, 1)
            nc.gpsimd.affine_select(out=below[:, :], in_=ones[:, :], pattern=[[1, P]], compare_op=ALU.is_gt,
                                    fill=0.0, base=0, channel_multiplier=-1).then_inc(pool_consts, 1)

            def scatter(k, s, turn):
                pool.wait_ge(pad_stored, 16 * -(-NG * G // 1024))
                since(pool, rec_staged, k + 1)
                since(pool, pos_staged, k + 1)
                pool.sem_inc(pool_steps, 1)
                for c in range(SU):
                    pool.indirect_dma_start(records["src"], bass.IndirectOffsetOnAxis(ap=pos_slot[:, s, c:c + 1], axis=0),
                                            rec_slot[:, s, c, :], None).then_inc(scattered[s], 16)
            pipelined(pool, SC // SU, 2, [(0, scatter)])
            for s in range(2):
                pool.wait_ge(scattered[s], 16 * SC // 2)
            pool.sem_inc(scatter_done, 1)

            asks = 0
            for q in passes:
                if q.n in (0, 2, 3):
                    asks += 1
                    pool.wait_ge(score_max, asks)
                    nc.gpsimd.partition_all_reduce(gm[:, 1, 0:2 * q.H], gm[:, 0, 0:2 * q.H], P, RMAX).then_inc(score_all, 1)
                    pool.wait_ge(flag_ready, asks)
                    pool.wait_ge(table_written, 16 * (q.n + 1))
                    wide = pool.value_load(flagi[0:1, 0:1], min_val=0, max_val=1)
                    with pool.If(wide > 0):
                        with pool.Fori(0, NG) as k:
                            pool.wait_ge(q.m_idx, k + 1)
                            pool.sem_inc(pool_steps, 1)
                            for g in range(G):
                                pool.indirect_dma_start(rows[:, 0, g * q.F:(g + 1) * q.F], None, tables[q.n],
                                                        bass.IndirectOffsetOnAxis(ap=idx_slot[:, 0, g:g + 1], axis=0))\
                                    .then_inc(q.m_landed, 16)
                    pool.sem_inc(pool_steps, 1)

                def gather(k, s, turn):
                    pool.wait_ge(table_written, 16 * (q.n + 1))
                    since(pool, q.idx_staged, k + 1)
                    if q.H:
                        since(pool, q.rhs_made, k - U + 1)
                    else:
                        since(pool, q.summed, k - U + 1)
                    pool.sem_inc(pool_steps, 1)
                    for g in range(G):
                        pool.indirect_dma_start(rows[:, s, g * q.F:(g + 1) * q.F], None, tables[q.n],
                                                bass.IndirectOffsetOnAxis(ap=idx_slot[:, s, g:g + 1], axis=0))\
                            .then_inc(q.landed[s], 16)
                pipelined(pool, NG, U, [(0, gather)])

        @block.scalar
        def _(act):
            def stage_pos(k, s, turn):
                act.wait_ge(sorted_, 1)
                since(act, scattered[s], 16 * SU * turn)
                nc.scalar.copy(pos_slot[:, s, :], posi[:, bass.ds(k * SU, SU)]).then_inc(pos_staged, 1)
            pipelined(act, SC // SU, 2, [(0, stage_pos)])

            def project(j):
                act.wait_ge(j.ready, j.number)

                def evacuate(b, s, turn):
                    since(act, j.transposed, b + 1, j.before)
                    since(act, j.multiplied, b - 1, j.before)
                    same = all(K == P for K, _ in j.chunks)
                    parts = [(0, P, len(j.chunks))] if same else [(c, K, 1) for c, (K, _) in enumerate(j.chunks)]
                    for n, (c, K, m) in enumerate(parts):
                        ins = nc.scalar.copy(node_t[0:K, s, c * WB * P:(c + m) * WB * P],
                                             ps_a[0:K, s, c * WB * P:(c + m) * WB * P])
                    ins.then_inc(j.copied, 1)
                pipelined(act, NP // WB, 2, [(1, evacuate)])

            def edges(q):
                def stage_idx(k, s, turn):
                    act.wait_ge(q.begun, 1)
                    since(act, q.landed[s], 16 * G * turn)
                    nc.scalar.copy(idx_slot[:, s, :], idx[:, bass.ds(k * G, G)]).then_inc(q.idx_staged, 1)

                def copy_onehot(k, s, turn):
                    since(act, q.transposed, k + 1)
                    since(act, q.expanded, k - 1)
                    nc.scalar.copy(onehot_t[:, s % 2, :, :].rearrange("p g n -> p (g n)"), ps_t[:, s % 2, :])\
                        .then_inc(q.copied, 1)

                def weigh(k, s, turn):
                    since(act, q.clipped, k + 1)
                    since(act, q.summed, k - 1)
                    w = rhs[:, s % 2, 0:G * q.W].rearrange("p (g f) -> p g f", g=G)
                    nc.scalar.activation(w[:, :, q.W - q.H:q.W],
                                         zmax[:, s % 2, 0:G * q.H].rearrange("p (g h) -> p g h", g=G), ACT.Exp)\
                        .then_inc(q.weighed, 1)
                if q.H:
                    pipelined(act, NG, U, [(1, weigh), (3, copy_onehot), (4, stage_idx)])
                else:
                    pipelined(act, NG, U, [(4, stage_idx)])

            asked = [0]

            def serve(func, out_, in_):
                asked[0] += 1
                act.wait_ge(act_ask, asked[0])
                nc.scalar.activation(out_, in_, func).then_inc(act_done, 1)

            for s_name, p, o_name in ORDER:
                q = passes[p]
                if s_name:
                    project(J[s_name])
                edges(q)
                if p in (2, 3):
                    serve(ACT.Exp, mtmp[:, :, 0:q.H], mtmp[:, :, 0:q.H])
                    serve(ACT.Sqrt, stat[:, :], stat[:, :])
                    serve(ACT.Exp, tmp, tmp)
                if o_name:
                    project(J[o_name])
                if p in (4, 5):
                    serve(ACT.Sqrt, stat[:, :], stat[:, :])
                if p != 2 and p != 4:
                    serve(ACT.Sqrt, stat[:, :], stat[:, :])

        @block.tensor
        def _(pe):
            for n in range(2):
                pe.wait_ge(pool_consts, 5)
                pe.wait_ge(counted, n + 1)
                nc.tensor.matmul(ps_x[:, n, 0:NB], ones[0:SP_, :], cnt[0:SP_, n, :], start=True, stop=True).then_inc(totals, 1)
                if n == 1:
                    nc.tensor.matmul(ps_t[0:SP_, 0, 0:NB], below[0:SP_, 0:SP_], cnt[0:SP_, 1, :],
                                     start=True, stop=True).then_inc(totals, 1)
            pe.wait_ge(loaded_w, 16 * 27)
            nc.tensor.matmul(ps_a[0:D + DE, 0, 0:D], w_proj[:, :], w_a2[:, :], start=True, stop=True)
            for h in range(H1):
                nc.tensor.matmul(ps_a[0:D, 0, 64 + 2 * h:66 + 2 * h], w1t[:, h, :], a1v[:, h, :], start=True, stop=True)
            for h in range(H1):
                c = h // 2
                ins = nc.tensor.matmul(ps_a[:, 1, h * D:(h + 1) * D], w1t[:, 2 * c:2 * c + 2, :].rearrange("u a f -> u (a f)"),
                                       mk[:, h, :], start=True, stop=True)
            ins.then_inc(weights_mm, 1)

            def project(j):
                pe.wait_ge(j.ready, j.number)

                def transpose(b, s, turn):
                    since(pe, j.staged, b + 1, j.before)
                    since(pe, j.copied, b - 1, j.before)
                    pe.sem_inc(pe_steps, 1)
                    for c, (K, _) in enumerate(j.chunks):
                        for w in range(WB):
                            at = (w * len(j.chunks) + c) * P
                            o = (c * WB + w) * P
                            ins = nc.tensor.transpose(ps_a[0:K, s, o:o + P], staged[:, s, at:at + K], ident[:, :])
                    ins.then_inc(j.transposed, 1)

                def multiply(b, s, turn):
                    since(pe, j.copied, b + 1, j.before)
                    since(pe, j.stored, b - 1, j.before)
                    for w in range(WB):
                        for c, (K, weight) in enumerate(j.chunks):
                            o = (c * WB + w) * P
                            ins = nc.tensor.matmul(ps_x[:, s, w * j.N:(w + 1) * j.N], node_t[0:K, s, o:o + P], weight,
                                                   start=(c == 0), stop=(c == len(j.chunks) - 1))
                    ins.then_inc(j.multiplied, 1)
                pipelined(pe, NP // WB, 2, [(1, transpose), (0, multiply)])

            def edges(q):
                window = {}

                def load_windows(i):
                    for s in range(2, U + 2):
                        if not isinstance(i, int) or i * U + s < NG:
                            window[s % U] = pe.value_load(wrow[0:1, bass.ds(i * U + s, 1)], min_val=0, max_val=NW)

                def transpose(k, s, turn):
                    since(pe, q.onehot_made, k + 1)
                    since(pe, q.copied, k - 1)
                    for g in range(G):
                        ins = nc.tensor.transpose(ps_t[:, s % 2, g * P:(g + 1) * P], onehot[:, s, g, :], ident[:, :])
                    ins.then_inc(q.transposed, 1)

                def expand(k, s, turn):
                    w = window[s] if not isinstance(k, int) or k > 1 else \
                        pe.value_load(wrow[0:1, k:k + 1], min_val=0, max_val=NW)
                    since(pe, q.copied, k + 1)
                    since(pe, q.scored, 2 * (k - 1))
                    for g in range(G):
                        for part in range(3):
                            ins = nc.tensor.matmul(ps_x[:, s % 2, g * 2 * q.H:(g + 1) * 2 * q.H], onehot_t[:, s % 2, g, :],
                                                   ntab3[:, part, bass.ds(w, 1), 0:2 * q.H].rearrange("p a h -> p (a h)"),
                                                   start=(part == 0), stop=(part == 2))
                    ins.then_inc(q.expanded, 1)

                def total(k, s, turn):
                    if q.H:
                        since(pe, q.rhs_made, k + 1)
                        r = rhs[:, s % 2, 0:G * q.W].rearrange("p (g f) -> p g f", g=G)
                    else:
                        since(pe, q.landed[s], 16 * G * (turn + 1))
                        since(pe, q.onehot_made, k + 1)
                        r = rows[:, s, 0:G * q.F].rearrange("p (g f) -> p g f", g=G)
                    since(pe, q.added, k - 1)
                    for b in range(q.banks):
                        n = q.W // q.banks
                        for g in range(G):
                            ins = nc.tensor.matmul(ps_a[:, s % 2, b * 512:b * 512 + n], onehot[:, s, g, :],
                                                   r[:, g, b * n:(b + 1) * n], start=(g == 0), stop=(g == G - 1))
                    ins.then_inc(q.summed, 1)
                pe.wait_ge(q.begun, 1)
                if q.H:
                    pipelined(pe, NG, U, [(0, total), (2, expand), (3, transpose)], load_windows)
                else:
                    pipelined(pe, NG, U, [(0, total)])

            def segment_maxima(q):
                pe.wait_ge(flag_ready, (0, 2, 3).index(q.n) + 1)
                wide = pe.value_load(flagi[0:1, 0:1], min_val=0, max_val=1)
                with pe.If(wide > 0):
                    with pe.Fori(0, NG * G * q.H) as t:
                        pe.wait_ge(q.m_masked, t + 1)
                        nc.tensor.transpose(ps_t[:, 0, 0:P], onehot[:, 0, 0, :], ident[:, :]).then_inc(q.m_transposed, 1)
                pe.sem_inc(pe_steps, 1)

            for s_name, p, o_name in ORDER:
                if s_name:
                    project(J[s_name])
                if p in (0, 2, 3):
                    segment_maxima(passes[p])
                edges(passes[p])
                if o_name:
                    project(J[o_name])

        @block.vector
        def _(dve):
            V = nc.vector
            link = Chain(dve, dve_chain)
            dve.wait_ge(pool_consts, 5)
            link(V.tensor_copy(iota_n[:, :], iota_ni[:, :]))
            link(V.tensor_copy(iota_g[:, :], iota_gi[:, :]))
            link(V.memset(cnt[:, :, :], 0.0))

            dve.wait_ge(loaded_rec, 16)
            for n, col in ((0, 1), (1, 0)):
                link(V.tensor_scalar(keyi, flat_rec[:, :, col], 7, None, ALU.logical_shift_right))
                link(V.tensor_copy(keyw, keyi))
                with dve.Fori(0, NW) as w:
                    V.tensor_scalar(ind, keyw, iota_n[0:SP_, bass.ds(w, 1)], None, ALU.is_equal, ALU.add,
                                    accum_out=cnt[0:SP_, n, bass.ds(w, 1)]).then_inc(loop_count, 1)
                    dve.wait_ge(loop_count, w + 1 + n * NW)
                dve.sem_inc(counted, 1)

            def group_tables(n):
                dve.wait_ge(totals, 1 if n == 0 else 3)
                tot, ng, gend, gstart, off, delta, dd, ong = (gsm[:, i, :] for i in range(8))
                link(V.memset(ong, 1.0))
                link(V.tensor_copy(tot, ps_x[:, n, 0:NB]))
                link(V.tensor_scalar(ng, tot, float(GE - 1), None, ALU.add))
                link(V.tensor_copy(gsi[:, 0, :], ng))
                link(V.tensor_scalar(gsi[:, 1, :], gsi[:, 0, :], GE.bit_length() - 1, None, ALU.logical_shift_right))
                link(V.tensor_copy(ng, gsi[:, 1, :]))
                link(V.tensor_tensor_scan(gend, ong, ng, 0.0, ALU.mult, ALU.add))
                link(V.tensor_tensor(gstart, gend, ng, ALU.subtract))
                en = gend[0:GP, 0:NW].unsqueeze(1).to_broadcast([GP, GC, NW])
                ig = iota_g[0:GP, :].unsqueeze(2).to_broadcast([GP, GC, NW])
                link(V.tensor_tensor(gcmp, en, ig, ALU.is_le))
                link(V.tensor_reduce(gw[0:GP, 0, :], gcmp, AX, ALU.add))
                if n == 0:
                    link(V.tensor_tensor_scan(off, ong, tot, 0.0, ALU.mult, ALU.add))
                    link(V.tensor_tensor(off, off, tot, ALU.subtract))
                    link(V.scalar_tensor_tensor(delta, gstart, -float(GE), off, ALU.mult, ALU.add))
                    link(V.tensor_tensor(dd[:, 0:NW], delta[:, 1:NB], delta[:, 0:NW], ALU.subtract))
                    link(V.tensor_tensor(gcmp, gcmp, dd[0:GP, 0:NW].unsqueeze(1).to_broadcast([GP, GC, NW]), ALU.mult))
                    link(V.tensor_reduce(gw[0:GP, 1, :], gcmp, AX, ALU.add))
                    link(V.scalar_tensor_tensor(gw[0:GP, 1, :], iota_g[0:GP, :], float(GE), gw[0:GP, 1, :], ALU.mult, ALU.add))
                    link(V.tensor_scalar(gw[0:GP, 1, :], gw[0:GP, 1, :], float(E), None, ALU.min))
                else:
                    dve.wait_ge(groups_stored, 32)
                link(V.tensor_copy(gwi[0:GP, :, :], gw[0:GP, :, :]))
                dve.sem_inc(groups_ready, 1)
                return gstart

            group_tables(0)
            gstart = group_tables(1)
            link(V.scalar_tensor_tensor(base[0:SP_, :], gstart[0:SP_, :], float(GE), ps_t[0:SP_, 0, 0:NB],
                                        ALU.mult, ALU.add))
            link(V.memset(pos, 0.0))
            with dve.Fori(0, NW) as w:
                V.tensor_scalar(ind, keyw, iota_n[0:SP_, bass.ds(w, 1)], None, ALU.is_equal).then_inc(loop_ind, 1)
                dve.wait_ge(loop_ind, w + 1)
                V.tensor_tensor_scan(cum, ind, ind, base[0:SP_, bass.ds(w, 1)], ALU.add, ALU.max).then_inc(loop_cum, 1)
                dve.wait_ge(totals, 3)
                dve.wait_ge(loop_cum, w + 1)
                V.copy_predicated(pos, ind.bitcast(i32), cum).then_inc(loop_pos, 1)
                dve.wait_ge(loop_pos, w + 1)
            link(V.tensor_scalar(posi, pos, -1.0, None, ALU.add))
            dve.sem_inc(sorted_, 1)

            dve.wait_ge(loaded_w, 16 * 27)
            dve.wait_ge(weights_mm, 1)
            link(V.tensor_copy(w_pa[:, :], ps_a[0:D + DE, 0, 0:D]))
            sv = ps_a[0:D, 0, 64:64 + 2 * H1].rearrange("p (h t) -> p t h", t=2)
            link(V.tensor_copy(w_s1[:, 0:H1], sv[:, 1, :]))
            link(V.tensor_copy(w_s1[:, H1:2 * H1], sv[:, 0, :]))
            pm = ps_a[:, 1, 0:512].rearrange("p (c a f) -> p c a f", c=H1 // 2, a=2)
            link(V.tensor_copy(w_m1[0:D, :, :], pm[0:D, :, 0, :]))
            link(V.tensor_copy(w_m1[D:P, :, :], pm[D:P, :, 1, :]))
            for t in range(2):
                link(V.tensor_tensor(wtmp[:, t, :], w_2[:, 0:D], a2b[:, t, :], ALU.mult))
                link(V.tensor_reduce(w_2[:, D + t * H2:D + (t + 1) * H2],
                                     wtmp[:, t, :].rearrange("p (h c) -> p h c", h=H2), AX, ALU.add))
                link(V.tensor_tensor(wtmp[:, t, :], w_3[:, 0:D], a3b[:, t, :], ALU.mult))
                link(V.tensor_reduce(w_3[:, D + t:D + t + 1], wtmp[:, t, :], AX, ALU.add))
            dve.wait_ge(loaded_x, 32)

            def stage_rec(k, s, turn):
                dve.wait_ge(loaded_rec, 16)
                since(dve, scattered[s], 16 * SU * turn)
                V.tensor_copy(rec_slot[:, s, :, 0:1], flat_rec[:, bass.ds(k * SU, SU), 0:1]).then_inc(rec_half, 1)
                V.tensor_copy(rec_slot[:, s, :, 1:2], flat_rec[:, bass.ds(k * SU, SU), 1:2]).then_inc(rec_staged, 1)
            pipelined(dve, SC // SU, 2, [(0, stage_rec)])

            def project(j, stage_ops):
                dve.sem_inc(j.ready, 1)

                def stage(b, s, turn):
                    since(dve, j.transposed, b - 1, j.before)
                    o = staged[:, s, 0:WB * len(j.chunks) * P].rearrange("p (w c) -> p w c", w=WB)
                    stage_ops(b, o, j.staged)

                def store(b, s, turn):
                    dve.wait_ge(j.ready, j.number)
                    since(dve, j.multiplied, b + 1, j.before)
                    V.tensor_copy(j.dst[:, bass.ds(b * WB, WB), j.at:j.at + j.N],
                                  ps_x[:, s, 0:WB * j.N].rearrange("p (w n) -> p w n", w=WB)).then_inc(j.stored, 1)
                pipelined(dve, NP // WB, 2, [(2, stage), (0, store)])
                dve.wait_ge(j.stored, NP // WB + j.before)

            def stage_copy(src, width):
                def ops(b, o, done):
                    dve.wait_ge(loaded_x, 32)
                    V.tensor_copy(o[:, :, 0:width], src[:, bass.ds(b * WB, WB), 0:width]).then_inc(done, 1)
                return ops

            def per(v, n, shape):
                return v.unsqueeze(n).to_broadcast(shape)

            def bc(v):
                return v.unsqueeze(1).to_broadcast([P, NP, D])

            full = [P, NP, D]
            asked = [0]

            def ask():
                asked[0] += 1
                dve.sem_inc(act_ask, 1)
                dve.wait_ge(act_done, asked[0])

            def normalise(v):
                link(V.tensor_reduce(stat[:, :], v, AX, ALU.add))
                link(V.tensor_scalar(stat[:, :], stat[:, :], 1.0 / D, None, ALU.mult))
                link(V.tensor_tensor(v, v, per(stat[:, :], 2, full), ALU.subtract))
                link(V.tensor_tensor(tmp, v, v, ALU.mult))
                link(V.tensor_reduce(stat[:, :], tmp, AX, ALU.add))
                link(V.tensor_scalar(stat[:, :], stat[:, :], 1.0 / D, 1e-5, ALU.mult, ALU.add))
                ask()
                link(V.reciprocal(stat[:, :], stat[:, :]))
                link(V.tensor_tensor(v, v, per(stat[:, :], 2, full), ALU.mult))

            def load_side(n):
                dve.sem_inc(side_free, 1)
                dve.wait_ge(side_loaded, 48 * (n + 1))
                key, other = (1, 0) if n != 1 else (0, 1)
                link(V.tensor_copy(idx[:, :], grec[:, :, other]))
                link(V.tensor_scalar(wbi[:, :], wbi[:, :], 7, None, ALU.logical_shift_left))
                link(V.tensor_copy(wb[:, :], wbi[:, :]))
                link(V.tensor_tensor(local[:, :].rearrange("p (k g) -> p k g", g=G),
                                     grec[:, :, key].rearrange("p (k g) -> p k g", g=G),
                                     wb[:, :].unsqueeze(2).to_broadcast([P, NG, G]), ALU.subtract))

            maxes = [0]

            def segment_maxima(q):
                H = q.H
                chain = [0]

                with dve.Fori(0, NG) as k:
                    w = dve.value_load(wrow[0:1, bass.ds(k, 1)], min_val=0, max_val=NW)
                    V.tensor_copy(idx_slot[:, 0, :], idx[:, bass.ds(k * G, G)]).then_inc(q.m_idx, 1)
                    dve.wait_ge(q.m_landed, k * (16 * G) + 16 * G)
                    links = 3 * G * H
                    n = 0
                    for g in range(G):
                        for h in range(H):
                            V.tensor_scalar(onehot[:, 1, 0, :], iota_n[:, :], local[:, bass.ds(k * G + g, 1)], -3e38,
                                            ALU.not_equal, ALU.mult).then_inc(q.m_chain, 1)
                            n += 1
                            dve.wait_ge(q.m_chain, k * links + n)
                            V.tensor_scalar(onehot[:, 0, 0, :], onehot[:, 1, 0, :],
                                            rows[:, 0, g * q.F + D + h:g * q.F + D + h + 1], None, ALU.add)\
                                .then_inc(q.m_masked, 1)
                            dve.wait_ge(q.m_transposed, k * (G * H) + g * H + h + 1)
                            V.tensor_reduce(stat[:, 0:1], ps_t[:, 0, 0:P], AX, ALU.max).then_inc(q.m_chain, 1)
                            n += 1
                            dve.wait_ge(q.m_chain, k * links + n)
                            m = mtmp[:, bass.ds(w, 1), h:h + 1].rearrange("p a h -> p (a h)")
                            V.tensor_tensor(m, m, stat[:, 0:1], ALU.max).then_inc(q.m_chain, 1)
                            n += 1
                            dve.wait_ge(q.m_chain, k * links + n)
                if q.n != 0:
                    link(V.tensor_tensor(mtmp[:, :, 0:H], mtmp[:, :, 0:H], tab[:, :, D:D + H], ALU.max))

            def key_table(q, src, key):
                H = q.H
                a_s, b_k = tab[:, :, src:src + H], tab[:, :, key:key + H]
                link(V.tensor_reduce(gm[:, 0, 0:H], a_s.rearrange("p w h -> p h w"), AX, ALU.max))
                link(V.tensor_reduce(gm[:, 0, H:2 * H], a_s.rearrange("p w h -> p h w"), AX, ALU.min, negate=True))
                dve.sem_inc(score_max, 1)
                maxes[0] += 1
                dve.wait_ge(score_all, maxes[0])
                m = mtmp[:, :, 0:H]
                link(V.tensor_copy(m, gm[:, 1, 0:H].unsqueeze(1).to_broadcast([P, NP, H])))
                link(V.tensor_tensor(gm[:, 0, 0:H], gm[:, 1, 0:H], gm[:, 1, H:2 * H], ALU.add))
                link(V.tensor_reduce(flag[:, 0:1], gm[:, 0, 0:H], AX, ALU.max))
                link(V.tensor_scalar(flag[:, 1:2], flag[:, 0:1], SPAN, None, ALU.is_gt))
                link(V.tensor_copy(flagi[:, :], flag[:, 1:2]))
                dve.sem_inc(flag_ready, 1)
                wide = dve.value_load(flagi[0:1, 0:1], min_val=0, max_val=1)
                before = link.n
                with dve.If(wide > 0):
                    link(V.tensor_scalar(m, gm[:, 1, H:2 * H].unsqueeze(1).to_broadcast([P, NP, H]), -1.0, None, ALU.mult))
                    segment_maxima(q)
                with dve.Else():
                    dve.sem_inc(dve_chain, link.n - before)
                link(V.tensor_tensor(m, b_k, m, ALU.add))
                link(V.scalar_tensor_tensor(m, m, SLOPE, m, ALU.mult, ALU.max))
                link(V.tensor_tensor(ntab[:, :, 0:H], b_k, m, ALU.subtract))
                link(V.scalar_tensor_tensor(ntab[:, :, H:2 * H], b_k, SLOPE, m, ALU.mult, ALU.subtract))

            def split_key_table(n):
                rest = ntab[:, :, 0:n]
                for part in range(3):
                    link(V.tensor_copy(ntab3[:, part, :, 0:n], rest))
                    if part < 2:
                        link(V.tensor_tensor(tmp[:, :, 0:n], rest, ntab3[:, part, :, 0:n], ALU.subtract))
                        rest = tmp[:, :, 0:n]

            def edges(q):
                if q.H:
                    split_key_table(2 * q.H)
                acc = acc_all[:, 0:NP * q.W].rearrange("p (w f) -> p w f", w=NP)
                link(V.memset(acc_all[:, 0:NP * q.W], 0.0))
                dve.sem_inc(q.begun, 1)
                window = {}

                def load_windows(i):
                    for s in range(U):
                        k = i * U + s - 2
                        if isinstance(i, int) and k < 0:
                            continue
                        window[(s - 2) % U] = dve.value_load(wrow[0:1, bass.ds(k, 1)], min_val=0, max_val=NW)

                def make_onehot(k, s, turn):
                    since(dve, q.summed, k - U + 1)
                    V.tensor_tensor(onehot[:, s, :, :], iota_n[:, :].unsqueeze(1).to_broadcast([P, G, P]),
                                    local[:, bass.ds(k * G, G)].unsqueeze(2).to_broadcast([P, G, P]), ALU.is_equal)\
                        .then_inc(q.onehot_made, 1)

                r = lambda s: rows[:, s, 0:G * q.F].rearrange("p (g f) -> p g f", g=G)
                o = lambda s: rhs[:, s % 2, 0:G * q.W].rearrange("p (g f) -> p g f", g=G)

                def score(k, s, turn):
                    H = q.H
                    since(dve, q.landed[s], 16 * G * (turn + 1))
                    since(dve, q.expanded, k + 1)
                    since(dve, q.maxed, k - 1)
                    share = ps_x[:, s % 2, 0:G * 2 * H].rearrange("p (g h) -> p g h", g=G)
                    t = t12[:, s % 2, :, :]
                    V.tensor_tensor(t[:, :, 0:H], share[:, :, 0:H], r(s)[:, :, D:D + H], ALU.add).then_inc(q.scored, 1)
                    V.scalar_tensor_tensor(t[:, :, H:2 * H], r(s)[:, :, D:D + H], SLOPE, share[:, :, H:2 * H],
                                           ALU.mult, ALU.add).then_inc(q.scored, 1)

                def larger(k, s, turn):
                    H = q.H
                    since(dve, q.scored, 2 * (k + 1))
                    since(dve, q.weighed, k - 1)
                    t = t12[:, s % 2, :, :]
                    V.tensor_tensor(zmax[:, s % 2, 0:G * H].rearrange("p (g h) -> p g h", g=G),
                                    t[:, :, 0:H], t[:, :, H:2 * H], ALU.max).then_inc(q.maxed, 1)

                def clip(k, s, turn):
                    since(dve, q.maxed, k + 1)
                    z = zmax[:, s % 2, 0:G * q.H]
                    if q.n == 1:
                        V.tensor_scalar(z, z, 2.0, -2.0, ALU.min, ALU.max).then_inc(q.clipped, 1)
                    else:
                        V.tensor_scalar(z, z, 0.0, None, ALU.min).then_inc(q.clipped, 1)

                def weight_rows(k, s, turn):
                    since(dve, q.weighed, k + 1)
                    x, w = r(s), o(s)
                    e = w[:, :, q.W - q.H:q.W]
                    if q.n == 0:
                        since(dve, q.attr_landed[s], 16 * (turn + 1))
                        V.tensor_tensor(w[:, :, 0:D], x[:, :, 0:D], e.to_broadcast([P, G, D]), ALU.mult).then_inc(q.rhs_half, 1)
                        V.tensor_tensor(w[:, :, D:D + DE], attrs[:, s, :, :], e.to_broadcast([P, G, DE]), ALU.mult)\
                            .then_inc(q.rhs_made, 1)
                    elif q.n == 1:
                        V.tensor_tensor(w[:, :, 0:H1 * D].rearrange("p g (h f) -> p g h f", h=H1),
                                        x[:, :, 0:D].unsqueeze(2).to_broadcast([P, G, H1, D]),
                                        e.unsqueeze(3).to_broadcast([P, G, H1, D]), ALU.mult).then_inc(q.rhs_made, 1)
                    else:
                        V.tensor_tensor(w[:, :, 0:D].rearrange("p g (h f) -> p g h f", h=q.H),
                                        x[:, :, 0:D].rearrange("p g (h f) -> p g h f", h=q.H),
                                        e.unsqueeze(3).to_broadcast([P, G, q.H, D // q.H]), ALU.mult).then_inc(q.rhs_made, 1)

                def add(k, s, turn):
                    w = window[s] if not isinstance(k, int) or k < NG - 2 else \
                        dve.value_load(wrow[0:1, k:k + 1], min_val=0, max_val=NW)
                    since(dve, q.added, k)
                    since(dve, q.summed, k + 1)
                    t = acc[:, bass.ds(w, 1), :].rearrange("p a (b f) -> p (a b) f", b=q.banks)
                    sums = ps_a[:, s % 2, :].rearrange("p (b f) -> p b f", f=512)[:, 0:q.banks, 0:q.W // q.banks]
                    V.tensor_tensor(t, sums, t, ALU.add).then_inc(q.added, 1)

                if q.H:
                    stages = [(-2, add), (0, weight_rows), (1, score), (3, make_onehot), (1, larger), (1, clip)]
                else:
                    stages = [(-2, add), (3, make_onehot)]
                pipelined(dve, NG, U, stages, load_windows)
                dve.wait_ge(q.added, NG)
                return acc

            def reciprocals(den, H, eps):
                d = rden[:, :, 0:H]
                if eps:
                    link(V.tensor_scalar(d, den, eps, None, ALU.add))
                else:
                    link(V.tensor_scalar(d, den, 0.0, None, ALU.is_equal))
                    link(V.tensor_tensor(d, d, den, ALU.add))
                link(V.reciprocal(d, d))

            project(J["s0"], stage_copy(xcur, D))
            link(V.tensor_scalar(tab[:, :, D + 1:D + 2], tab[:, :, D + 1:D + 2], b_attn[:, 0:1], None, ALU.add))
            link(V.tensor_copy(tab[:, :, 0:D], xcur[:, :, :]))
            dve.sem_inc(table_made, 1)
            dve.wait_ge(records_stored, 16)
            for s in range(2):
                dve.wait_ge(scattered[s], 16 * SC // 2)
            load_side(0)
            key_table(passes[0], D, D + 1)
            acc = edges(passes[0])
            reciprocals(acc[:, :, D + DE:D + DE + 1], 1, 0)

            def stage0(b, o, done):
                w = bass.ds(b * WB, WB)
                V.tensor_tensor(o[:, :, 0:D + DE], acc0[:, w, 0:D + DE], rden[:, w, 0:1].to_broadcast([P, WB, D + DE]),
                                ALU.mult).then_inc(half_staged, 1)
                V.tensor_copy(o[:, :, P:P + D], xcur[:, w, :]).then_inc(done, 1)
            acc0 = acc
            project(J["o0"], stage0)
            link(V.tensor_tensor(pre[:, :, :], pre[:, :, :], bc(b_apply[:, :]), ALU.add))
            link(V.scalar_tensor_tensor(xcur[:, :, :], pre[:, :, :], 0.0, xcur[:, :, :], ALU.max, ALU.add))
            normalise(xcur[:, :, :])

            project(J["s1"], stage_copy(xcur, D))
            link(V.tensor_copy(tab[:, :, 0:D], xcur[:, :, :]))
            dve.sem_inc(table_made, 1)
            link(V.tensor_copy(ntab[:, :, 0:H1], tab[:, :, D + H1:D + 2 * H1]))
            link(V.tensor_scalar(ntab[:, :, H1:2 * H1], tab[:, :, D + H1:D + 2 * H1], SLOPE, None, ALU.mult))
            load_side(1)
            acc1 = edges(passes[1])
            reciprocals(acc1[:, :, H1 * D:H1 * D + H1], H1, 0)

            def stage1(b, o, done):
                for w in range(WB):
                    ins = V.tensor_tensor(o[:, w, :].rearrange("p (h f) -> p h f", h=H1),
                                          acc1[:, bass.ds(b * WB + w, 1), 0:H1 * D].rearrange("p a (h f) -> p (a h) f", h=H1),
                                          rden[:, bass.ds(b * WB + w, 1), :].rearrange("p a h -> p (a h)").unsqueeze(2)
                                          .to_broadcast([P, H1, D]), ALU.mult)
                    ins.then_inc(half_staged if w == 0 else done, 1)
            project(J["o1"], stage1)
            link(V.scalar_tensor_tensor(pre[:, :, :], pre[:, :, :], SLOPE, pre[:, :, :], ALU.mult, ALU.max))
            link(V.tensor_tensor(xcur[:, :, :], xcur[:, :, :], pre[:, :, :], ALU.add))
            normalise(xcur[:, :, :])

            for p, j, src in ((2, "s2", xcur), (3, "s3", pre)):
                q, H = passes[p], HEADS[p]
                v0 = 0 if p == 2 else 3
                project(J[j], stage_copy(src, D))
                dve.sem_inc(table_made, 1)
                if p == 2:
                    load_side(2)
                key_table(q, D, D + H)
                acc = edges(q)
                s_, m = mtmp[:, :, 0:H], rden[:, :, 0:H]
                link(V.tensor_tensor(s_, tab[:, :, D:D + H], ntab[:, :, 0:H], ALU.add))
                link(V.scalar_tensor_tensor(m, tab[:, :, D:D + H], SLOPE, ntab[:, :, H:2 * H], ALU.mult, ALU.add))
                link(V.tensor_tensor(s_, s_, m, ALU.max))
                ask()
                for h in range(H):
                    c = slice(h * (D // H), (h + 1) * (D // H))
                    link(V.tensor_tensor(tmp[:, :, c], tab[:, :, c], mtmp[:, :, h:h + 1].to_broadcast([P, NP, D // H]), ALU.mult))
                link(V.tensor_tensor(pre[:, :, :], acc[:, :, 0:D], tmp, ALU.add))
                link(V.tensor_tensor(s_, s_, acc[:, :, D:D + H], ALU.add))
                reciprocals(s_, H, 1e-16)
                for h in range(H):
                    c = slice(h * (D // H), (h + 1) * (D // H))
                    link(V.tensor_tensor(pre[:, :, c], pre[:, :, c], rden[:, :, h:h + 1].to_broadcast([P, NP, D // H]), ALU.mult))
                link(V.tensor_tensor(pre[:, :, :], pre[:, :, :], bc(vec[:, v0, :]), ALU.add))
                normalise(pre[:, :, :])
                link(V.tensor_tensor(pre[:, :, :], pre[:, :, :], bc(vec[:, v0 + 1, :]), ALU.mult))
                link(V.tensor_tensor(pre[:, :, :], pre[:, :, :], bc(vec[:, v0 + 2, :]), ALU.add))
                link(V.tensor_scalar(tmp, pre[:, :, :], 0.0, None, ALU.min))
                ask()
                link(V.tensor_scalar(pre[:, :, :], pre[:, :, :], 0.0, -1.0, ALU.max, ALU.add))
                link(V.tensor_tensor(pre[:, :, :], pre[:, :, :], tmp, ALU.add))
            link(V.tensor_tensor(xcur[:, :, :], xcur[:, :, :], pre[:, :, :], ALU.add))
            normalise(xcur[:, :, :])

            for p, j, src in ((4, "o4", xcur), (5, "o5", pre)):
                q = passes[p]
                link(V.tensor_copy(tab[:, :, 0:D], src[:, :, :]))
                link(V.memset(tab[:, :, D:D + 1], 1.0))
                dve.sem_inc(table_made, 1)
                accs = edges(q)
                link(V.tensor_scalar(deginv[:, :].unsqueeze(2), accs[:, :, D:D + 1], 1.0, None, ALU.max))
                link(V.reciprocal(deginv[:, :], deginv[:, :]))

                def stage_sage(b, o, done, accs=accs):
                    w = bass.ds(b * WB, WB)
                    V.tensor_tensor(o[:, :, 0:D], accs[:, w, 0:D], deginv[:, w].unsqueeze(2).to_broadcast([P, WB, D]),
                                    ALU.mult).then_inc(half_staged, 1)
                    V.tensor_copy(o[:, :, D:2 * D], tab[:, w, 0:D]).then_inc(done, 1)
                project(J[j], stage_sage)
                link(V.tensor_tensor(pre[:, :, :], pre[:, :, :], bc(vec[:, 6 + p - 4, :]), ALU.add))
                link(V.tensor_tensor(tmp, pre[:, :, :], pre[:, :, :], ALU.mult))
                link(V.tensor_reduce(stat[:, :], tmp, AX, ALU.add))
                ask()
                link(V.tensor_scalar(stat[:, :], stat[:, :], 1e-12, None, ALU.max))
                link(V.reciprocal(stat[:, :], stat[:, :]))
                link(V.tensor_tensor(pre[:, :, :], pre[:, :, :], per(stat[:, :], 2, full), ALU.mult))
                link(V.tensor_scalar(pre[:, :, :], pre[:, :, :], 0.0, None, ALU.max))
            link(V.tensor_tensor(xcur[:, :, :], xcur[:, :, :], pre[:, :, :], ALU.add))
            normalise(xcur[:, :, :])
            dve.sem_inc(final_made, 1)


def kernel(x, src, dst, edge_attr_32, **w):
    import numpy as np
    import concourse.bacc as bacc
    from concourse.bass_utils import run_bass_kernel_spmd as run

    rec = np.empty((E + GE, 2), np.int32)
    rec[:E, 0], rec[:E, 1] = np.asarray(src), np.asarray(dst)
    rec[E:, 0], rec[E:, 1] = 0, BIG_NODE
    attr = np.zeros((E + GE, DE), np.float32)
    attr[:E] = np.asarray(edge_attr_32)
    v = {k: np.asarray(a) for k, a in w.items()}
    arrays = {
        "x": np.asarray(x), "rec": rec, "attr": attr,
        "attn_wT": v["L0_gnn_attn_w"].reshape(2, D).T, "attn_b": v["L0_gnn_attn_b"],
        "proj_w": v["L0_gnn_proj_w"], "apply_wT": v["L0_gnn_apply_w"].T, "apply_b": v["L0_gnn_apply_b"],
        "W_t": v["L1_gnn_W"].transpose(2, 0, 1), "a_t": v["L1_gnn_a"].reshape(H1, 2, D).transpose(2, 0, 1),
        "merge_t": v["L1_gnn_merge_kernel"].reshape(H1, D, D).transpose(1, 0, 2),
        "W1": v["L2_gnn_W1"], "W2": v["L2_gnn_W2"],
        "a1_src": v["L2_gnn_a1_src"].reshape(-1), "a1_dst": v["L2_gnn_a1_dst"].reshape(-1),
        "a2_src": v["L2_gnn_a2_src"].reshape(-1), "a2_dst": v["L2_gnn_a2_dst"].reshape(-1),
        "b1": v["L2_gnn_b1"], "b2": v["L2_gnn_b2"],
        "ln1_g": v["L2_gnn_ln1_g"], "ln1_b": v["L2_gnn_ln1_b"],
        "ln2_g": v["L2_gnn_ln2_g"], "ln2_b": v["L2_gnn_ln2_b"],
        "Wl0T": v["L3_gnn_Wl0"].T, "Wr0T": v["L3_gnn_Wr0"].T, "bl0": v["L3_gnn_bl0"],
        "Wl1T": v["L3_gnn_Wl1"].T, "Wr1T": v["L3_gnn_Wr1"].T, "bl1": v["L3_gnn_bl1"],
    }
    nc = bacc.Bacc("TRN2", target_bir_lowering=False, num_devices=1)
    ins, aps = {}, {}
    for name, arr in arrays.items():
        arr = np.ascontiguousarray(arr)
        ins[f"in_{name}"] = arr
        aps[name] = nc.dram_tensor(f"in_{name}", arr.shape, mybir.dt.from_np(arr.dtype), kind="ExternalInput").ap()
    out = nc.dram_tensor("out_0", (N, D), fp32, kind="ExternalOutput").ap()
    build(nc, aps, out)
    r = run(nc, [ins], core_ids=[0])
    return r.results[0]["out_0"]
```

```python
from contextlib import ExitStack

import concourse.bass as bass
from concourse import mybir

fp32 = mybir.dt.float32
i32 = mybir.dt.int32
bf16 = mybir.dt.bfloat16
ALU = mybir.AluOpType
ACT = mybir.ActivationFunctionType
AX = mybir.AxisListType.X
RMAX = bass.bass_isa.ReduceOp.max

P = 128
N, E, D, DE = 6250, 200000, 64, 32
NW = -(-N // P)
NB = NW + 1
WB = 2
NP = 52
FULL, TAIL = N // P, N % P
SP_, SC = 125, E // 125
SU = 16
H1, H2 = 8, 4
SLOPE = 0.2
SPAN = 16.0
BIG_NODE = 1 << 20


class Side:

    def __init__(self, name, number, G, U):
        self.name, self.number = name, number
        self.G = G
        self.GE = G * P
        self.U = U
        self.NG = -(-((E + NW * (self.GE - 1)) // self.GE) // U) * U
        self.T = self.NG * G
        self.GP = max(p for p in range(1, P + 1) if self.NG % p == 0)
        self.GC = self.NG // self.GP


BY = {"dst": Side("dst", 0, 2, 8), "src": Side("src", 1, 4, 4)}
UG = max(b.U * b.G for b in BY.values())
GMAX = max(b.G for b in BY.values())
GEMAX = max(b.GE for b in BY.values())
NGMAX = max(b.NG for b in BY.values())
TMAX = max(b.T for b in BY.values())
GCMAX = max(b.GC for b in BY.values())


class Chain:

    def __init__(self, eng, sem):
        self.eng, self.sem, self.n = eng, sem, 0

    def __call__(self, ins):
        self.n += 1
        ins.then_inc(self.sem, 1)
        self.eng.wait_ge(self.sem, self.n)


def since(eng, sem, value, before=0):
    if isinstance(value, int) and value <= 0:
        return
    eng.wait_ge(sem, value + before)


def pipelined(eng, count, unroll, stages):
    def step(i, s):
        for lag, stage in stages:
            k = i * unroll + s + lag
            if not isinstance(i, int) or 0 <= k < count:
                stage(k, (s + lag) % unroll, i + (s + lag) // unroll)

    ahead = max(lag for lag, _ in stages)
    behind = -min(lag for lag, _ in stages)
    assert ahead < unroll + 1 and behind <= unroll
    for k in range(-ahead, unroll):
        step(k // unroll, k % unroll)
    with eng.Fori(1, count // unroll - 1) as i:
        for s in range(unroll):
            step(i, s)
    for k in range(count - unroll, count + behind):
        step(k // unroll, k % unroll)


def build(nc, a, out):
    ctx = ExitStack()
    with ctx:
        def sb(name, shape, dt=fp32):
            return ctx.enter_context(nc.sbuf_tensor(name, shape, dt))

        def ps(name, shape):
            return ctx.enter_context(nc.psum_tensor(name, shape, fp32))

        def sem(name):
            return ctx.enter_context(nc.semaphore(name))

        def dram(name, shape, dt=fp32):
            return nc.dram_tensor(name, shape, dt, kind="Internal").ap()

        records = {s: dram(f"records_{s}", [BY[s].NG * BY[s].GE, 2], i32) for s in ("dst", "src")}
        group_window = {s: dram(f"group_window_{s}", [BY[s].NG], i32) for s in ("dst", "src")}
        group_start = dram("group_start", [BY["dst"].NG], i32)
        ROW = [65, 72, 68, 65, 65, 65]
        tables = [dram(f"table{p}", [NP * P, ROW[p]]) for p in range(6)]

        HEADS = [1, H1, H2, 1, 0, 0]
        OUTW = [D + DE + 1, H1 * D + H1, D + H2, D + 1, D + 1, D + 1]
        SIDE = ["dst", "src", "dst", "dst", "dst", "dst"]

        ACCF = NP * OUTW[1]
        acc_all = sb("acc_all", [P, ACCF])
        xcur = sb("xcur", [P, NP, D])
        pre = sb("pre", [P, NP, D])
        tab = sb("tab", [P, NP, 80])
        ntab = sb("ntab", [P, NP, 2 * H1])
        ntab3 = sb("ntab3", [P, 3, NP, 2 * H1], bf16)
        rden = sb("rden", [P, NP, H1])
        mtmp = acc_all[:, 19400:19400 + NP * H1].rearrange("p (w h) -> p w h", w=NP)
        deginv = sb("deginv", [P, NP])
        stat = sb("stat", [P, NP])
        idx = sb("idx", [P, TMAX], i32)
        local = sb("local", [P, TMAX])
        group_rows = sb("group_rows", [P, NGMAX], i32)
        wrow = group_rows[0:1, :]
        srow = group_rows[32:33, 0:BY["dst"].NG]
        idx_slot = sb("idx_slot", [P, UG], i32)
        rows = sb("rows", [P, UG * 72])
        attrs = sb("attrs", [P, UG, DE])
        flat_pre = pre[:, :, :].rearrange("p w f -> p (w f)")
        onehots = flat_pre[:, 0:UG * P].rearrange("p (t n) -> p t n", n=P)
        onehot_ts = flat_pre[:, UG * P:UG * P + GEMAX].bitcast(bf16).rearrange("p (t n) -> p t n", n=P)
        t12 = sb("t12", [P, 2, GMAX, 2 * H1])
        zmax = sb("zmax", [P, 2, GMAX * H1])
        rhs = sb("rhs", [P, 2, GMAX * OUTW[1]])
        flat_rhs = rhs[:, :, :].rearrange("p a b -> p (a b)")
        staged = flat_rhs[:, 0:2048].rearrange("p (a b) -> p a b", a=2)
        node_t = flat_rhs[:, 2048:4096].rearrange("p (a b) -> p a b", a=2)

        def region(at, shape, dt=fp32):
            n = 1
            for d in shape[1:]:
                n *= d
            v = acc_all[0:shape[0], at:at + n]
            if dt is not fp32:
                v = v.bitcast(dt)
            if len(shape) == 2:
                return v
            names = "abc"[:len(shape) - 1]
            return v.rearrange(f"p ({' '.join(names)}) -> p {' '.join(names)}",
                               **{c: d for c, d in zip(names, shape[1:])})

        flat_rec = region(0, [SP_, SC, 2], i32)
        keyw = region(2 * SC, [SP_, SC])
        keyi = region(3 * SC, [SP_, SC], i32)
        ind = region(4 * SC, [SP_, SC])
        cum = region(5 * SC, [SP_, SC])
        pos = region(6 * SC, [SP_, SC])
        posi = region(7 * SC, [SP_, SC], i32)
        grec = region(20000, [P, TMAX, 2], i32)
        wbi = region(23520, [P, NGMAX], i32)
        wb = region(24400, [P, NGMAX])
        pad = region(24000, [P, 1024, 2], i32)
        tmp = region(16000, [P, NP, D])
        assert 20000 + 2 * TMAX <= 23520

        ident = sb("ident", [P, P])
        ones = sb("ones", [P, P])
        below = sb("below", [P, P])
        iota_n = sb("iota_n", [P, P])
        iota_ni = sb("iota_ni", [P, P], i32)
        iota_g = sb("iota_g", [P, 2, GCMAX])
        iota_gi = sb("iota_gi", [P, 2, GCMAX], i32)
        gsm = region(12800, [P, 8, NB])
        gsi = region(13200, [P, 2, NB], i32)
        cnt = region(13300, [P, 2, NB])
        base = region(13400, [P, NB])
        gcmps = region(26100, [P, GCMAX, NW])
        gws = region(13450, [P, 2, GCMAX])
        gwis = region(13470, [P, 2, GCMAX], i32)
        pos_slot = region(13500, [SP_, 2, SU], i32)
        rec_slot = region(13550, [SP_, 2, SU, 2], i32)
        gm = sb("gm", [P, 2, 2 * H2]); flag = sb("flag", [P, 2]); flagi = sb("flagi", [P, 1], i32)

        w_attn = sb("w_attn", [D, 2]); b_attn = sb("b_attn", [P, 1])
        w_proj = region(13800, [D, D + DE]); w_a1 = sb("w_a1", [D, D]); w_a2 = region(13900, [D, D])
        b_apply = sb("b_apply", [P, D]); w_pa = sb("w_pa", [D + DE, D])
        w1t = region(14000, [D, H1, D]); a1v = region(14520, [D, H1, 2]); mk = region(14600, [D, H1, D])
        w_s1 = sb("w_s1", [D, 2 * H1]); w_m1 = sb("w_m1", [P, H1 // 2, D])
        w_2 = sb("w_2", [D, D + 2 * H2]); a2b = region(15120, [D, 2, D]); w_3 = sb("w_3", [D, D + 2])
        a3b = region(15260, [D, 2, D]); wtmp = region(15400, [D, 2, D])
        vec = sb("vec", [P, 8, D])
        w_sage = sb("w_sage", [P, 2, D])

        ps_t = ps("ps_t", [P, 2, 512])
        ps_x = ps("ps_x", [P, 2, 512])
        ps_a = ps("ps_a", [P, 2, 1024])

        loaded_w = sem("loaded_w"); loaded_x = sem("loaded_x"); loaded_rec = sem("loaded_rec")
        pool_consts = sem("pool_consts"); rec_half = sem("rec_half"); half_staged = sem("half_staged")
        consts_ready = sem("consts_ready")
        dve_chain = sem("dve_chain")
        loop_count = sem("loop_count"); loop_ind = sem("loop_ind"); loop_cum = sem("loop_cum")
        loop_pos = sem("loop_pos")
        counted = sem("counted"); totals = sem("totals"); sorted_ = sem("sorted")
        groups_ready = sem("groups_ready"); groups_stored = sem("groups_stored")
        starts_loaded = sem("starts_loaded"); dst_runs = sem("dst_runs")
        records_stored = sem("records_stored"); pad_ready = sem("pad_ready")
        pad_stored = sem("pad_stored")
        pos_staged = sem("pos_staged"); rec_staged = sem("rec_staged")
        scattered = [sem(f"scattered{i}") for i in range(2)]
        scatter_done = sem("scatter_done")
        weights_made = sem("weights_made"); weights_mm = sem("weights_mm")
        pool_steps = sem("pool_steps"); pe_steps = sem("pe_steps")
        score_max = sem("score_max"); score_all = sem("score_all")
        flag_ready = sem("flag_ready"); side_free = sem("side_free"); side_loaded = sem("side_loaded"); side_ready = sem("side_ready")
        table_made = sem("table_made"); table_written = sem("table_written")
        act_ask = sem("act_ask"); act_done = sem("act_done")
        final_made = sem("final_made"); out_written = sem("out_written")

        class Pass:
            pass

        landings = {by.name: [sem(f"landed_{by.name}{s}") for s in range(by.U)] for by in BY.values()}
        landed_before = {"dst": 0, "src": 0}
        passes = []
        for p in range(6):
            q = Pass()
            q.n, q.H, q.F, q.W, q.by = p, HEADS[p], ROW[p], OUTW[p], BY[SIDE[p]]
            q.banks = -(-q.W // 512)
            q.idx_staged = sem(f"p{p}_idx_staged")
            q.begun = sem(f"p{p}_begun")
            q.landed = landings[q.by.name]
            q.land0 = landed_before[q.by.name]
            landed_before[q.by.name] += 16 * q.by.G * (q.by.NG // q.by.U)
            q.attr_landed = [sem(f"p{p}_attr{s}") for s in range(q.by.U)] if p == 0 else None
            q.onehot_made = sem(f"p{p}_onehot_made")
            q.summed = sem(f"p{p}_summed")
            q.added = sem(f"p{p}_added")
            if q.H:
                q.transposed = sem(f"p{p}_transposed")
                q.copied = sem(f"p{p}_copied")
                q.expanded = sem(f"p{p}_expanded")
                q.scored = sem(f"p{p}_scored")
                q.maxed = sem(f"p{p}_maxed")
                q.clipped = sem(f"p{p}_clipped")
                q.weighed = sem(f"p{p}_weighed")
                q.rhs_made = sem(f"p{p}_rhs_made")
            if p in (0, 2, 3):
                q.m_idx = sem(f"p{p}_m_idx"); q.m_landed = sem(f"p{p}_m_landed")
                q.m_masked = sem(f"p{p}_m_masked"); q.m_transposed = sem(f"p{p}_m_transposed")
                q.m_chain = sem(f"p{p}_m_chain")
            if p == 0:
                q.rhs_half = sem(f"p{p}_rhs_half")
            passes.append(q)

        class Projection:
            pass

        def projection(chunks, dst, at, width):
            j = Projection()
            j.chunks, j.dst, j.at, j.N = chunks, dst, at, width
            j.before = numbered[0] * (NP // WB)
            numbered[0] += 1
            j.number = numbered[0]
            j.ready, j.staged, j.transposed, j.copied, j.multiplied, j.stored = proj_sems
            return j

        numbered = [0]
        proj_sems = [sem(f"proj_{n}") for n in ("ready", "staged", "transposed", "copied", "multiplied", "stored")]

        J = {
            "s0": projection([(D, w_attn[:, :])], tab, D, 2),
            "o0": projection([(D + DE, w_pa[:, :]), (D, w_a1[:, :])], pre, 0, D),
            "s1": projection([(D, w_s1[:, :])], tab, D, 2 * H1),
            "o1": projection([(P, w_m1[:, c, :]) for c in range(H1 // 2)], pre, 0, D),
            "s2": projection([(D, w_2[:, :])], tab, 0, D + 2 * H2),
            "s3": projection([(D, w_3[:, :])], tab, 0, D + 2),
            "o4": projection([(P, w_sage[:, 0, :])], pre, 0, D),
            "o5": projection([(P, w_sage[:, 1, :])], pre, 0, D),
        }
        ORDER = [("s0", 0, "o0"), ("s1", 1, "o1"), ("s2", 2, None), ("s3", 3, None),
                 (None, 4, "o4"), (None, 5, "o5")]

        block = ctx.enter_context(nc.Block())

        @block.sync
        def _(sp):
            sp.dma_start(flat_rec, a["rec"][0:E, :].rearrange("(p c) t -> p c t", p=SP_))\
              .then_inc(loaded_rec, 16)
            sp.wait_ge(consts_ready, 1)
            sp.dma_start(xcur[:, 0:FULL, :], a["x"][0:FULL * P, :].rearrange("(w p) f -> p w f", p=P))\
              .then_inc(loaded_x, 16)
            sp.dma_start(xcur[0:TAIL, FULL, :], a["x"][FULL * P:N, :]).then_inc(loaded_x, 16)
            loads = [
                (w_attn[:, :], a["attn_wT"]), (b_attn[:, :], a["attn_b"].partition_broadcast(P)),
                (w_proj[:, :], a["proj_w"]), (w_a1[:, :], a["apply_wT"][0:D, :]),
                (w_a2[:, :], a["apply_wT"][D:2 * D, :]), (b_apply[:, :], a["apply_b"].partition_broadcast(P)),
                (w1t[:, :, :], a["W_t"]), (a1v[:, :, :], a["a_t"]), (mk[:, :, :], a["merge_t"]),
                (w_2[:, 0:D], a["W1"]), (w_3[:, 0:D], a["W2"]),
                (a2b[:, 0, :], a["a1_src"].partition_broadcast(D)),
                (a2b[:, 1, :], a["a1_dst"].partition_broadcast(D)),
                (a3b[:, 0, :], a["a2_src"].partition_broadcast(D)),
                (a3b[:, 1, :], a["a2_dst"].partition_broadcast(D)),
                (w_sage[0:D, 0, :], a["Wl0T"]), (w_sage[D:P, 0, :], a["Wr0T"]),
                (w_sage[0:D, 1, :], a["Wl1T"]), (w_sage[D:P, 1, :], a["Wr1T"]),
            ] + [(vec[:, i, :], a[n].partition_broadcast(P)) for i, n in
                 enumerate(("b1", "ln1_g", "ln1_b", "b2", "ln2_g", "ln2_b", "bl0", "bl1"))]
            for dst, src in loads:
                sp.dma_start(dst, src).then_inc(loaded_w, 16)
            sp.wait_ge(pad_ready, 2)
            rec_flat = records["src"].rearrange("(p c) t -> p c t", p=P)
            per = BY["src"].T
            for c in range(0, per, 1024):
                n = min(1024, per - c)
                sp.dma_start(rec_flat[:, c:c + n, :], pad[:, 0:n, :]).then_inc(pad_stored, 16)
            by = BY["dst"]
            sp.wait_ge(groups_ready, 1)
            sp.dma_start(group_window["dst"].rearrange("(p c) -> p c", p=by.GP), gwis[0:by.GP, 0, 0:by.GC]).then_inc(groups_stored, 16)
            sp.dma_start(group_start.rearrange("(p c) -> p c", p=by.GP), gwis[0:by.GP, 1, 0:by.GC]).then_inc(groups_stored, 16)
            sp.wait_ge(groups_stored, 32)
            sp.dma_start(srow, group_start.rearrange("(a n) -> a n", a=1)).then_inc(starts_loaded, 16)
            sp.wait_ge(groups_ready, 2)
            sp.dma_start(group_window["src"].rearrange("(p c) -> p c", p=BY["src"].GP),
                         gwis[0:BY["src"].GP, 0, 0:BY["src"].GC]).then_inc(groups_stored, 16)
            sp.wait_ge(starts_loaded, 16)
            with sp.Fori(0, by.NG) as k:
                start = sp.value_load(srow[0:1, bass.ds(k, 1)], min_val=0, max_val=E)
                sp.dma_start(grec[:, bass.ds(k * by.G, by.G), :],
                             a["rec"][bass.ds(start, by.GE), :].rearrange("(p g) t -> p g t", p=P))\
                  .then_inc(dst_runs, 16)
            sp.wait_ge(dst_runs, 16 * by.NG)
            sp.dma_start(records["dst"].rearrange("(k p g) t -> p k g t", p=P, g=by.G),
                         grec[:, 0:by.T, :].rearrange("p (k g) t -> p k g t", g=by.G)).then_inc(records_stored, 16)

            def side(q, n):
                sp.wait_ge(side_free, n + 1)
                by = q.by
                if by.name == "src":
                    sp.wait_ge(scatter_done, 1)
                sp.wait_ge(records_stored, 16)
                sp.wait_ge(groups_stored, 48)
                sp.dma_start(grec[:, 0:by.T, :].rearrange("p (k g) t -> p k g t", g=by.G),
                             records[by.name].rearrange("(k p g) t -> p k g t", p=P, g=by.G)).then_inc(side_loaded, 16)
                sp.dma_start(wrow[:, 0:by.NG], group_window[by.name].rearrange("(a n) -> a n", a=1)).then_inc(side_loaded, 16)
                sp.dma_start(wbi[:, 0:by.NG], group_window[by.name].partition_broadcast(P)).then_inc(side_loaded, 16)

            for q in passes:
                sp.wait_ge(table_made, q.n + 1)
                sp.dma_start(tables[q.n].rearrange("(w p) f -> p w f", p=P), tab[:, :, 0:q.F])\
                  .then_inc(table_written, 16)
                if q.n in (0, 1, 2):
                    side(q, q.n)
                if q.n == 0:
                    def attr_load(k, s, turn):
                        start = sp.value_load(srow[0:1, bass.ds(k, 1)], min_val=0, max_val=E)
                        since(sp, q.rhs_made, k - by.U + 1)
                        sp.dma_start(attrs[:, s * by.G:(s + 1) * by.G, :],
                                     a["attr"][bass.ds(start, by.GE), :].rearrange("(p g) f -> p g f", p=P))\
                          .then_inc(q.attr_landed[s], 16)
                    pipelined(sp, by.NG, by.U, [(0, attr_load)])
            sp.wait_ge(final_made, 1)
            sp.dma_start(out[0:FULL * P, :].rearrange("(w p) f -> p w f", p=P), xcur[:, 0:FULL, :]).then_inc(out_written, 16)
            sp.dma_start(out[FULL * P:N, :], xcur[0:TAIL, FULL, :]).then_inc(out_written, 16)
            sp.wait_ge(out_written, 32)

        @block.gpsimd
        def _(pool):
            nc.gpsimd.memset(xcur[:, :, :], 0.0).then_inc(consts_ready, 1)
            nc.gpsimd.iota(pad[:, :, 0:1], pattern=[[0, 1024]], base=BIG_NODE, channel_multiplier=0).then_inc(pad_ready, 1)
            nc.gpsimd.iota(pad[:, :, 1:2], pattern=[[0, 1024]], base=0, channel_multiplier=0).then_inc(pad_ready, 1)
            nc.gpsimd.memset(ones[:, :], 1.0).then_inc(pool_consts, 1)
            nc.gpsimd.iota(iota_ni[:, :], pattern=[[1, P]], base=0, channel_multiplier=0).then_inc(pool_consts, 1)
            for by in BY.values():
                nc.gpsimd.iota(iota_gi[:, by.number, :], pattern=[[1, GCMAX]], base=0, channel_multiplier=by.GC)\
                    .then_inc(pool_consts, 1)
            pool.wait_ge(pool_consts, 4)
            nc.gpsimd.affine_select(out=ident[:, :], in_=ones[:, :], pattern=[[-1, P]], compare_op=ALU.is_equal,
                                    fill=0.0, base=0, channel_multiplier=1).then_inc(pool_consts, 1)
            nc.gpsimd.affine_select(out=below[:, :], in_=ones[:, :], pattern=[[1, P]], compare_op=ALU.is_gt,
                                    fill=0.0, base=0, channel_multiplier=-1).then_inc(pool_consts, 1)

            def scatter(k, s, turn):
                pool.wait_ge(pad_stored, 16 * -(-BY["src"].T // 1024))
                since(pool, rec_staged, k + 1)
                since(pool, pos_staged, k + 1)
                pool.sem_inc(pool_steps, 1)
                for c in range(SU):
                    pool.indirect_dma_start(records["src"], bass.IndirectOffsetOnAxis(ap=pos_slot[:, s, c:c + 1], axis=0),
                                            rec_slot[:, s, c, :], None).then_inc(scattered[s], 16)
            pipelined(pool, SC // SU, 2, [(0, scatter)])
            for s in range(2):
                pool.wait_ge(scattered[s], 16 * SC // 2)
            pool.sem_inc(scatter_done, 1)

            asks = 0
            for q in passes:
                NG, G, U = q.by.NG, q.by.G, q.by.U
                if q.n in (0, 2, 3):
                    asks += 1
                    pool.wait_ge(score_max, asks)
                    nc.gpsimd.partition_all_reduce(gm[:, 1, 0:2 * q.H], gm[:, 0, 0:2 * q.H], P, RMAX).then_inc(score_all, 1)
                    pool.wait_ge(flag_ready, asks)
                    pool.wait_ge(table_written, 16 * (q.n + 1))
                    wide = pool.value_load(flagi[0:1, 0:1], min_val=0, max_val=1)
                    with pool.If(wide > 0):
                        with pool.Fori(0, NG) as k:
                            pool.wait_ge(q.m_idx, k + 1)
                            pool.sem_inc(pool_steps, 1)
                            for g in range(G):
                                pool.indirect_dma_start(rows[:, g * q.F:(g + 1) * q.F], None, tables[q.n],
                                                        bass.IndirectOffsetOnAxis(ap=idx_slot[:, g:g + 1], axis=0))\
                                    .then_inc(q.m_landed, 16)
                    pool.sem_inc(pool_steps, 1)

                def gather(k, s, turn, q=q, G=G, U=U):
                    pool.wait_ge(table_written, 16 * (q.n + 1))
                    since(pool, q.idx_staged, k + 1)
                    if q.H:
                        since(pool, q.rhs_made, k - U + 1)
                    else:
                        since(pool, q.summed, k - U + 1)
                    pool.sem_inc(pool_steps, 1)
                    for t in range(s * G, (s + 1) * G):
                        pool.indirect_dma_start(rows[:, t * q.F:(t + 1) * q.F], None, tables[q.n],
                                                bass.IndirectOffsetOnAxis(ap=idx_slot[:, t:t + 1], axis=0))\
                            .then_inc(q.landed[s], 16)
                pipelined(pool, NG, U, [(0, gather)])

        @block.scalar
        def _(act):
            def stage_pos(k, s, turn):
                act.wait_ge(sorted_, 1)
                since(act, scattered[s], 16 * SU * turn)
                nc.scalar.copy(pos_slot[:, s, :], posi[:, bass.ds(k * SU, SU)]).then_inc(pos_staged, 1)
            pipelined(act, SC // SU, 2, [(0, stage_pos)])

            def project(j):
                act.wait_ge(j.ready, j.number)

                def evacuate(b, s, turn):
                    since(act, j.transposed, b + 1, j.before)
                    since(act, j.multiplied, b - 1, j.before)
                    same = all(K == P for K, _ in j.chunks)
                    parts = [(0, P, len(j.chunks))] if same else [(c, K, 1) for c, (K, _) in enumerate(j.chunks)]
                    for n, (c, K, m) in enumerate(parts):
                        ins = nc.scalar.copy(node_t[0:K, s, c * WB * P:(c + m) * WB * P],
                                             ps_a[0:K, s, c * WB * P:(c + m) * WB * P])
                    ins.then_inc(j.copied, 1)
                pipelined(act, NP // WB, 2, [(1, evacuate)])

            def edges(q):
                NG, G, U = q.by.NG, q.by.G, q.by.U

                def stage_idx(k, s, turn):
                    act.wait_ge(q.begun, 1)
                    since(act, q.landed[s], 16 * G * turn, q.land0)
                    nc.scalar.copy(idx_slot[:, s * G:(s + 1) * G], idx[:, bass.ds(k * G, G)]).then_inc(q.idx_staged, 1)

                def copy_onehot(k, s, turn):
                    since(act, q.transposed, k + 1)
                    since(act, q.expanded, k - 1)
                    half = slice(s % 2 * G, (s % 2 + 1) * G)
                    nc.scalar.copy(onehot_ts[:, half, :].rearrange("p g n -> p (g n)"), ps_t[:, s % 2, 0:G * P])\
                        .then_inc(q.copied, 1)

                def weigh(k, s, turn):
                    since(act, q.clipped, k + 1)
                    since(act, q.summed, k - 1)
                    w = rhs[:, s % 2, 0:G * q.W].rearrange("p (g f) -> p g f", g=G)
                    nc.scalar.activation(w[:, :, q.W - q.H:q.W],
                                         zmax[:, s % 2, 0:G * q.H].rearrange("p (g h) -> p g h", g=G), ACT.Exp)\
                        .then_inc(q.weighed, 1)
                if q.H:
                    pipelined(act, NG, U, [(1, weigh), (3, copy_onehot), (U - 1 if U > 4 else U, stage_idx)])
                else:
                    pipelined(act, NG, U, [(U, stage_idx)])

            asked = [0]

            def serve(func, out_, in_):
                asked[0] += 1
                act.wait_ge(act_ask, asked[0])
                nc.scalar.activation(out_, in_, func).then_inc(act_done, 1)

            for s_name, p, o_name in ORDER:
                q = passes[p]
                if s_name:
                    project(J[s_name])
                edges(q)
                if p in (2, 3):
                    serve(ACT.Exp, mtmp[:, :, 0:q.H], mtmp[:, :, 0:q.H])
                    serve(ACT.Sqrt, stat[:, :], stat[:, :])
                    serve(ACT.Exp, tmp, tmp)
                if o_name:
                    project(J[o_name])
                if p in (4, 5):
                    serve(ACT.Sqrt, stat[:, :], stat[:, :])
                if p != 2 and p != 4:
                    serve(ACT.Sqrt, stat[:, :], stat[:, :])

        @block.tensor
        def _(pe):
            for n in range(2):
                pe.wait_ge(pool_consts, 6)
                pe.wait_ge(counted, n + 1)
                nc.tensor.matmul(ps_x[:, n, 0:NB], ones[0:SP_, :], cnt[0:SP_, n, :], start=True, stop=True).then_inc(totals, 1)
                if n == 1:
                    nc.tensor.matmul(ps_t[0:SP_, 0, 0:NB], below[0:SP_, 0:SP_], cnt[0:SP_, 1, :],
                                     start=True, stop=True).then_inc(totals, 1)
            pe.wait_ge(loaded_w, 16 * 27)
            nc.tensor.matmul(ps_a[0:D + DE, 0, 0:D], w_proj[:, :], w_a2[:, :], start=True, stop=True)
            for h in range(H1):
                nc.tensor.matmul(ps_a[0:D, 0, 64 + 2 * h:66 + 2 * h], w1t[:, h, :], a1v[:, h, :], start=True, stop=True)
            for h in range(H1):
                c = h // 2
                ins = nc.tensor.matmul(ps_a[:, 1, h * D:(h + 1) * D], w1t[:, 2 * c:2 * c + 2, :].rearrange("u a f -> u (a f)"),
                                       mk[:, h, :], start=True, stop=True)
            ins.then_inc(weights_mm, 1)

            def project(j):
                pe.wait_ge(j.ready, j.number)

                def transpose(b, s, turn):
                    since(pe, j.staged, b + 1, j.before)
                    since(pe, j.copied, b - 1, j.before)
                    pe.sem_inc(pe_steps, 1)
                    for c, (K, _) in enumerate(j.chunks):
                        for w in range(WB):
                            at = (w * len(j.chunks) + c) * P
                            o = (c * WB + w) * P
                            ins = nc.tensor.transpose(ps_a[0:K, s, o:o + P], staged[:, s, at:at + K], ident[:, :])
                    ins.then_inc(j.transposed, 1)

                def multiply(b, s, turn):
                    since(pe, j.copied, b + 1, j.before)
                    since(pe, j.stored, b - 1, j.before)
                    for w in range(WB):
                        for c, (K, weight) in enumerate(j.chunks):
                            o = (c * WB + w) * P
                            ins = nc.tensor.matmul(ps_x[:, s, w * j.N:(w + 1) * j.N], node_t[0:K, s, o:o + P], weight,
                                                   start=(c == 0), stop=(c == len(j.chunks) - 1))
                    ins.then_inc(j.multiplied, 1)
                pipelined(pe, NP // WB, 2, [(1, transpose), (0, multiply)])

            def edges(q):
                NG, G, U = q.by.NG, q.by.G, q.by.U

                def transpose(k, s, turn):
                    since(pe, q.onehot_made, k + 1)
                    since(pe, q.copied, k - 1)
                    for g in range(G):
                        ins = nc.tensor.transpose(ps_t[:, s % 2, g * P:(g + 1) * P], onehots[:, s * G + g, :], ident[:, :])
                    ins.then_inc(q.transposed, 1)

                def expand(k, s, turn):
                    w = pe.value_load(wrow[0:1, bass.ds(k, 1)], min_val=0, max_val=NW)
                    since(pe, q.copied, k + 1)
                    since(pe, q.scored, 2 * (k - 1))
                    for g in range(G):
                        for part in range(3):
                            ins = nc.tensor.matmul(ps_x[:, s % 2, g * 2 * q.H:(g + 1) * 2 * q.H], onehot_ts[:, s % 2 * G + g, :],
                                                   ntab3[:, part, bass.ds(w, 1), 0:2 * q.H].rearrange("p a h -> p (a h)"),
                                                   start=(part == 0), stop=(part == 2))
                    ins.then_inc(q.expanded, 1)

                def total(k, s, turn):
                    if q.H:
                        since(pe, q.rhs_made, k + 1)
                        r = rhs[:, s % 2, 0:G * q.W].rearrange("p (g f) -> p g f", g=G)
                    else:
                        since(pe, q.landed[s], 16 * G * (turn + 1), q.land0)
                        since(pe, q.onehot_made, k + 1)
                        r = rows[:, s * G * q.F:(s + 1) * G * q.F].rearrange("p (g f) -> p g f", g=G)
                    since(pe, q.added, k - 1)
                    for b in range(q.banks):
                        n = q.W // q.banks
                        for g in range(G):
                            ins = nc.tensor.matmul(ps_a[:, s % 2, b * 512:b * 512 + n], onehots[:, s * G + g, :],
                                                   r[:, g, b * n:(b + 1) * n], start=(g == 0), stop=(g == G - 1))
                    ins.then_inc(q.summed, 1)
                pe.wait_ge(q.begun, 1)
                if q.H:
                    pipelined(pe, NG, U, [(0, total), (2, expand), (3, transpose)])
                else:
                    pipelined(pe, NG, U, [(0, total)])

            def segment_maxima(q):
                pe.wait_ge(flag_ready, (0, 2, 3).index(q.n) + 1)
                wide = pe.value_load(flagi[0:1, 0:1], min_val=0, max_val=1)
                with pe.If(wide > 0):
                    with pe.Fori(0, q.by.T * q.H) as t:
                        pe.wait_ge(q.m_masked, t + 1)
                        nc.tensor.transpose(ps_t[:, 0, 0:P], onehots[:, 0, :], ident[:, :]).then_inc(q.m_transposed, 1)
                pe.sem_inc(pe_steps, 1)

            for s_name, p, o_name in ORDER:
                if s_name:
                    project(J[s_name])
                if p in (0, 2, 3):
                    segment_maxima(passes[p])
                edges(passes[p])
                if o_name:
                    project(J[o_name])

        @block.vector
        def _(dve):
            V = nc.vector
            link = Chain(dve, dve_chain)
            dve.wait_ge(pool_consts, 6)
            link(V.tensor_copy(iota_n[:, :], iota_ni[:, :]))
            link(V.tensor_copy(iota_g[:, :, :], iota_gi[:, :, :]))
            link(V.memset(cnt[:, :, :], 0.0))

            dve.wait_ge(loaded_rec, 16)
            for n, col in ((0, 1), (1, 0)):
                link(V.tensor_scalar(keyi, flat_rec[:, :, col], 7, None, ALU.logical_shift_right))
                link(V.tensor_copy(keyw, keyi))
                with dve.Fori(0, NW) as w:
                    V.tensor_scalar(ind, keyw, iota_n[0:SP_, bass.ds(w, 1)], None, ALU.is_equal, ALU.add,
                                    accum_out=cnt[0:SP_, n, bass.ds(w, 1)]).then_inc(loop_count, 1)
                    dve.wait_ge(loop_count, w + 1 + n * NW)
                dve.sem_inc(counted, 1)

            def group_tables(by):
                n, GE, GP, GC = by.number, by.GE, by.GP, by.GC
                gcmp, gw, gwi = gcmps[0:GP, 0:GC, :], gws[:, :, 0:GC], gwis[:, :, 0:GC]
                dve.wait_ge(totals, 1 if n == 0 else 3)
                tot, ng, gend, gstart, off, delta, dd, ong = (gsm[:, i, :] for i in range(8))
                link(V.memset(ong, 1.0))
                link(V.tensor_copy(tot, ps_x[:, n, 0:NB]))
                link(V.tensor_scalar(ng, tot, float(GE - 1), None, ALU.add))
                link(V.tensor_copy(gsi[:, 0, :], ng))
                link(V.tensor_scalar(gsi[:, 1, :], gsi[:, 0, :], GE.bit_length() - 1, None, ALU.logical_shift_right))
                link(V.tensor_copy(ng, gsi[:, 1, :]))
                link(V.tensor_tensor_scan(gend, ong, ng, 0.0, ALU.mult, ALU.add))
                link(V.tensor_tensor(gstart, gend, ng, ALU.subtract))
                en = gend[0:GP, 0:NW].unsqueeze(1).to_broadcast([GP, GC, NW])
                ig = iota_g[0:GP, n, 0:GC].unsqueeze(2).to_broadcast([GP, GC, NW])
                link(V.tensor_tensor(gcmp, en, ig, ALU.is_le))
                link(V.tensor_reduce(gw[0:GP, 0, :], gcmp, AX, ALU.add))
                if n == 0:
                    link(V.tensor_tensor_scan(off, ong, tot, 0.0, ALU.mult, ALU.add))
                    link(V.tensor_tensor(off, off, tot, ALU.subtract))
                    link(V.scalar_tensor_tensor(delta, gstart, -float(GE), off, ALU.mult, ALU.add))
                    link(V.tensor_tensor(dd[:, 0:NW], delta[:, 1:NB], delta[:, 0:NW], ALU.subtract))
                    link(V.tensor_tensor(gcmp, gcmp, dd[0:GP, 0:NW].unsqueeze(1).to_broadcast([GP, GC, NW]), ALU.mult))
                    link(V.tensor_reduce(gw[0:GP, 1, :], gcmp, AX, ALU.add))
                    link(V.scalar_tensor_tensor(gw[0:GP, 1, :], iota_g[0:GP, n, 0:GC], float(GE), gw[0:GP, 1, :], ALU.mult, ALU.add))
                    link(V.tensor_scalar(gw[0:GP, 1, :], gw[0:GP, 1, :], float(E), None, ALU.min))
                else:
                    dve.wait_ge(groups_stored, 32)
                for i in range(2 - n):
                    link(V.tensor_copy(gwi[0:GP, i, :], gw[0:GP, i, :]))
                dve.sem_inc(groups_ready, 1)
                return gstart

            group_tables(BY["dst"])
            gstart = group_tables(BY["src"])
            link(V.scalar_tensor_tensor(base[0:SP_, :], gstart[0:SP_, :], float(BY["src"].GE), ps_t[0:SP_, 0, 0:NB],
                                        ALU.mult, ALU.add))
            link(V.memset(pos, 0.0))
            with dve.Fori(0, NW) as w:
                V.tensor_scalar(ind, keyw, iota_n[0:SP_, bass.ds(w, 1)], None, ALU.is_equal).then_inc(loop_ind, 1)
                dve.wait_ge(loop_ind, w + 1)
                V.tensor_tensor_scan(cum, ind, ind, base[0:SP_, bass.ds(w, 1)], ALU.add, ALU.max).then_inc(loop_cum, 1)
                dve.wait_ge(totals, 3)
                dve.wait_ge(loop_cum, w + 1)
                V.copy_predicated(pos, ind.bitcast(i32), cum).then_inc(loop_pos, 1)
                dve.wait_ge(loop_pos, w + 1)
            link(V.tensor_scalar(posi, pos, -1.0, None, ALU.add))
            dve.sem_inc(sorted_, 1)

            dve.wait_ge(loaded_w, 16 * 27)
            dve.wait_ge(weights_mm, 1)
            link(V.tensor_copy(w_pa[:, :], ps_a[0:D + DE, 0, 0:D]))
            sv = ps_a[0:D, 0, 64:64 + 2 * H1].rearrange("p (h t) -> p t h", t=2)
            link(V.tensor_copy(w_s1[:, 0:H1], sv[:, 1, :]))
            link(V.tensor_copy(w_s1[:, H1:2 * H1], sv[:, 0, :]))
            pm = ps_a[:, 1, 0:512].rearrange("p (c a f) -> p c a f", c=H1 // 2, a=2)
            link(V.tensor_copy(w_m1[0:D, :, :], pm[0:D, :, 0, :]))
            link(V.tensor_copy(w_m1[D:P, :, :], pm[D:P, :, 1, :]))
            for t in range(2):
                link(V.tensor_tensor(wtmp[:, t, :], w_2[:, 0:D], a2b[:, t, :], ALU.mult))
                link(V.tensor_reduce(w_2[:, D + t * H2:D + (t + 1) * H2],
                                     wtmp[:, t, :].rearrange("p (h c) -> p h c", h=H2), AX, ALU.add))
                link(V.tensor_tensor(wtmp[:, t, :], w_3[:, 0:D], a3b[:, t, :], ALU.mult))
                link(V.tensor_reduce(w_3[:, D + t:D + t + 1], wtmp[:, t, :], AX, ALU.add))
            dve.wait_ge(loaded_x, 32)

            def stage_rec(k, s, turn):
                dve.wait_ge(loaded_rec, 16)
                since(dve, scattered[s], 16 * SU * turn)
                V.tensor_copy(rec_slot[:, s, :, 0:1], flat_rec[:, bass.ds(k * SU, SU), 0:1]).then_inc(rec_half, 1)
                V.tensor_copy(rec_slot[:, s, :, 1:2], flat_rec[:, bass.ds(k * SU, SU), 1:2]).then_inc(rec_staged, 1)
            pipelined(dve, SC // SU, 2, [(0, stage_rec)])

            def project(j, stage_ops):
                dve.sem_inc(j.ready, 1)

                def stage(b, s, turn):
                    since(dve, j.transposed, b - 1, j.before)
                    o = staged[:, s, 0:WB * len(j.chunks) * P].rearrange("p (w c) -> p w c", w=WB)
                    stage_ops(b, o, j.staged)

                def store(b, s, turn):
                    dve.wait_ge(j.ready, j.number)
                    since(dve, j.multiplied, b + 1, j.before)
                    V.tensor_copy(j.dst[:, bass.ds(b * WB, WB), j.at:j.at + j.N],
                                  ps_x[:, s, 0:WB * j.N].rearrange("p (w n) -> p w n", w=WB)).then_inc(j.stored, 1)
                pipelined(dve, NP // WB, 2, [(2, stage), (0, store)])
                dve.wait_ge(j.stored, NP // WB + j.before)

            def stage_copy(src, width):
                def ops(b, o, done):
                    dve.wait_ge(loaded_x, 32)
                    V.tensor_copy(o[:, :, 0:width], src[:, bass.ds(b * WB, WB), 0:width]).then_inc(done, 1)
                return ops

            def per(v, n, shape):
                return v.unsqueeze(n).to_broadcast(shape)

            def bc(v):
                return v.unsqueeze(1).to_broadcast([P, NP, D])

            full = [P, NP, D]
            asked = [0]

            def ask():
                asked[0] += 1
                dve.sem_inc(act_ask, 1)
                dve.wait_ge(act_done, asked[0])

            def normalise(v):
                link(V.tensor_reduce(stat[:, :], v, AX, ALU.add))
                link(V.tensor_scalar(stat[:, :], stat[:, :], 1.0 / D, None, ALU.mult))
                link(V.tensor_tensor(v, v, per(stat[:, :], 2, full), ALU.subtract))
                link(V.tensor_tensor(tmp, v, v, ALU.mult))
                link(V.tensor_reduce(stat[:, :], tmp, AX, ALU.add))
                link(V.tensor_scalar(stat[:, :], stat[:, :], 1.0 / D, 1e-5, ALU.mult, ALU.add))
                ask()
                link(V.reciprocal(stat[:, :], stat[:, :]))
                link(V.tensor_tensor(v, v, per(stat[:, :], 2, full), ALU.mult))

            def load_side(n):
                dve.sem_inc(side_free, 1)
                dve.wait_ge(side_loaded, 48 * (n + 1))
                NG, G, T = passes[n].by.NG, passes[n].by.G, passes[n].by.T
                key, other = (1, 0) if n != 1 else (0, 1)
                link(V.tensor_copy(idx[:, 0:T], grec[:, 0:T, other]))
                link(V.tensor_scalar(wbi[:, 0:NG], wbi[:, 0:NG], 7, None, ALU.logical_shift_left))
                link(V.tensor_copy(wb[:, 0:NG], wbi[:, 0:NG]))
                link(V.tensor_tensor(local[:, 0:T].rearrange("p (k g) -> p k g", g=G),
                                     grec[:, 0:T, key].rearrange("p (k g) -> p k g", g=G),
                                     wb[:, 0:NG].unsqueeze(2).to_broadcast([P, NG, G]), ALU.subtract))

            maxes = [0]

            def segment_maxima(q):
                H, NG, G = q.H, q.by.NG, q.by.G
                with dve.Fori(0, NG) as k:
                    w = dve.value_load(wrow[0:1, bass.ds(k, 1)], min_val=0, max_val=NW)
                    V.tensor_copy(idx_slot[:, 0:G], idx[:, bass.ds(k * G, G)]).then_inc(q.m_idx, 1)
                    dve.wait_ge(q.m_landed, k * (16 * G) + 16 * G)
                    links = 3 * G * H
                    n = 0
                    for g in range(G):
                        for h in range(H):
                            V.tensor_scalar(onehots[:, 1, :], iota_n[:, :], local[:, bass.ds(k * G + g, 1)], -3e38,
                                            ALU.not_equal, ALU.mult).then_inc(q.m_chain, 1)
                            n += 1
                            dve.wait_ge(q.m_chain, k * links + n)
                            V.tensor_scalar(onehots[:, 0, :], onehots[:, 1, :],
                                            rows[:, g * q.F + D + h:g * q.F + D + h + 1], None, ALU.add)\
                                .then_inc(q.m_masked, 1)
                            dve.wait_ge(q.m_transposed, k * (G * H) + g * H + h + 1)
                            V.tensor_reduce(stat[:, 0:1], ps_t[:, 0, 0:P], AX, ALU.max).then_inc(q.m_chain, 1)
                            n += 1
                            dve.wait_ge(q.m_chain, k * links + n)
                            m = mtmp[:, bass.ds(w, 1), h:h + 1].rearrange("p a h -> p (a h)")
                            V.tensor_tensor(m, m, stat[:, 0:1], ALU.max).then_inc(q.m_chain, 1)
                            n += 1
                            dve.wait_ge(q.m_chain, k * links + n)
                if q.n != 0:
                    link(V.tensor_tensor(mtmp[:, :, 0:H], mtmp[:, :, 0:H], tab[:, :, D:D + H], ALU.max))

            def key_table(q, src, key):
                H = q.H
                a_s, b_k = tab[:, :, src:src + H], tab[:, :, key:key + H]
                link(V.tensor_reduce(gm[:, 0, 0:H], a_s.rearrange("p w h -> p h w"), AX, ALU.max))
                link(V.tensor_reduce(gm[:, 0, H:2 * H], a_s.rearrange("p w h -> p h w"), AX, ALU.min, negate=True))
                dve.sem_inc(score_max, 1)
                maxes[0] += 1
                dve.wait_ge(score_all, maxes[0])
                m = mtmp[:, :, 0:H]
                link(V.tensor_copy(m, gm[:, 1, 0:H].unsqueeze(1).to_broadcast([P, NP, H])))
                link(V.tensor_tensor(gm[:, 0, 0:H], gm[:, 1, 0:H], gm[:, 1, H:2 * H], ALU.add))
                link(V.tensor_reduce(flag[:, 0:1], gm[:, 0, 0:H], AX, ALU.max))
                link(V.tensor_scalar(flag[:, 1:2], flag[:, 0:1], SPAN, None, ALU.is_gt))
                link(V.tensor_copy(flagi[:, :], flag[:, 1:2]))
                dve.sem_inc(flag_ready, 1)
                wide = dve.value_load(flagi[0:1, 0:1], min_val=0, max_val=1)
                before = link.n
                with dve.If(wide > 0):
                    link(V.tensor_scalar(m, gm[:, 1, H:2 * H].unsqueeze(1).to_broadcast([P, NP, H]), -1.0, None, ALU.mult))
                    segment_maxima(q)
                with dve.Else():
                    dve.sem_inc(dve_chain, link.n - before)
                link(V.tensor_tensor(m, b_k, m, ALU.add))
                link(V.scalar_tensor_tensor(m, m, SLOPE, m, ALU.mult, ALU.max))
                link(V.tensor_tensor(ntab[:, :, 0:H], b_k, m, ALU.subtract))
                link(V.scalar_tensor_tensor(ntab[:, :, H:2 * H], b_k, SLOPE, m, ALU.mult, ALU.subtract))

            def split_key_table(n):
                rest = ntab[:, :, 0:n]
                for part in range(3):
                    link(V.tensor_copy(ntab3[:, part, :, 0:n], rest))
                    if part < 2:
                        link(V.tensor_tensor(tmp[:, :, 0:n], rest, ntab3[:, part, :, 0:n], ALU.subtract))
                        rest = tmp[:, :, 0:n]

            def edges(q):
                NG, G, U = q.by.NG, q.by.G, q.by.U
                if q.H:
                    split_key_table(2 * q.H)
                acc = acc_all[:, 0:NP * q.W].rearrange("p (w f) -> p w f", w=NP)
                link(V.memset(acc_all[:, 0:NP * q.W], 0.0))
                dve.sem_inc(q.begun, 1)
                def make_onehot(k, s, turn):
                    since(dve, q.summed, k - U + 1)
                    V.tensor_tensor(onehots[:, s * G:(s + 1) * G, :], iota_n[:, :].unsqueeze(1).to_broadcast([P, G, P]),
                                    local[:, bass.ds(k * G, G)].unsqueeze(2).to_broadcast([P, G, P]), ALU.is_equal)\
                        .then_inc(q.onehot_made, 1)

                r = lambda s: rows[:, s * G * q.F:(s + 1) * G * q.F].rearrange("p (g f) -> p g f", g=G)
                o = lambda s: rhs[:, s % 2, 0:G * q.W].rearrange("p (g f) -> p g f", g=G)

                def score(k, s, turn):
                    H = q.H
                    since(dve, q.landed[s], 16 * G * (turn + 1), q.land0)
                    since(dve, q.expanded, k + 1)
                    since(dve, q.maxed, k - 1)
                    share = ps_x[:, s % 2, 0:G * 2 * H].rearrange("p (g h) -> p g h", g=G)
                    t = t12[:, s % 2, 0:G, :]
                    V.tensor_tensor(t[:, :, 0:H], share[:, :, 0:H], r(s)[:, :, D:D + H], ALU.add).then_inc(q.scored, 1)
                    V.scalar_tensor_tensor(t[:, :, H:2 * H], r(s)[:, :, D:D + H], SLOPE, share[:, :, H:2 * H],
                                           ALU.mult, ALU.add).then_inc(q.scored, 1)

                def larger(k, s, turn):
                    H = q.H
                    since(dve, q.scored, 2 * (k + 1))
                    since(dve, q.weighed, k - 1)
                    t = t12[:, s % 2, 0:G, :]
                    V.tensor_tensor(zmax[:, s % 2, 0:G * H].rearrange("p (g h) -> p g h", g=G),
                                    t[:, :, 0:H], t[:, :, H:2 * H], ALU.max).then_inc(q.maxed, 1)

                def clip(k, s, turn):
                    since(dve, q.maxed, k + 1)
                    z = zmax[:, s % 2, 0:G * q.H]
                    if q.n == 1:
                        V.tensor_scalar(z, z, 2.0, -2.0, ALU.min, ALU.max).then_inc(q.clipped, 1)
                    else:
                        V.tensor_scalar(z, z, 0.0, None, ALU.min).then_inc(q.clipped, 1)

                def weight_rows(k, s, turn):
                    since(dve, q.weighed, k + 1)
                    x, w = r(s), o(s)
                    e = w[:, :, q.W - q.H:q.W]
                    if q.n == 0:
                        since(dve, q.attr_landed[s], 16 * (turn + 1))
                        V.tensor_tensor(w[:, :, 0:D], x[:, :, 0:D], e.to_broadcast([P, G, D]), ALU.mult).then_inc(q.rhs_half, 1)
                        V.tensor_tensor(w[:, :, D:D + DE], attrs[:, s * G:(s + 1) * G, :], e.to_broadcast([P, G, DE]), ALU.mult)\
                            .then_inc(q.rhs_made, 1)
                    elif q.n == 1:
                        V.tensor_tensor(w[:, :, 0:H1 * D].rearrange("p g (h f) -> p g h f", h=H1),
                                        x[:, :, 0:D].unsqueeze(2).to_broadcast([P, G, H1, D]),
                                        e.unsqueeze(3).to_broadcast([P, G, H1, D]), ALU.mult).then_inc(q.rhs_made, 1)
                    else:
                        V.tensor_tensor(w[:, :, 0:D].rearrange("p g (h f) -> p g h f", h=q.H),
                                        x[:, :, 0:D].rearrange("p g (h f) -> p g h f", h=q.H),
                                        e.unsqueeze(3).to_broadcast([P, G, q.H, D // q.H]), ALU.mult).then_inc(q.rhs_made, 1)

                def add(k, s, turn):
                    w = dve.value_load(wrow[0:1, bass.ds(k, 1)], min_val=0, max_val=NW)
                    since(dve, q.added, k)
                    since(dve, q.summed, k + 1)
                    t = acc[:, bass.ds(w, 1), :].rearrange("p a (b f) -> p (a b) f", b=q.banks)
                    sums = ps_a[:, s % 2, :].rearrange("p (b f) -> p b f", f=512)[:, 0:q.banks, 0:q.W // q.banks]
                    V.tensor_tensor(t, sums, t, ALU.add).then_inc(q.added, 1)

                if q.H:
                    stages = [(0, weight_rows), (-2, add), (1, score), (3, make_onehot), (1, larger), (1, clip)] \
                        if q.n == 1 else \
                        [(0, score), (3, make_onehot), (0, larger), (0, clip), (-2, add), (0, weight_rows)]
                else:
                    stages = [(-2, add), (3, make_onehot)]
                pipelined(dve, NG, U, stages)
                dve.wait_ge(q.added, NG)
                return acc

            def reciprocals(den, H, eps):
                d = rden[:, :, 0:H]
                if eps:
                    link(V.tensor_scalar(d, den, eps, None, ALU.add))
                else:
                    link(V.tensor_scalar(d, den, 0.0, None, ALU.is_equal))
                    link(V.tensor_tensor(d, d, den, ALU.add))
                link(V.reciprocal(d, d))

            project(J["s0"], stage_copy(xcur, D))
            link(V.tensor_scalar(tab[:, :, D + 1:D + 2], tab[:, :, D + 1:D + 2], b_attn[:, 0:1], None, ALU.add))
            link(V.tensor_copy(tab[:, :, 0:D], xcur[:, :, :]))
            dve.sem_inc(table_made, 1)
            dve.wait_ge(records_stored, 16)
            for s in range(2):
                dve.wait_ge(scattered[s], 16 * SC // 2)
            load_side(0)
            key_table(passes[0], D, D + 1)
            acc = edges(passes[0])
            reciprocals(acc[:, :, D + DE:D + DE + 1], 1, 0)

            def stage0(b, o, done):
                w = bass.ds(b * WB, WB)
                V.tensor_tensor(o[:, :, 0:D + DE], acc0[:, w, 0:D + DE], rden[:, w, 0:1].to_broadcast([P, WB, D + DE]),
                                ALU.mult).then_inc(half_staged, 1)
                V.tensor_copy(o[:, :, P:P + D], xcur[:, w, :]).then_inc(done, 1)
            acc0 = acc
            project(J["o0"], stage0)
            link(V.tensor_tensor(pre[:, :, :], pre[:, :, :], bc(b_apply[:, :]), ALU.add))
            link(V.scalar_tensor_tensor(xcur[:, :, :], pre[:, :, :], 0.0, xcur[:, :, :], ALU.max, ALU.add))
            normalise(xcur[:, :, :])

            project(J["s1"], stage_copy(xcur, D))
            link(V.tensor_copy(tab[:, :, 0:D], xcur[:, :, :]))
            dve.sem_inc(table_made, 1)
            link(V.tensor_copy(ntab[:, :, 0:H1], tab[:, :, D + H1:D + 2 * H1]))
            link(V.tensor_scalar(ntab[:, :, H1:2 * H1], tab[:, :, D + H1:D + 2 * H1], SLOPE, None, ALU.mult))
            load_side(1)
            acc1 = edges(passes[1])
            reciprocals(acc1[:, :, H1 * D:H1 * D + H1], H1, 0)

            def stage1(b, o, done):
                for w in range(WB):
                    ins = V.tensor_tensor(o[:, w, :].rearrange("p (h f) -> p h f", h=H1),
                                          acc1[:, bass.ds(b * WB + w, 1), 0:H1 * D].rearrange("p a (h f) -> p (a h) f", h=H1),
                                          rden[:, bass.ds(b * WB + w, 1), :].rearrange("p a h -> p (a h)").unsqueeze(2)
                                          .to_broadcast([P, H1, D]), ALU.mult)
                    ins.then_inc(half_staged if w == 0 else done, 1)
            project(J["o1"], stage1)
            link(V.scalar_tensor_tensor(pre[:, :, :], pre[:, :, :], SLOPE, pre[:, :, :], ALU.mult, ALU.max))
            link(V.tensor_tensor(xcur[:, :, :], xcur[:, :, :], pre[:, :, :], ALU.add))
            normalise(xcur[:, :, :])

            for p, j, src in ((2, "s2", xcur), (3, "s3", pre)):
                q, H = passes[p], HEADS[p]
                v0 = 0 if p == 2 else 3
                project(J[j], stage_copy(src, D))
                dve.sem_inc(table_made, 1)
                if p == 2:
                    load_side(2)
                key_table(q, D, D + H)
                acc = edges(q)
                s_, m = mtmp[:, :, 0:H], rden[:, :, 0:H]
                link(V.tensor_tensor(s_, tab[:, :, D:D + H], ntab[:, :, 0:H], ALU.add))
                link(V.scalar_tensor_tensor(m, tab[:, :, D:D + H], SLOPE, ntab[:, :, H:2 * H], ALU.mult, ALU.add))
                link(V.tensor_tensor(s_, s_, m, ALU.max))
                ask()
                for h in range(H):
                    c = slice(h * (D // H), (h + 1) * (D // H))
                    link(V.tensor_tensor(tmp[:, :, c], tab[:, :, c], mtmp[:, :, h:h + 1].to_broadcast([P, NP, D // H]), ALU.mult))
                link(V.tensor_tensor(pre[:, :, :], acc[:, :, 0:D], tmp, ALU.add))
                link(V.tensor_tensor(s_, s_, acc[:, :, D:D + H], ALU.add))
                reciprocals(s_, H, 1e-16)
                for h in range(H):
                    c = slice(h * (D // H), (h + 1) * (D // H))
                    link(V.tensor_tensor(pre[:, :, c], pre[:, :, c], rden[:, :, h:h + 1].to_broadcast([P, NP, D // H]), ALU.mult))
                link(V.tensor_tensor(pre[:, :, :], pre[:, :, :], bc(vec[:, v0, :]), ALU.add))
                normalise(pre[:, :, :])
                link(V.tensor_tensor(pre[:, :, :], pre[:, :, :], bc(vec[:, v0 + 1, :]), ALU.mult))
                link(V.tensor_tensor(pre[:, :, :], pre[:, :, :], bc(vec[:, v0 + 2, :]), ALU.add))
                link(V.tensor_scalar(tmp, pre[:, :, :], 0.0, None, ALU.min))
                ask()
                link(V.tensor_scalar(pre[:, :, :], pre[:, :, :], 0.0, -1.0, ALU.max, ALU.add))
                link(V.tensor_tensor(pre[:, :, :], pre[:, :, :], tmp, ALU.add))
            link(V.tensor_tensor(xcur[:, :, :], xcur[:, :, :], pre[:, :, :], ALU.add))
            normalise(xcur[:, :, :])

            for p, j, src in ((4, "o4", xcur), (5, "o5", pre)):
                q = passes[p]
                link(V.tensor_copy(tab[:, :, 0:D], src[:, :, :]))
                link(V.memset(tab[:, :, D:D + 1], 1.0))
                dve.sem_inc(table_made, 1)
                accs = edges(q)
                link(V.tensor_scalar(deginv[:, :].unsqueeze(2), accs[:, :, D:D + 1], 1.0, None, ALU.max))
                link(V.reciprocal(deginv[:, :], deginv[:, :]))

                def stage_sage(b, o, done, accs=accs):
                    w = bass.ds(b * WB, WB)
                    V.tensor_tensor(o[:, :, 0:D], accs[:, w, 0:D], deginv[:, w].unsqueeze(2).to_broadcast([P, WB, D]),
                                    ALU.mult).then_inc(half_staged, 1)
                    V.tensor_copy(o[:, :, D:2 * D], tab[:, w, 0:D]).then_inc(done, 1)
                project(J[j], stage_sage)
                link(V.tensor_tensor(pre[:, :, :], pre[:, :, :], bc(vec[:, 6 + p - 4, :]), ALU.add))
                link(V.tensor_tensor(tmp, pre[:, :, :], pre[:, :, :], ALU.mult))
                link(V.tensor_reduce(stat[:, :], tmp, AX, ALU.add))
                ask()
                link(V.tensor_scalar(stat[:, :], stat[:, :], 1e-12, None, ALU.max))
                link(V.reciprocal(stat[:, :], stat[:, :]))
                link(V.tensor_tensor(pre[:, :, :], pre[:, :, :], per(stat[:, :], 2, full), ALU.mult))
                link(V.tensor_scalar(pre[:, :, :], pre[:, :, :], 0.0, None, ALU.max))
            link(V.tensor_tensor(xcur[:, :, :], xcur[:, :, :], pre[:, :, :], ALU.add))
            normalise(xcur[:, :, :])
            dve.sem_inc(final_made, 1)


def kernel(x, src, dst, edge_attr_32, **w):
    import numpy as np
    import concourse.bacc as bacc
    from concourse.bass_utils import run_bass_kernel_spmd as run

    rec = np.empty((E + GEMAX, 2), np.int32)
    rec[:E, 0], rec[:E, 1] = np.asarray(src), np.asarray(dst)
    rec[E:, 0], rec[E:, 1] = 0, BIG_NODE
    attr = np.zeros((E + GEMAX, DE), np.float32)
    attr[:E] = np.asarray(edge_attr_32)
    v = {k: np.asarray(a) for k, a in w.items()}
    arrays = {
        "x": np.asarray(x), "rec": rec, "attr": attr,
        "attn_wT": v["L0_gnn_attn_w"].reshape(2, D).T, "attn_b": v["L0_gnn_attn_b"],
        "proj_w": v["L0_gnn_proj_w"], "apply_wT": v["L0_gnn_apply_w"].T, "apply_b": v["L0_gnn_apply_b"],
        "W_t": v["L1_gnn_W"].transpose(2, 0, 1), "a_t": v["L1_gnn_a"].reshape(H1, 2, D).transpose(2, 0, 1),
        "merge_t": v["L1_gnn_merge_kernel"].reshape(H1, D, D).transpose(1, 0, 2),
        "W1": v["L2_gnn_W1"], "W2": v["L2_gnn_W2"],
        "a1_src": v["L2_gnn_a1_src"].reshape(-1), "a1_dst": v["L2_gnn_a1_dst"].reshape(-1),
        "a2_src": v["L2_gnn_a2_src"].reshape(-1), "a2_dst": v["L2_gnn_a2_dst"].reshape(-1),
        "b1": v["L2_gnn_b1"], "b2": v["L2_gnn_b2"],
        "ln1_g": v["L2_gnn_ln1_g"], "ln1_b": v["L2_gnn_ln1_b"],
        "ln2_g": v["L2_gnn_ln2_g"], "ln2_b": v["L2_gnn_ln2_b"],
        "Wl0T": v["L3_gnn_Wl0"].T, "Wr0T": v["L3_gnn_Wr0"].T, "bl0": v["L3_gnn_bl0"],
        "Wl1T": v["L3_gnn_Wl1"].T, "Wr1T": v["L3_gnn_Wr1"].T, "bl1": v["L3_gnn_bl1"],
    }
    nc = bacc.Bacc("TRN2", target_bir_lowering=False, num_devices=1)
    ins, aps = {}, {}
    for name, arr in arrays.items():
        arr = np.ascontiguousarray(arr)
        ins[f"in_{name}"] = arr
        aps[name] = nc.dram_tensor(f"in_{name}", arr.shape, mybir.dt.from_np(arr.dtype), kind="ExternalInput").ap()
    out = nc.dram_tensor("out_0", (N, D), fp32, kind="ExternalOutput").ap()
    build(nc, aps, out)
    r = run(nc, [ins], core_ids=[0])
    return r.results[0]["out_0"]
```

```python
from contextlib import ExitStack

import concourse.bass as bass
from concourse import mybir

fp32 = mybir.dt.float32
i32 = mybir.dt.int32
bf16 = mybir.dt.bfloat16
ALU = mybir.AluOpType
ACT = mybir.ActivationFunctionType
AX = mybir.AxisListType.X
RMAX = bass.bass_isa.ReduceOp.max

P = 128
N, E, D, DE = 6250, 200000, 64, 32
NW = -(-N // P)
NB = NW + 1
NP = 52
FULL, TAIL = N // P, N % P
SP_, SC = 125, E // 125
SU, SLOTS = 40, 4
CC = SU * SLOTS
WU = 7
assert SC % CC == 0 and NW % WU == 0 and WU * CC <= SC
H1, H2 = 8, 4
SLOPE = 0.2
SPAN = 16.0
BIG_NODE = 1 << 20


class Side:

    def __init__(self, name, number, G, U):
        self.name, self.number = name, number
        self.G = G
        self.GE = G * P
        self.U = U
        self.NG = -(-((E + NW * (self.GE - 1)) // self.GE) // U) * U
        self.T = self.NG * G
        self.GP = max(p for p in range(1, P + 1) if self.NG % p == 0)
        self.GC = self.NG // self.GP


BY = {"dst": Side("dst", 0, 2, 8), "src": Side("src", 1, 4, 4)}
UG = max(b.U * b.G for b in BY.values())
GMAX = max(b.G for b in BY.values())
GEMAX = max(b.GE for b in BY.values())
NGMAX = max(b.NG for b in BY.values())
TMAX = max(b.T for b in BY.values())
GCMAX = max(b.GC for b in BY.values())


class Chain:

    def __init__(self, eng, sem):
        self.eng, self.sem, self.n = eng, sem, 0

    def __call__(self, ins):
        self.n += 1
        ins.then_inc(self.sem, 1)
        self.eng.wait_ge(self.sem, self.n)


def since(eng, sem, value, before=0):
    if isinstance(value, int) and value <= 0:
        return
    eng.wait_ge(sem, value + before)


def pipelined(eng, count, unroll, stages):
    def step(i, s):
        for lag, stage in stages:
            k = i * unroll + s + lag
            if not isinstance(i, int) or 0 <= k < count:
                stage(k, (s + lag) % unroll, i + (s + lag) // unroll)

    ahead = max(lag for lag, _ in stages)
    behind = -min(lag for lag, _ in stages)
    assert ahead < unroll + 1 and behind <= unroll
    for k in range(-ahead, unroll):
        step(k // unroll, k % unroll)
    bodies = count // unroll
    with eng.Fori(1, bodies - 1) as i:
        for s in range(unroll):
            step(i, s)
    for k in range((bodies - 1) * unroll, count + behind):
        step(k // unroll, k % unroll)


def build(nc, a, out):
    ctx = ExitStack()
    with ctx:
        def sb(name, shape, dt=fp32):
            return ctx.enter_context(nc.sbuf_tensor(name, shape, dt))

        def ps(name, shape):
            return ctx.enter_context(nc.psum_tensor(name, shape, fp32))

        def sem(name):
            return ctx.enter_context(nc.semaphore(name))

        def dram(name, shape, dt=fp32):
            return nc.dram_tensor(name, shape, dt, kind="Internal").ap()

        records_src = dram("records_src", [BY["src"].T * P, 2], i32)
        saved_idx = dram("saved_idx", [P, BY["dst"].T], i32)
        saved_local = dram("saved_local", [P, BY["dst"].T])
        group_window = {s: dram(f"group_window_{s}", [BY[s].NG], i32) for s in ("dst", "src")}
        group_start = dram("group_start", [BY["dst"].NG], i32)
        ROW = [65, 72, 68, 65, 65, 65]
        tables = [dram(f"table{p}", [NP * P, ROW[p]]) for p in range(6)]

        HEADS = [1, H1, H2, 1, 0, 0]
        OUTW = [D + DE + 1, H1 * D + H1, D + H2, D + 1, D + 1, D + 1]
        SIDE = ["dst", "src", "dst", "dst", "dst", "dst"]

        ACCF = NP * OUTW[1]
        acc_all = sb("acc_all", [P, ACCF])
        xcur = sb("xcur", [P, NP, D])
        pre = sb("pre", [P, NP, D])
        tab = sb("tab", [P, NP, 80])
        ntab = sb("ntab", [P, NP, 2 * H1])
        ntab3 = sb("ntab3", [P, 3, NP, 2 * H1], bf16)
        rden = sb("rden", [P, NP, H1])
        mtmp = acc_all[:, 19400:19400 + NP * H1].rearrange("p (w h) -> p w h", w=NP)
        deginv = sb("deginv", [P, NP])
        stat = sb("stat", [P, NP])
        idx = sb("idx", [P, TMAX], i32)
        local = sb("local", [P, TMAX])
        group_rows = sb("group_rows", [P, NGMAX], i32)
        wrow = {"dst": group_rows[0:1, :], "src": group_rows[64:65, :]}
        srow = group_rows[32:33, 0:BY["dst"].NG]
        idx_slot = sb("idx_slot", [P, UG], i32)
        rows = sb("rows", [P, UG * 72])
        attrs = sb("attrs", [P, UG, DE])
        flat_pre = pre[:, :, :].rearrange("p w f -> p (w f)")
        onehots = flat_pre[:, 0:UG * P].rearrange("p (t n) -> p t n", n=P)
        onehot_ts = flat_pre[:, UG * P:UG * P + GEMAX].bitcast(bf16).rearrange("p (t n) -> p t n", n=P)
        t12 = sb("t12", [P, 2, GMAX, 2 * H1])
        zmax = sb("zmax", [P, 2, GMAX * H1])
        rhs = sb("rhs", [P, 2, GMAX * OUTW[1]])
        flat_rhs = rhs[:, :, :].rearrange("p a b -> p (a b)")
        staged = flat_rhs[:, 0:2048].rearrange("p (a b) -> p a b", a=2)
        node_t = flat_rhs[:, 2048:4096].rearrange("p (a b) -> p a b", a=2)

        def region(at, shape, dt=fp32):
            n = 1
            for d in shape[1:]:
                n *= d
            v = acc_all[0:shape[0], at:at + n]
            if dt is not fp32:
                v = v.bitcast(dt)
            if len(shape) == 2:
                return v
            names = "abc"[:len(shape) - 1]
            return v.rearrange(f"p ({' '.join(names)}) -> p {' '.join(names)}",
                               **{c: d for c, d in zip(names, shape[1:])})

        flat_rec = region(0, [SP_, SC, 2], i32)
        keyw = region(2 * SC, [SP_, SC])
        keyi = region(3 * SC, [SP_, SC], i32)
        ind = region(4 * SC, [SP_, SC])
        cum = region(5 * SC, [SP_, SC])
        pos = region(6 * SC, [SP_, SC])
        posi = region(7 * SC, [SP_, SC], i32)
        grec = region(20000, [P, TMAX, 2], i32)
        wbi = region(23520, [P, NGMAX], i32)
        wb = region(24400, [P, NGMAX])
        keyh = acc_all[0:SP_, 16000:16000 + SC // 2].bitcast(bf16)
        indh = acc_all[0:SP_, 16000 + SC // 2:16000 + SC].bitcast(bf16)
        pad = region(24000, [P, 1024, 2], i32)
        CLEARED = 16000
        tmp = region(CLEARED, [P, NP, D])
        assert 20000 + 2 * TMAX <= 23520

        ident = sb("ident", [P, P])
        ones = sb("ones", [P, P])
        below = sb("below", [P, P])
        iota_n = sb("iota_n", [P, P])
        iota_ni = sb("iota_ni", [P, P], i32)
        iota_g = sb("iota_g", [P, 2, GCMAX])
        iota_gi = sb("iota_gi", [P, 2, GCMAX], i32)
        gsm = region(12800, [P, 8, NB])
        gsi = region(13200, [P, 2, NB], i32)
        cnt = region(13300, [P, 2, NB])
        base = region(13400, [P, NB])
        gcmps = region(26100, [P, GCMAX, NW])
        gws = region(13450, [P, 2, GCMAX])
        gwis = region(13470, [P, 2, GCMAX], i32)
        pos_slot = region(26500, [SP_, SLOTS, SU], i32)
        rec_slot = region(26500 + SLOTS * SU, [SP_, SLOTS * SU, 2], i32)
        assert 26500 + 3 * SLOTS * SU <= ACCF
        gm = sb("gm", [P, 2, 2 * H2]); flag = sb("flag", [P, 2]); flagi = sb("flagi", [P, 1], i32)

        w_attn = sb("w_attn", [D, 2]); b_attn = sb("b_attn", [P, 1])
        w_proj = region(13800, [D, D + DE]); w_a1 = sb("w_a1", [D, D]); w_a2 = region(13900, [D, D])
        b_apply = sb("b_apply", [P, D]); w_pa = sb("w_pa", [D + DE, D])
        w1t = region(14000, [D, H1, D]); a1v = region(14520, [D, H1, 2]); mk = region(14600, [D, H1, D])
        w_s1 = sb("w_s1", [D, 2 * H1]); w_m1 = sb("w_m1", [P, H1 // 2, D])
        w_2 = sb("w_2", [D, D + 2 * H2]); a2b = region(15120, [D, 2, D]); w_3 = sb("w_3", [D, D + 2])
        a3b = region(15260, [D, 2, D]); wtmp = region(15400, [D, 2, D])
        vec = sb("vec", [P, 8, D])
        w_sage = sb("w_sage", [P, 2, D])

        ps_t = ps("ps_t", [P, 2, 512])
        ps_x = ps("ps_x", [P, 2, 512])
        ps_a = ps("ps_a", [P, 2, 1024])

        loaded_w = sem("loaded_w"); loaded_x = sem("loaded_x"); loaded_rec = sem("loaded_rec")
        pool_consts = sem("pool_consts"); half_staged = sem("half_staged")
        consts_ready = sem("consts_ready")
        dve_chain = sem("dve_chain")
        loop_count = sem("loop_count"); loop_ind = sem("loop_ind"); loop_cum = sem("loop_cum")
        loop_pos = sem("loop_pos"); loop_base = sem("loop_base")
        counted = sem("counted"); totals = sem("totals"); sorted_ = sem("sorted")
        groups_ready = sem("groups_ready"); groups_stored = sem("groups_stored")
        starts_loaded = sem("starts_loaded"); dst_runs = sem("dst_runs")
        pad_ready = sem("pad_ready")
        pad_stored = sem("pad_stored")
        slot_staged = sem("slot_staged")
        scattered = [sem(f"scattered{i}") for i in range(SLOTS)]
        scatter_done = sem("scatter_done")
        weights_made = sem("weights_made"); weights_mm = sem("weights_mm")
        pool_steps = sem("pool_steps"); pe_steps = sem("pe_steps"); dve_steps = sem("dve_steps")
        score_max = sem("score_max"); score_all = sem("score_all")
        flag_ready = sem("flag_ready"); side_made = sem("side_made"); side_saved = sem("side_saved")
        side_loaded = sem("side_loaded"); side_free = sem("side_free"); side_back = sem("side_back")
        acc_free = sem("acc_free"); acc_cleared = sem("acc_cleared")
        table_made = sem("table_made"); table_written = sem("table_written")
        act_ask = sem("act_ask"); act_done = sem("act_done")
        final_made = sem("final_made"); out_written = sem("out_written")

        class Pass:
            pass

        landings = {by.name: [sem(f"landed_{by.name}{s}") for s in range(by.U)] for by in BY.values()}
        landed_before = {"dst": 0, "src": 0}
        passes = []
        for p in range(6):
            q = Pass()
            q.n, q.H, q.F, q.W, q.by = p, HEADS[p], ROW[p], OUTW[p], BY[SIDE[p]]
            q.banks = -(-q.W // 512)
            q.idx_staged = sem(f"p{p}_idx_staged")
            q.begun = sem(f"p{p}_begun")
            q.landed = landings[q.by.name]
            q.land0 = landed_before[q.by.name]
            landed_before[q.by.name] += 16 * q.by.G * (q.by.NG // q.by.U)
            q.attr_landed = [sem(f"p{p}_attr{s}") for s in range(q.by.U)] if p == 0 else None
            q.onehot_made = sem(f"p{p}_onehot_made")
            q.summed = sem(f"p{p}_summed")
            q.added = sem(f"p{p}_added")
            if q.H:
                q.transposed = sem(f"p{p}_transposed")
                q.copied = sem(f"p{p}_copied")
                q.expanded = sem(f"p{p}_expanded")
                q.scored = sem(f"p{p}_scored")
                q.maxed = sem(f"p{p}_maxed")
                q.clipped = sem(f"p{p}_clipped")
                q.weighed = sem(f"p{p}_weighed")
                q.rhs_made = sem(f"p{p}_rhs_made")
            if p in (0, 2, 3):
                q.m_idx = sem(f"p{p}_m_idx"); q.m_landed = sem(f"p{p}_m_landed")
                q.m_masked = sem(f"p{p}_m_masked"); q.m_transposed = sem(f"p{p}_m_transposed")
                q.m_chain = sem(f"p{p}_m_chain")
            if p == 0:
                q.rhs_half = sem(f"p{p}_rhs_half")
            passes.append(q)

        class Projection:
            pass

        def projection(chunks, dst, at, width, WB=4):
            j = Projection()
            j.chunks, j.dst, j.at, j.N = chunks, dst, at, width
            j.WB, j.steps = WB, NP // WB
            j.before = numbered[1]
            numbered[0] += 1
            numbered[1] += j.steps
            j.number = numbered[0]
            j.ready, j.staged, j.transposed, j.copied, j.multiplied, j.stored = proj_sems
            return j

        numbered = [0, 0]
        proj_sems = [sem(f"proj_{n}") for n in ("ready", "staged", "transposed", "copied", "multiplied", "stored")]

        J = {
            "s0": projection([(D, w_attn[:, :])], tab, D, 2),
            "o0": projection([(D + DE, w_pa[:, :]), (D, w_a1[:, :])], pre, 0, D),
            "s1": projection([(D, w_s1[:, :])], tab, D, 2 * H1),
            "o1": projection([(P, w_m1[:, c, :]) for c in range(H1 // 2)], pre, 0, D, WB=2),
            "s2": projection([(D, w_2[:, :])], tab, 0, D + 2 * H2),
            "s3": projection([(D, w_3[:, :])], tab, 0, D + 2),
            "o4": projection([(P, w_sage[:, 0, :])], pre, 0, D),
            "o5": projection([(P, w_sage[:, 1, :])], pre, 0, D),
        }
        ORDER = [("s0", 0, "o0"), ("s1", 1, "o1"), ("s2", 2, None), ("s3", 3, None),
                 (None, 4, "o4"), (None, 5, "o5")]

        block = ctx.enter_context(nc.Block())

        @block.sync
        def _(sp):
            sp.dma_start(flat_rec, a["rec"][0:E, :].rearrange("(p c) t -> p c t", p=SP_))\
              .then_inc(loaded_rec, 16)
            sp.wait_ge(consts_ready, 1)
            sp.dma_start(xcur[:, 0:FULL, :], a["x"][0:FULL * P, :].rearrange("(w p) f -> p w f", p=P))\
              .then_inc(loaded_x, 16)
            sp.dma_start(xcur[0:TAIL, FULL, :], a["x"][FULL * P:N, :]).then_inc(loaded_x, 16)
            loads = [
                (w_attn[:, :], a["attn_wT"]), (b_attn[:, :], a["attn_b"].partition_broadcast(P)),
                (w_proj[:, :], a["proj_w"]), (w_a1[:, :], a["apply_wT"][0:D, :]),
                (w_a2[:, :], a["apply_wT"][D:2 * D, :]), (b_apply[:, :], a["apply_b"].partition_broadcast(P)),
                (w1t[:, :, :], a["W_t"]), (a1v[:, :, :], a["a_t"]), (mk[:, :, :], a["merge_t"]),
                (w_2[:, 0:D], a["W1"]), (w_3[:, 0:D], a["W2"]),
                (a2b[:, 0, :], a["a1_src"].partition_broadcast(D)),
                (a2b[:, 1, :], a["a1_dst"].partition_broadcast(D)),
                (a3b[:, 0, :], a["a2_src"].partition_broadcast(D)),
                (a3b[:, 1, :], a["a2_dst"].partition_broadcast(D)),
                (w_sage[0:D, 0, :], a["Wl0T"]), (w_sage[D:P, 0, :], a["Wr0T"]),
                (w_sage[0:D, 1, :], a["Wl1T"]), (w_sage[D:P, 1, :], a["Wr1T"]),
            ] + [(vec[:, i, :], a[n].partition_broadcast(P)) for i, n in
                 enumerate(("b1", "ln1_g", "ln1_b", "b2", "ln2_g", "ln2_b", "bl0", "bl1"))]
            for dst, src in loads:
                sp.dma_start(dst, src).then_inc(loaded_w, 16)
            sp.wait_ge(pad_ready, 2)
            rec_flat = records_src.rearrange("(p c) t -> p c t", p=P)
            per = BY["src"].T
            for c in range(0, per, 1024):
                n = min(1024, per - c)
                sp.dma_start(rec_flat[:, c:c + n, :], pad[:, 0:n, :]).then_inc(pad_stored, 16)
            by = BY["dst"]
            sp.wait_ge(groups_ready, 1)
            sp.dma_start(group_window["src"].rearrange("(p c) -> p c", p=BY["src"].GP),
                         gwis[0:BY["src"].GP, 0, 0:BY["src"].GC]).then_inc(groups_stored, 16)
            sp.wait_ge(groups_ready, 2)
            sp.dma_start(group_window["dst"].rearrange("(p c) -> p c", p=by.GP), gwis[0:by.GP, 0, 0:by.GC]).then_inc(groups_stored, 16)
            sp.dma_start(group_start.rearrange("(p c) -> p c", p=by.GP), gwis[0:by.GP, 1, 0:by.GC]).then_inc(groups_stored, 16)
            sp.wait_ge(groups_stored, 48)
            sp.dma_start(srow, group_start.rearrange("(a n) -> a n", a=1)).then_inc(starts_loaded, 16)
            for b in BY.values():
                sp.dma_start(wrow[b.name][:, 0:b.NG], group_window[b.name].rearrange("(a n) -> a n", a=1))\
                  .then_inc(starts_loaded, 16)
            sp.wait_ge(pad_stored, 16 * -(-per // 1024))
            sp.dma_start(wbi[:, 0:by.NG], group_window["dst"].partition_broadcast(P)).then_inc(side_loaded, 16)
            sp.wait_ge(starts_loaded, 48)
            with sp.Fori(0, by.NG) as k:
                start = sp.value_load(srow[0:1, bass.ds(k, 1)], min_val=0, max_val=E)
                sp.dma_start(grec[:, bass.ds(k * by.G, by.G), :],
                             a["rec"][bass.ds(start, by.GE), :].rearrange("(p g) t -> p g t", p=P))\
                  .then_inc(dst_runs, 16)

            for q in passes:
                sp.wait_ge(table_made, q.n + 1)
                sp.dma_start(tables[q.n].rearrange("(w p) f -> p w f", p=P), tab[:, :, 0:q.F])\
                  .then_inc(table_written, 16)
                if q.n == 0:
                    def attr_load(k, s, turn):
                        start = sp.value_load(srow[0:1, bass.ds(k, 1)], min_val=0, max_val=E)
                        since(sp, q.rhs_made, k - by.U + 1)
                        sp.dma_start(attrs[:, s * by.G:(s + 1) * by.G, :],
                                     a["attr"][bass.ds(start, by.GE), :].rearrange("(p g) f -> p g f", p=P))\
                          .then_inc(q.attr_landed[s], 16)
                    sp.wait_ge(side_made, 1)
                    sp.dma_start(saved_idx, idx[:, 0:by.T]).then_inc(side_saved, 16)
                    sp.dma_start(saved_local, local[:, 0:by.T]).then_inc(side_saved, 16)
                    pipelined(sp, by.NG, by.U, [(0, attr_load)])
                    src = BY["src"]
                    sp.wait_ge(scatter_done, 1)
                    sp.dma_start(grec[:, 0:src.T, :].rearrange("p (k g) t -> p k g t", g=src.G),
                                 records_src.rearrange("(k p g) t -> p k g t", p=P, g=src.G)).then_inc(side_loaded, 16)
                    sp.dma_start(wbi[:, 0:src.NG], group_window["src"].partition_broadcast(P)).then_inc(side_loaded, 16)
                if q.n == 1:
                    sp.wait_ge(side_free, 1)
                    sp.wait_ge(side_saved, 32)
                    sp.dma_start(idx[:, 0:by.T], saved_idx).then_inc(side_back, 16)
                    sp.dma_start(local[:, 0:by.T], saved_local).then_inc(side_back, 16)
            sp.wait_ge(final_made, 1)
            sp.dma_start(out[0:FULL * P, :].rearrange("(w p) f -> p w f", p=P), xcur[:, 0:FULL, :]).then_inc(out_written, 16)
            sp.dma_start(out[FULL * P:N, :], xcur[0:TAIL, FULL, :]).then_inc(out_written, 16)
            sp.wait_ge(out_written, 32)

        @block.gpsimd
        def _(pool):
            nc.gpsimd.memset(xcur[:, :, :], 0.0).then_inc(consts_ready, 1)
            nc.gpsimd.iota(pad[:, :, 0:1], pattern=[[0, 1024]], base=BIG_NODE, channel_multiplier=0).then_inc(pad_ready, 1)
            nc.gpsimd.iota(pad[:, :, 1:2], pattern=[[0, 1024]], base=0, channel_multiplier=0).then_inc(pad_ready, 1)
            nc.gpsimd.memset(ones[:, :], 1.0).then_inc(pool_consts, 1)
            nc.gpsimd.iota(iota_ni[:, :], pattern=[[1, P]], base=0, channel_multiplier=0).then_inc(pool_consts, 1)
            for by in BY.values():
                nc.gpsimd.iota(iota_gi[:, by.number, :], pattern=[[1, GCMAX]], base=0, channel_multiplier=by.GC)\
                    .then_inc(pool_consts, 1)
            pool.wait_ge(pool_consts, 4)
            nc.gpsimd.affine_select(out=ident[:, :], in_=ones[:, :], pattern=[[-1, P]], compare_op=ALU.is_equal,
                                    fill=0.0, base=0, channel_multiplier=1).then_inc(pool_consts, 1)
            nc.gpsimd.affine_select(out=below[:, :], in_=ones[:, :], pattern=[[1, P]], compare_op=ALU.is_gt,
                                    fill=0.0, base=0, channel_multiplier=-1).then_inc(pool_consts, 1)

            def scatter(k, s, turn):
                pool.wait_ge(pad_stored, 16 * -(-BY["src"].T // 1024))
                since(pool, slot_staged, 2 * (k + 1))
                pool.sem_inc(pool_steps, 1)
                for c in range(SU):
                    pool.indirect_dma_start(records_src, bass.IndirectOffsetOnAxis(ap=pos_slot[:, s, c:c + 1], axis=0),
                                            rec_slot[:, s * SU + c, :], None).then_inc(scattered[s], 16)
            pipelined(pool, SC // SU, SLOTS, [(0, scatter)])
            for s in range(SLOTS):
                pool.wait_ge(scattered[s], 16 * SC // SLOTS)
            pool.sem_inc(scatter_done, 1)

            asks = 0
            for q in passes:
                NG, G, U = q.by.NG, q.by.G, q.by.U
                if q.n in (0, 2, 3):
                    asks += 1
                    pool.wait_ge(score_max, asks)
                    nc.gpsimd.partition_all_reduce(gm[:, 1, 0:2 * q.H], gm[:, 0, 0:2 * q.H], P, RMAX).then_inc(score_all, 1)
                    pool.wait_ge(flag_ready, asks)
                    pool.wait_ge(table_written, 16 * (q.n + 1))
                    wide = pool.value_load(flagi[0:1, 0:1], min_val=0, max_val=1)
                    with pool.If(wide > 0):
                        with pool.Fori(0, NG) as k:
                            pool.wait_ge(q.m_idx, k + 1)
                            pool.sem_inc(pool_steps, 1)
                            for g in range(G):
                                pool.indirect_dma_start(rows[:, g * q.F:(g + 1) * q.F], None, tables[q.n],
                                                        bass.IndirectOffsetOnAxis(ap=idx_slot[:, g:g + 1], axis=0))\
                                    .then_inc(q.m_landed, 16)
                    pool.sem_inc(pool_steps, 1)
                if q.n == 1:
                    pool.wait_ge(acc_free, 1)
                    nc.gpsimd.memset(acc_all[:, 0:CLEARED], 0.0).then_inc(acc_cleared, 1)

                def gather(k, s, turn, q=q, G=G, U=U):
                    pool.wait_ge(table_written, 16 * (q.n + 1))
                    since(pool, q.idx_staged, k + 1)
                    if q.H:
                        since(pool, q.rhs_made, k - U + 1)
                    else:
                        since(pool, q.summed, k - U + 1)
                    pool.sem_inc(pool_steps, 1)
                    for t in range(s * G, (s + 1) * G):
                        pool.indirect_dma_start(rows[:, t * q.F:(t + 1) * q.F], None, tables[q.n],
                                                bass.IndirectOffsetOnAxis(ap=idx_slot[:, t:t + 1], axis=0))\
                            .then_inc(q.landed[s], 16)
                pipelined(pool, NG, U, [(0, gather)])

        @block.scalar
        def _(act):
            def stage_scatter(k, s, turn):
                act.wait_ge(sorted_, turn + 1)
                since(act, scattered[s], 16 * SU * turn)
                nc.scalar.copy(pos_slot[:, s, :], posi[:, bass.ds(k * SU, SU)]).then_inc(slot_staged, 1)
                nc.scalar.copy(rec_slot[:, s * SU:(s + 1) * SU, :], flat_rec[:, bass.ds(k * SU, SU), :]).then_inc(slot_staged, 1)
            pipelined(act, SC // SU, SLOTS, [(0, stage_scatter)])

            def project(j):
                act.wait_ge(j.ready, j.number)

                def evacuate(b, s, turn):
                    since(act, j.transposed, b + 1, j.before)
                    since(act, j.multiplied, b - 1, j.before)
                    same = all(K == P for K, _ in j.chunks)
                    WB = j.WB
                    parts = [(0, P, len(j.chunks))] if same else [(c, K, 1) for c, (K, _) in enumerate(j.chunks)]
                    for n, (c, K, m) in enumerate(parts):
                        ins = nc.scalar.copy(node_t[0:K, s, c * WB * P:(c + m) * WB * P],
                                             ps_a[0:K, s, c * WB * P:(c + m) * WB * P])
                    ins.then_inc(j.copied, 1)
                pipelined(act, j.steps, 2, [(1, evacuate)])

            def edges(q):
                NG, G, U = q.by.NG, q.by.G, q.by.U

                def stage_idx(k, s, turn):
                    act.wait_ge(q.begun, 1)
                    since(act, q.landed[s], 16 * G * turn, q.land0)
                    nc.scalar.copy(idx_slot[:, s * G:(s + 1) * G], idx[:, bass.ds(k * G, G)]).then_inc(q.idx_staged, 1)

                def copy_onehot(k, s, turn):
                    since(act, q.transposed, k + 1)
                    since(act, q.expanded, k - 1)
                    half = slice(s % 2 * G, (s % 2 + 1) * G)
                    nc.scalar.copy(onehot_ts[:, half, :].rearrange("p g n -> p (g n)"), ps_t[:, s % 2, 0:G * P])\
                        .then_inc(q.copied, 1)

                def weigh(k, s, turn):
                    since(act, q.clipped, k + 1)
                    since(act, q.summed, k - 1)
                    w = rhs[:, s % 2, 0:G * q.W].rearrange("p (g f) -> p g f", g=G)
                    nc.scalar.activation(w[:, :, q.W - q.H:q.W],
                                         zmax[:, s % 2, 0:G * q.H].rearrange("p (g h) -> p g h", g=G), ACT.Exp)\
                        .then_inc(q.weighed, 1)
                if q.H:
                    pipelined(act, NG, U, [(1, weigh), (3, copy_onehot), (U - 1 if U > 4 else U, stage_idx)])
                else:
                    pipelined(act, NG, U, [(U, stage_idx)])

            asked = [0]

            def serve(func, out_, in_):
                asked[0] += 1
                act.wait_ge(act_ask, asked[0])
                nc.scalar.activation(out_, in_, func).then_inc(act_done, 1)

            for s_name, p, o_name in ORDER:
                q = passes[p]
                if s_name:
                    project(J[s_name])
                if p in (2, 3):
                    serve(ACT.Exp, mtmp[:, :, 0:q.H], mtmp[:, :, 0:q.H])
                edges(q)
                if p in (2, 3):
                    serve(ACT.Sqrt, stat[:, :], stat[:, :])
                    serve(ACT.Exp, tmp, tmp)
                if o_name:
                    project(J[o_name])
                if p in (4, 5):
                    serve(ACT.Sqrt, stat[:, :], stat[:, :])
                if p != 2 and p != 4:
                    serve(ACT.Sqrt, stat[:, :], stat[:, :])

        @block.tensor
        def _(pe):
            for turn, n in enumerate((1, 0)):
                pe.wait_ge(pool_consts, 6)
                pe.wait_ge(counted, turn + 1)
                nc.tensor.matmul(ps_x[:, n, 0:NB], ones[0:SP_, :], cnt[0:SP_, n, :], start=True, stop=True).then_inc(totals, 1)
                if n == 1:
                    nc.tensor.matmul(ps_t[0:SP_, 0, 0:NB], below[0:SP_, 0:SP_], cnt[0:SP_, 1, :],
                                     start=True, stop=True).then_inc(totals, 1)
            pe.wait_ge(loaded_w, 16 * 27)
            nc.tensor.matmul(ps_a[0:D + DE, 0, 0:D], w_proj[:, :], w_a2[:, :], start=True, stop=True)
            for h in range(H1):
                nc.tensor.matmul(ps_a[0:D, 0, 64 + 2 * h:66 + 2 * h], w1t[:, h, :], a1v[:, h, :], start=True, stop=True)
            for h in range(H1):
                c = h // 2
                ins = nc.tensor.matmul(ps_a[:, 1, h * D:(h + 1) * D], w1t[:, 2 * c:2 * c + 2, :].rearrange("u a f -> u (a f)"),
                                       mk[:, h, :], start=True, stop=True)
            ins.then_inc(weights_mm, 1)

            def project(j):
                pe.wait_ge(j.ready, j.number)
                WB = j.WB

                def transpose(b, s, turn):
                    since(pe, j.staged, b + 1, j.before)
                    since(pe, j.copied, b - 1, j.before)
                    pe.sem_inc(pe_steps, 1)
                    for c, (K, _) in enumerate(j.chunks):
                        for w in range(WB):
                            at = (w * len(j.chunks) + c) * P
                            o = (c * WB + w) * P
                            ins = nc.tensor.transpose(ps_a[0:K, s, o:o + P], staged[:, s, at:at + K], ident[:, :])
                    ins.then_inc(j.transposed, 1)

                def multiply(b, s, turn):
                    since(pe, j.copied, b + 1, j.before)
                    since(pe, j.stored, b - 1, j.before)
                    for w in range(WB):
                        for c, (K, weight) in enumerate(j.chunks):
                            o = (c * WB + w) * P
                            ins = nc.tensor.matmul(ps_x[:, s, w * j.N:(w + 1) * j.N], node_t[0:K, s, o:o + P], weight,
                                                   start=(c == 0), stop=(c == len(j.chunks) - 1))
                    ins.then_inc(j.multiplied, 1)
                pipelined(pe, j.steps, 2, [(1, transpose), (0, multiply)])

            def edges(q):
                NG, G, U = q.by.NG, q.by.G, q.by.U

                def transpose(k, s, turn):
                    since(pe, q.onehot_made, k + 1)
                    since(pe, q.copied, k - 1)
                    for g in range(G):
                        ins = nc.tensor.transpose(ps_t[:, s % 2, g * P:(g + 1) * P], onehots[:, s * G + g, :], ident[:, :])
                    ins.then_inc(q.transposed, 1)

                def expand(k, s, turn):
                    w = pe.value_load(wrow[q.by.name][0:1, bass.ds(k, 1)], min_val=0, max_val=NW)
                    since(pe, q.copied, k + 1)
                    since(pe, q.scored, 2 * (k - 1))
                    for g in range(G):
                        for part in range(3):
                            ins = nc.tensor.matmul(ps_x[:, s % 2, g * 2 * q.H:(g + 1) * 2 * q.H], onehot_ts[:, s % 2 * G + g, :],
                                                   ntab3[:, part, bass.ds(w, 1), 0:2 * q.H].rearrange("p a h -> p (a h)"),
                                                   start=(part == 0), stop=(part == 2))
                    ins.then_inc(q.expanded, 1)

                def total(k, s, turn):
                    if q.H:
                        since(pe, q.rhs_made, k + 1)
                        r = rhs[:, s % 2, 0:G * q.W].rearrange("p (g f) -> p g f", g=G)
                    else:
                        since(pe, q.landed[s], 16 * G * (turn + 1), q.land0)
                        since(pe, q.onehot_made, k + 1)
                        r = rows[:, s * G * q.F:(s + 1) * G * q.F].rearrange("p (g f) -> p g f", g=G)
                    since(pe, q.added, k - 1)
                    for b in range(q.banks):
                        n = q.W // q.banks
                        for g in range(G):
                            ins = nc.tensor.matmul(ps_a[:, s % 2, b * 512:b * 512 + n], onehots[:, s * G + g, :],
                                                   r[:, g, b * n:(b + 1) * n], start=(g == 0), stop=(g == G - 1))
                    ins.then_inc(q.summed, 1)
                pe.wait_ge(q.begun, 1)
                if q.H:
                    pipelined(pe, NG, U, [(0, total), (2, expand), (3, transpose)])
                else:
                    pipelined(pe, NG, U, [(0, total)])

            def segment_maxima(q):
                pe.wait_ge(flag_ready, (0, 2, 3).index(q.n) + 1)
                wide = pe.value_load(flagi[0:1, 0:1], min_val=0, max_val=1)
                with pe.If(wide > 0):
                    with pe.Fori(0, q.by.T * q.H) as t:
                        pe.wait_ge(q.m_masked, t + 1)
                        nc.tensor.transpose(ps_t[:, 0, 0:P], onehots[:, 0, :], ident[:, :]).then_inc(q.m_transposed, 1)
                pe.sem_inc(pe_steps, 1)

            for s_name, p, o_name in ORDER:
                if s_name:
                    project(J[s_name])
                if p in (0, 2, 3):
                    segment_maxima(passes[p])
                edges(passes[p])
                if o_name:
                    project(J[o_name])

        @block.vector
        def _(dve):
            V = nc.vector
            link = Chain(dve, dve_chain)
            dve.wait_ge(pool_consts, 6)
            link(V.tensor_copy(iota_n[:, :], iota_ni[:, :]))
            link(V.tensor_copy(iota_g[:, :, :], iota_gi[:, :, :]))
            link(V.memset(cnt[:, :, :], 0.0))

            dve.wait_ge(loaded_rec, 16)

            def count_windows(n, col, before):
                link(V.tensor_scalar(keyi, flat_rec[:, :, col], 7, None, ALU.logical_shift_right))
                if n == 1:
                    link(V.tensor_copy(keyw, keyi))
                link(V.tensor_copy(keyh, keyi))
                with dve.Fori(0, NW) as w:
                    V.tensor_scalar(indh, keyh, iota_n[0:SP_, bass.ds(w, 1)], None, ALU.is_equal, ALU.add,
                                    accum_out=cnt[0:SP_, n, bass.ds(w, 1)]).then_inc(loop_count, 1)
                    dve.wait_ge(loop_count, w + 1 + before * NW)
                dve.sem_inc(counted, 1)

            def group_tables(by):
                n, GE, GP, GC = by.number, by.GE, by.GP, by.GC
                gcmp, gw, gwi = gcmps[0:GP, 0:GC, :], gws[:, :, 0:GC], gwis[:, :, 0:GC]
                dve.wait_ge(totals, 3 if n == 0 else 2)
                tot, ng, gend, gstart, off, delta, dd, ong = (gsm[:, i, :] for i in range(8))
                link(V.memset(ong, 1.0))
                link(V.tensor_copy(tot, ps_x[:, n, 0:NB]))
                link(V.tensor_scalar(ng, tot, float(GE - 1), None, ALU.add))
                link(V.tensor_copy(gsi[:, 0, :], ng))
                link(V.tensor_scalar(gsi[:, 1, :], gsi[:, 0, :], GE.bit_length() - 1, None, ALU.logical_shift_right))
                link(V.tensor_copy(ng, gsi[:, 1, :]))
                link(V.tensor_tensor_scan(gend, ong, ng, 0.0, ALU.mult, ALU.add))
                link(V.tensor_tensor(gstart, gend, ng, ALU.subtract))
                en = gend[0:GP, 0:NW].unsqueeze(1).to_broadcast([GP, GC, NW])
                ig = iota_g[0:GP, n, 0:GC].unsqueeze(2).to_broadcast([GP, GC, NW])
                link(V.tensor_tensor(gcmp, en, ig, ALU.is_le))
                link(V.tensor_reduce(gw[0:GP, 0, :], gcmp, AX, ALU.add))
                if n == 0:
                    link(V.tensor_tensor_scan(off, ong, tot, 0.0, ALU.mult, ALU.add))
                    link(V.tensor_tensor(off, off, tot, ALU.subtract))
                    link(V.scalar_tensor_tensor(delta, gstart, -float(GE), off, ALU.mult, ALU.add))
                    link(V.tensor_tensor(dd[:, 0:NW], delta[:, 1:NB], delta[:, 0:NW], ALU.subtract))
                    link(V.tensor_tensor(gcmp, gcmp, dd[0:GP, 0:NW].unsqueeze(1).to_broadcast([GP, GC, NW]), ALU.mult))
                    link(V.tensor_reduce(gw[0:GP, 1, :], gcmp, AX, ALU.add))
                    link(V.scalar_tensor_tensor(gw[0:GP, 1, :], iota_g[0:GP, n, 0:GC], float(GE), gw[0:GP, 1, :], ALU.mult, ALU.add))
                    link(V.tensor_scalar(gw[0:GP, 1, :], gw[0:GP, 1, :], float(E), None, ALU.min))
                    dve.wait_ge(groups_stored, 16)
                for i in range(2 - n):
                    link(V.tensor_copy(gwi[0:GP, i, :], gw[0:GP, i, :]))
                dve.sem_inc(groups_ready, 1)
                return gstart

            def sort_columns(c):
                cols = bass.ds(c * CC, CC)
                inds = ind[:, 0:WU * CC].rearrange("p (w c) -> p w c", w=WU)
                cums = cum[:, 0:WU * CC].rearrange("p (w c) -> p w c", w=WU)
                with dve.Fori(0, NW // WU) as j:
                    turn = c * (NW // WU) + j + 1
                    for i in range(WU):
                        V.tensor_scalar(inds[:, i, :], keyw[:, cols], iota_n[0:SP_, bass.ds(j * WU + i, 1)], None, ALU.is_equal)\
                            .then_inc(loop_ind, 1)
                    dve.wait_ge(loop_ind, turn * WU)
                    dve.wait_ge(totals, 2)
                    for i in range(WU):
                        V.tensor_tensor_scan(cums[:, i, :], inds[:, i, :], inds[:, i, :], base[0:SP_, bass.ds(j * WU + i, 1)],
                                             ALU.add, ALU.max).then_inc(loop_cum, 1)
                    dve.wait_ge(loop_cum, turn * WU)
                    dve.sem_inc(dve_steps, 1)
                    V.tensor_copy(base[0:SP_, bass.ds(j * WU, WU)].unsqueeze(2), cums[:, :, CC - 1:CC]).then_inc(loop_base, 1)
                    for i in range(WU):
                        V.copy_predicated(pos[:, 0:CC], inds[:, i, :].bitcast(i32), cums[:, i, :]).then_inc(loop_pos, 1)
                        dve.wait_ge(loop_pos, turn * WU - (WU - 1 - i))
                        dve.sem_inc(dve_steps, 1)
                    dve.wait_ge(loop_base, turn)
                    dve.sem_inc(dve_steps, 1)
                V.tensor_scalar(posi[:, cols], pos[:, 0:CC], -1.0, None, ALU.add).then_inc(sorted_, 1)

            count_windows(1, 0, 0)
            gstart = group_tables(BY["src"])
            link(V.scalar_tensor_tensor(base[0:SP_, :], gstart[0:SP_, :], float(BY["src"].GE), ps_t[0:SP_, 0, 0:NB],
                                        ALU.mult, ALU.add))
            link(V.memset(pos, 0.0))
            sort_columns(0)
            count_windows(0, 1, 1)
            group_tables(BY["dst"])
            with dve.Fori(1, SC // CC) as c:
                dve.wait_ge(sorted_, c)
                dve.sem_inc(dve_steps, 1)
                sort_columns(c)

            dve.wait_ge(loaded_w, 16 * 27)
            dve.wait_ge(weights_mm, 1)
            link(V.tensor_copy(w_pa[:, :], ps_a[0:D + DE, 0, 0:D]))
            sv = ps_a[0:D, 0, 64:64 + 2 * H1].rearrange("p (h t) -> p t h", t=2)
            link(V.tensor_copy(w_s1[:, 0:H1], sv[:, 1, :]))
            link(V.tensor_copy(w_s1[:, H1:2 * H1], sv[:, 0, :]))
            pm = ps_a[:, 1, 0:512].rearrange("p (c a f) -> p c a f", c=H1 // 2, a=2)
            link(V.tensor_copy(w_m1[0:D, :, :], pm[0:D, :, 0, :]))
            link(V.tensor_copy(w_m1[D:P, :, :], pm[D:P, :, 1, :]))
            for t in range(2):
                link(V.tensor_tensor(wtmp[:, t, :], w_2[:, 0:D], a2b[:, t, :], ALU.mult))
                link(V.tensor_reduce(w_2[:, D + t * H2:D + (t + 1) * H2],
                                     wtmp[:, t, :].rearrange("p (h c) -> p h c", h=H2), AX, ALU.add))
                link(V.tensor_tensor(wtmp[:, t, :], w_3[:, 0:D], a3b[:, t, :], ALU.mult))
                link(V.tensor_reduce(w_3[:, D + t:D + t + 1], wtmp[:, t, :], AX, ALU.add))
            dve.wait_ge(loaded_x, 32)

            def project(j, stage_ops):
                WB = j.WB
                dve.sem_inc(j.ready, 1)

                def stage(b, s, turn):
                    since(dve, j.transposed, b - 1, j.before)
                    o = staged[:, s, 0:WB * len(j.chunks) * P].rearrange("p (w c) -> p w c", w=WB)
                    stage_ops(b, o, j.staged, WB)

                def store(b, s, turn):
                    dve.wait_ge(j.ready, j.number)
                    since(dve, j.multiplied, b + 1, j.before)
                    V.tensor_copy(j.dst[:, bass.ds(b * WB, WB), j.at:j.at + j.N],
                                  ps_x[:, s, 0:WB * j.N].rearrange("p (w n) -> p w n", w=WB)).then_inc(j.stored, 1)
                pipelined(dve, j.steps, 2, [(2, stage), (-1, store)])
                dve.wait_ge(j.stored, j.steps + j.before)

            def stage_copy(src, width):
                def ops(b, o, done, WB):
                    dve.wait_ge(loaded_x, 32)
                    V.tensor_copy(o[:, :, 0:width], src[:, bass.ds(b * WB, WB), 0:width]).then_inc(done, 1)
                return ops

            def per(v, n, shape):
                return v.unsqueeze(n).to_broadcast(shape)

            def bc(v):
                return v.unsqueeze(1).to_broadcast([P, NP, D])

            full = [P, NP, D]
            asked = [0]

            def ask():
                asked[0] += 1
                dve.sem_inc(act_ask, 1)
                dve.wait_ge(act_done, asked[0])

            def normalise(v):
                link(V.tensor_reduce(stat[:, :], v, AX, ALU.add))
                link(V.tensor_scalar(stat[:, :], stat[:, :], 1.0 / D, None, ALU.mult))
                link(V.tensor_tensor(v, v, per(stat[:, :], 2, full), ALU.subtract))
                link(V.tensor_tensor(tmp, v, v, ALU.mult))
                link(V.tensor_reduce(stat[:, :], tmp, AX, ALU.add))
                link(V.tensor_scalar(stat[:, :], stat[:, :], 1.0 / D, 1e-5, ALU.mult, ALU.add))
                ask()
                link(V.reciprocal(stat[:, :], stat[:, :]))
                link(V.tensor_tensor(v, v, per(stat[:, :], 2, full), ALU.mult))

            def load_side(n):
                dve.wait_ge(side_loaded, 16 if n == 0 else 48)
                if n == 0:
                    dve.wait_ge(dst_runs, 16 * BY["dst"].NG)
                NG, G, T = passes[n].by.NG, passes[n].by.G, passes[n].by.T
                key, other = (1, 0) if n != 1 else (0, 1)
                link(V.tensor_copy(idx[:, 0:T], grec[:, 0:T, other]))
                link(V.tensor_scalar(wbi[:, 0:NG], wbi[:, 0:NG], 7, None, ALU.logical_shift_left))
                link(V.tensor_copy(wb[:, 0:NG], wbi[:, 0:NG]))
                link(V.tensor_tensor(local[:, 0:T].rearrange("p (k g) -> p k g", g=G),
                                     grec[:, 0:T, key].rearrange("p (k g) -> p k g", g=G),
                                     wb[:, 0:NG].unsqueeze(2).to_broadcast([P, NG, G]), ALU.subtract))

            maxes = [0]

            def segment_maxima(q):
                H, NG, G = q.H, q.by.NG, q.by.G
                with dve.Fori(0, NG) as k:
                    w = dve.value_load(wrow[q.by.name][0:1, bass.ds(k, 1)], min_val=0, max_val=NW)
                    V.tensor_copy(idx_slot[:, 0:G], idx[:, bass.ds(k * G, G)]).then_inc(q.m_idx, 1)
                    dve.wait_ge(q.m_landed, k * (16 * G) + 16 * G)
                    links = 3 * G * H
                    n = 0
                    for g in range(G):
                        for h in range(H):
                            V.tensor_scalar(onehots[:, 1, :], iota_n[:, :], local[:, bass.ds(k * G + g, 1)], -3e38,
                                            ALU.not_equal, ALU.mult).then_inc(q.m_chain, 1)
                            n += 1
                            dve.wait_ge(q.m_chain, k * links + n)
                            V.tensor_scalar(onehots[:, 0, :], onehots[:, 1, :],
                                            rows[:, g * q.F + D + h:g * q.F + D + h + 1], None, ALU.add)\
                                .then_inc(q.m_masked, 1)
                            dve.wait_ge(q.m_transposed, k * (G * H) + g * H + h + 1)
                            V.tensor_reduce(stat[:, 0:1], ps_t[:, 0, 0:P], AX, ALU.max).then_inc(q.m_chain, 1)
                            n += 1
                            dve.wait_ge(q.m_chain, k * links + n)
                            m = mtmp[:, bass.ds(w, 1), h:h + 1].rearrange("p a h -> p (a h)")
                            V.tensor_tensor(m, m, stat[:, 0:1], ALU.max).then_inc(q.m_chain, 1)
                            n += 1
                            dve.wait_ge(q.m_chain, k * links + n)
                if q.n != 0:
                    link(V.tensor_tensor(mtmp[:, :, 0:H], mtmp[:, :, 0:H], tab[:, :, D:D + H], ALU.max))

            def key_table(q, src, key):
                H = q.H
                a_s, b_k = tab[:, :, src:src + H], tab[:, :, key:key + H]
                link(V.tensor_reduce(gm[:, 0, 0:H], a_s.rearrange("p w h -> p h w"), AX, ALU.max))
                link(V.tensor_reduce(gm[:, 0, H:2 * H], a_s.rearrange("p w h -> p h w"), AX, ALU.min, negate=True))
                dve.sem_inc(score_max, 1)
                maxes[0] += 1
                dve.wait_ge(score_all, maxes[0])
                m = mtmp[:, :, 0:H]
                link(V.tensor_copy(m, gm[:, 1, 0:H].unsqueeze(1).to_broadcast([P, NP, H])))
                link(V.tensor_tensor(gm[:, 0, 0:H], gm[:, 1, 0:H], gm[:, 1, H:2 * H], ALU.add))
                link(V.tensor_reduce(flag[:, 0:1], gm[:, 0, 0:H], AX, ALU.max))
                link(V.tensor_scalar(flag[:, 1:2], flag[:, 0:1], SPAN, None, ALU.is_gt))
                link(V.tensor_copy(flagi[:, :], flag[:, 1:2]))
                dve.sem_inc(flag_ready, 1)
                wide = dve.value_load(flagi[0:1, 0:1], min_val=0, max_val=1)
                before = link.n
                with dve.If(wide > 0):
                    link(V.tensor_scalar(m, gm[:, 1, H:2 * H].unsqueeze(1).to_broadcast([P, NP, H]), -1.0, None, ALU.mult))
                    segment_maxima(q)
                with dve.Else():
                    dve.sem_inc(dve_chain, link.n - before)
                link(V.tensor_tensor(m, b_k, m, ALU.add))
                link(V.scalar_tensor_tensor(m, m, SLOPE, m, ALU.mult, ALU.max))
                link(V.tensor_tensor(ntab[:, :, 0:H], b_k, m, ALU.subtract))
                link(V.scalar_tensor_tensor(ntab[:, :, H:2 * H], b_k, SLOPE, m, ALU.mult, ALU.subtract))

            def split_key_table(n):
                rest = ntab[:, :, 0:n]
                for part in range(3):
                    link(V.tensor_copy(ntab3[:, part, :, 0:n], rest))
                    if part < 2:
                        link(V.tensor_tensor(tmp[:, :, 0:n], rest, ntab3[:, part, :, 0:n], ALU.subtract))
                        rest = tmp[:, :, 0:n]

            def edges(q, start=None):
                NG, G, U = q.by.NG, q.by.G, q.by.U
                dve.sem_inc(q.begun, 1)
                if q.H:
                    split_key_table(2 * q.H)
                acc = acc_all[:, 0:NP * q.W].rearrange("p (w f) -> p w f", w=NP)
                if start:
                    start(acc)
                elif q.n == 1:
                    link(V.memset(acc_all[:, CLEARED:NP * q.W], 0.0))
                    dve.wait_ge(acc_cleared, 1)
                else:
                    link(V.memset(acc_all[:, 0:NP * q.W], 0.0))

                def make_onehot(k, s, turn):
                    since(dve, q.summed, k - U + 1)
                    V.tensor_tensor(onehots[:, s * G:(s + 1) * G, :], iota_n[:, :].unsqueeze(1).to_broadcast([P, G, P]),
                                    local[:, bass.ds(k * G, G)].unsqueeze(2).to_broadcast([P, G, P]), ALU.is_equal)\
                        .then_inc(q.onehot_made, 1)

                r = lambda s: rows[:, s * G * q.F:(s + 1) * G * q.F].rearrange("p (g f) -> p g f", g=G)
                o = lambda s: rhs[:, s % 2, 0:G * q.W].rearrange("p (g f) -> p g f", g=G)

                def score(k, s, turn):
                    H = q.H
                    since(dve, q.landed[s], 16 * G * (turn + 1), q.land0)
                    since(dve, q.expanded, k + 1)
                    since(dve, q.maxed, k - 1)
                    share = ps_x[:, s % 2, 0:G * 2 * H].rearrange("p (g h) -> p g h", g=G)
                    t = t12[:, s % 2, 0:G, :]
                    V.tensor_tensor(t[:, :, 0:H], share[:, :, 0:H], r(s)[:, :, D:D + H], ALU.add).then_inc(q.scored, 1)
                    V.scalar_tensor_tensor(t[:, :, H:2 * H], r(s)[:, :, D:D + H], SLOPE, share[:, :, H:2 * H],
                                           ALU.mult, ALU.add).then_inc(q.scored, 1)

                def larger(k, s, turn):
                    H = q.H
                    since(dve, q.scored, 2 * (k + 1))
                    since(dve, q.weighed, k - 1)
                    t = t12[:, s % 2, 0:G, :]
                    V.tensor_tensor(zmax[:, s % 2, 0:G * H].rearrange("p (g h) -> p g h", g=G),
                                    t[:, :, 0:H], t[:, :, H:2 * H], ALU.max).then_inc(q.maxed, 1)

                def clip(k, s, turn):
                    since(dve, q.maxed, k + 1)
                    z = zmax[:, s % 2, 0:G * q.H]
                    if q.n == 1:
                        V.tensor_scalar(z, z, 2.0, -2.0, ALU.min, ALU.max).then_inc(q.clipped, 1)
                    else:
                        V.tensor_scalar(z, z, 0.0, None, ALU.min).then_inc(q.clipped, 1)

                def weight_rows(k, s, turn):
                    since(dve, q.weighed, k + 1)
                    x, w = r(s), o(s)
                    e = w[:, :, q.W - q.H:q.W]
                    if q.n == 0:
                        since(dve, q.attr_landed[s], 16 * (turn + 1))
                        V.tensor_tensor(w[:, :, 0:D], x[:, :, 0:D], e.to_broadcast([P, G, D]), ALU.mult).then_inc(q.rhs_half, 1)
                        V.tensor_tensor(w[:, :, D:D + DE], attrs[:, s * G:(s + 1) * G, :], e.to_broadcast([P, G, DE]), ALU.mult)\
                            .then_inc(q.rhs_made, 1)
                    elif q.n == 1:
                        V.tensor_tensor(w[:, :, 0:H1 * D].rearrange("p g (h f) -> p g h f", h=H1),
                                        x[:, :, 0:D].unsqueeze(2).to_broadcast([P, G, H1, D]),
                                        e.unsqueeze(3).to_broadcast([P, G, H1, D]), ALU.mult).then_inc(q.rhs_made, 1)
                    else:
                        V.tensor_tensor(w[:, :, 0:D].rearrange("p g (h f) -> p g h f", h=q.H),
                                        x[:, :, 0:D].rearrange("p g (h f) -> p g h f", h=q.H),
                                        e.unsqueeze(3).to_broadcast([P, G, q.H, D // q.H]), ALU.mult).then_inc(q.rhs_made, 1)

                window = {}

                def find_window(k, s, turn):
                    window[0] = dve.value_load(wrow[q.by.name][0:1, bass.ds(k, 1)], min_val=0, max_val=NW)

                def add(k, s, turn):
                    w = window[0]
                    since(dve, q.added, k)
                    since(dve, q.summed, k + 1)
                    t = acc[:, bass.ds(w, 1), :].rearrange("p a (b f) -> p (a b) f", b=q.banks)
                    sums = ps_a[:, s % 2, :].rearrange("p (b f) -> p b f", f=512)[:, 0:q.banks, 0:q.W // q.banks]
                    V.tensor_tensor(t, sums, t, ALU.add).then_inc(q.added, 1)

                if q.H:
                    stages = [(0, weight_rows), (-2, find_window), (-2, add), (1, score), (3, make_onehot), (1, larger), (1, clip)] \
                        if q.n == 1 else \
                        [(0, score), (3, make_onehot), (-2, find_window), (0, larger), (0, clip), (-2, add),
                         (0, weight_rows)]
                else:
                    stages = [(-2, find_window), (-2, add), (3, make_onehot)]
                pipelined(dve, NG, U, stages)
                dve.wait_ge(q.added, NG)
                return acc

            def reciprocals(den, H, eps):
                d = rden[:, :, 0:H]
                if eps:
                    link(V.tensor_scalar(d, den, eps, None, ALU.add))
                else:
                    link(V.tensor_scalar(d, den, 0.0, None, ALU.is_equal))
                    link(V.tensor_tensor(d, d, den, ALU.add))
                link(V.reciprocal(d, d))

            load_side(0)
            dve.sem_inc(side_made, 1)
            project(J["s0"], stage_copy(xcur, D))
            link(V.tensor_scalar(tab[:, :, D + 1:D + 2], tab[:, :, D + 1:D + 2], b_attn[:, 0:1], None, ALU.add))
            link(V.tensor_copy(tab[:, :, 0:D], xcur[:, :, :]))
            dve.sem_inc(table_made, 1)
            key_table(passes[0], D, D + 1)
            acc = edges(passes[0])
            reciprocals(acc[:, :, D + DE:D + DE + 1], 1, 0)

            def stage0(b, o, done, WB):
                w = bass.ds(b * WB, WB)
                V.tensor_tensor(o[:, :, 0:D + DE], acc0[:, w, 0:D + DE], rden[:, w, 0:1].to_broadcast([P, WB, D + DE]),
                                ALU.mult).then_inc(half_staged, 1)
                V.tensor_copy(o[:, :, P:P + D], xcur[:, w, :]).then_inc(done, 1)
            acc0 = acc
            project(J["o0"], stage0)
            dve.sem_inc(acc_free, 1)
            link(V.tensor_tensor(pre[:, :, :], pre[:, :, :], bc(b_apply[:, :]), ALU.add))
            link(V.scalar_tensor_tensor(xcur[:, :, :], pre[:, :, :], 0.0, xcur[:, :, :], ALU.max, ALU.add))
            normalise(xcur[:, :, :])

            project(J["s1"], stage_copy(xcur, D))
            link(V.tensor_copy(tab[:, :, 0:D], xcur[:, :, :]))
            dve.sem_inc(table_made, 1)
            link(V.tensor_copy(ntab[:, :, 0:H1], tab[:, :, D + H1:D + 2 * H1]))
            link(V.tensor_scalar(ntab[:, :, H1:2 * H1], tab[:, :, D + H1:D + 2 * H1], SLOPE, None, ALU.mult))
            dve.wait_ge(side_saved, 32)
            load_side(1)
            acc1 = edges(passes[1])
            dve.sem_inc(side_free, 1)
            reciprocals(acc1[:, :, H1 * D:H1 * D + H1], H1, 0)

            def stage1(b, o, done, WB):
                for w in range(WB):
                    ins = V.tensor_tensor(o[:, w, :].rearrange("p (h f) -> p h f", h=H1),
                                          acc1[:, bass.ds(b * WB + w, 1), 0:H1 * D].rearrange("p a (h f) -> p (a h) f", h=H1),
                                          rden[:, bass.ds(b * WB + w, 1), :].rearrange("p a h -> p (a h)").unsqueeze(2)
                                          .to_broadcast([P, H1, D]), ALU.mult)
                    ins.then_inc(half_staged if w == 0 else done, 1)
            project(J["o1"], stage1)
            link(V.scalar_tensor_tensor(pre[:, :, :], pre[:, :, :], SLOPE, pre[:, :, :], ALU.mult, ALU.max))
            link(V.tensor_tensor(xcur[:, :, :], xcur[:, :, :], pre[:, :, :], ALU.add))
            normalise(xcur[:, :, :])

            for p, j, src in ((2, "s2", xcur), (3, "s3", pre)):
                q, H = passes[p], HEADS[p]
                v0 = 0 if p == 2 else 3
                project(J[j], stage_copy(src, D))
                dve.sem_inc(table_made, 1)
                if p == 2:
                    dve.wait_ge(side_back, 32)
                key_table(q, D, D + H)

                def loop_edges(acc, H=H):
                    s_, m = mtmp[:, :, 0:H], rden[:, :, 0:H]
                    link(V.tensor_tensor(s_, tab[:, :, D:D + H], ntab[:, :, 0:H], ALU.add))
                    link(V.scalar_tensor_tensor(m, tab[:, :, D:D + H], SLOPE, ntab[:, :, H:2 * H], ALU.mult, ALU.add))
                    link(V.tensor_tensor(s_, s_, m, ALU.max))
                    ask()
                    link(V.tensor_copy(acc[:, :, D:D + H], s_))
                    for h in range(H):
                        c = slice(h * (D // H), (h + 1) * (D // H))
                        link(V.tensor_tensor(acc[:, :, c], tab[:, :, c], s_[:, :, h:h + 1].to_broadcast([P, NP, D // H]), ALU.mult))

                acc = edges(q, loop_edges)
                reciprocals(acc[:, :, D:D + H], H, 1e-16)
                for h in range(H):
                    c = slice(h * (D // H), (h + 1) * (D // H))
                    link(V.tensor_tensor(pre[:, :, c], acc[:, :, c], rden[:, :, h:h + 1].to_broadcast([P, NP, D // H]), ALU.mult))
                link(V.tensor_tensor(pre[:, :, :], pre[:, :, :], bc(vec[:, v0, :]), ALU.add))
                normalise(pre[:, :, :])
                link(V.tensor_tensor(pre[:, :, :], pre[:, :, :], bc(vec[:, v0 + 1, :]), ALU.mult))
                link(V.tensor_tensor(pre[:, :, :], pre[:, :, :], bc(vec[:, v0 + 2, :]), ALU.add))
                link(V.tensor_scalar(tmp, pre[:, :, :], 0.0, None, ALU.min))
                asked[0] += 1
                dve.sem_inc(act_ask, 1)
                link(V.tensor_scalar(pre[:, :, :], pre[:, :, :], 0.0, -1.0, ALU.max, ALU.add))
                dve.wait_ge(act_done, asked[0])
                link(V.tensor_tensor(pre[:, :, :], pre[:, :, :], tmp, ALU.add))
            link(V.tensor_tensor(xcur[:, :, :], xcur[:, :, :], pre[:, :, :], ALU.add))
            normalise(xcur[:, :, :])

            for p, j, src in ((4, "o4", xcur), (5, "o5", pre)):
                q = passes[p]
                link(V.tensor_copy(tab[:, :, 0:D], src[:, :, :]))
                link(V.memset(tab[:, :, D:D + 1], 1.0))
                dve.sem_inc(table_made, 1)
                accs = edges(q)
                link(V.tensor_scalar(deginv[:, :].unsqueeze(2), accs[:, :, D:D + 1], 1.0, None, ALU.max))
                link(V.reciprocal(deginv[:, :], deginv[:, :]))

                def stage_sage(b, o, done, WB, accs=accs):
                    w = bass.ds(b * WB, WB)
                    V.tensor_tensor(o[:, :, 0:D], accs[:, w, 0:D], deginv[:, w].unsqueeze(2).to_broadcast([P, WB, D]),
                                    ALU.mult).then_inc(half_staged, 1)
                    V.tensor_copy(o[:, :, D:2 * D], tab[:, w, 0:D]).then_inc(done, 1)
                project(J[j], stage_sage)
                link(V.tensor_tensor(pre[:, :, :], pre[:, :, :], bc(vec[:, 6 + p - 4, :]), ALU.add))
                link(V.tensor_tensor(tmp, pre[:, :, :], pre[:, :, :], ALU.mult))
                link(V.tensor_reduce(stat[:, :], tmp, AX, ALU.add))
                ask()
                link(V.tensor_scalar(stat[:, :], stat[:, :], 1e-12, None, ALU.max))
                link(V.reciprocal(stat[:, :], stat[:, :]))
                link(V.tensor_tensor(pre[:, :, :], pre[:, :, :], per(stat[:, :], 2, full), ALU.mult))
                link(V.tensor_scalar(pre[:, :, :], pre[:, :, :], 0.0, None, ALU.max))
            link(V.tensor_tensor(xcur[:, :, :], xcur[:, :, :], pre[:, :, :], ALU.add))
            normalise(xcur[:, :, :])
            dve.sem_inc(final_made, 1)


def kernel(x, src, dst, edge_attr_32, **w):
    import numpy as np
    import concourse.bacc as bacc
    from concourse.bass_utils import run_bass_kernel_spmd as run

    rec = np.empty((E + GEMAX, 2), np.int32)
    rec[:E, 0], rec[:E, 1] = np.asarray(src), np.asarray(dst)
    rec[E:, 0], rec[E:, 1] = 0, BIG_NODE
    attr = np.zeros((E + GEMAX, DE), np.float32)
    attr[:E] = np.asarray(edge_attr_32)
    v = {k: np.asarray(a) for k, a in w.items()}
    arrays = {
        "x": np.asarray(x), "rec": rec, "attr": attr,
        "attn_wT": v["L0_gnn_attn_w"].reshape(2, D).T, "attn_b": v["L0_gnn_attn_b"],
        "proj_w": v["L0_gnn_proj_w"], "apply_wT": v["L0_gnn_apply_w"].T, "apply_b": v["L0_gnn_apply_b"],
        "W_t": v["L1_gnn_W"].transpose(2, 0, 1), "a_t": v["L1_gnn_a"].reshape(H1, 2, D).transpose(2, 0, 1),
        "merge_t": v["L1_gnn_merge_kernel"].reshape(H1, D, D).transpose(1, 0, 2),
        "W1": v["L2_gnn_W1"], "W2": v["L2_gnn_W2"],
        "a1_src": v["L2_gnn_a1_src"].reshape(-1), "a1_dst": v["L2_gnn_a1_dst"].reshape(-1),
        "a2_src": v["L2_gnn_a2_src"].reshape(-1), "a2_dst": v["L2_gnn_a2_dst"].reshape(-1),
        "b1": v["L2_gnn_b1"], "b2": v["L2_gnn_b2"],
        "ln1_g": v["L2_gnn_ln1_g"], "ln1_b": v["L2_gnn_ln1_b"],
        "ln2_g": v["L2_gnn_ln2_g"], "ln2_b": v["L2_gnn_ln2_b"],
        "Wl0T": v["L3_gnn_Wl0"].T, "Wr0T": v["L3_gnn_Wr0"].T, "bl0": v["L3_gnn_bl0"],
        "Wl1T": v["L3_gnn_Wl1"].T, "Wr1T": v["L3_gnn_Wr1"].T, "bl1": v["L3_gnn_bl1"],
    }
    nc = bacc.Bacc("TRN2", target_bir_lowering=False, num_devices=1)
    ins, aps = {}, {}
    for name, arr in arrays.items():
        arr = np.ascontiguousarray(arr)
        ins[f"in_{name}"] = arr
        aps[name] = nc.dram_tensor(f"in_{name}", arr.shape, mybir.dt.from_np(arr.dtype), kind="ExternalInput").ap()
    out = nc.dram_tensor("out_0", (N, D), fp32, kind="ExternalOutput").ap()
    build(nc, aps, out)
    r = run(nc, [ins], core_ids=[0])
    return r.results[0]["out_0"]
```
